# Optimizing a Trainium2 kernel written in Bass

```python
import numpy as np
import jax
import jax.numpy as jnp

def _softmax(x, axis=-1):
    return jax.nn.softmax(x, axis=axis)

def _gelu(x):
    return jax.nn.gelu(x, approximate=True)

def _silu(x):
    return jax.nn.silu(x)

def _sigmoid(x):
    return jax.nn.sigmoid(x)

def _layernorm(x, axis=-1, eps=1e-05):
    m = jnp.mean(x, axis=axis, keepdims=True)
    v = jnp.var(x, axis=axis, keepdims=True)
    return (x - m) / jnp.sqrt(v + eps)

def _scatter_add(tgt, idx, src, axis=0):
    return tgt.at[idx].add(src)

def _segment_sum(src, seg, n):
    return jax.ops.segment_sum(src, seg, n)
kernel_name = 'mk_flamingo_gated_d2_seqx_r4_7d18ed'

def setup_inputs(seed: int=0):
    np.random.seed(seed)
    _w = jnp.asarray

    def _rec_inputs():
        import jax
        import jax.numpy as jnp
        _rk = jax.random.key(seed)
        x = 6.313e-05 + 0.9998 * jax.random.normal(jax.random.fold_in(_rk, 1), (4, 512, 256), jnp.float32)
        _lenS = 512 - jax.random.randint(jax.random.fold_in(_rk, 7), (4,), 0, max(1, 512 // 4) + 1, jnp.int32)
        _lenS2 = 1024 - jax.random.randint(jax.random.fold_in(_rk, 8), (4,), 0, max(1, 1024 // 4) + 1, jnp.int32)
        _ctx_1024P = jax.random.normal(jax.random.fold_in(_rk, 11), (4, 16, 256), jnp.float32)
        _ctx_1024c = jax.random.dirichlet(jax.random.fold_in(_rk, 511), 0.3 * jnp.ones((16,), jnp.float32), (4, 1024))
        _ctx_1024t = jnp.einsum('bsk,bkd->bsd', _ctx_1024c, _ctx_1024P)
        _ctx_1024t = _ctx_1024t * jax.lax.rsqrt(jnp.mean(jnp.square(_ctx_1024t)) + 1e-12) * 0.953939
        ctx_1024 = -0.000214406 + 1.00034 * (_ctx_1024t + 0.3 * jax.random.normal(jax.random.fold_in(_rk, 611), (4, 1024, 256), jnp.float32))
        _validS = jnp.arange(512)[None, :] < _lenS[:, None]
        _validS2 = jnp.arange(1024)[None, :] < _lenS2[:, None]
        _causal = jnp.tril(jnp.ones((512, 512), dtype=bool))
        mask_BxSxS2_ik0 = jnp.where(jnp.broadcast_to(_validS2[:, None, :], (4, 512, 1024)), 0, 1).astype(jnp.int32)
        _g = jax.random.normal(jax.random.fold_in(_rk, 9001), (2, 2), jnp.float32)
        _g = jnp.sign(_g) * jnp.maximum(jnp.abs(_g), 1.0) + (_g == 0) * 1.0
        g_xattn = _g[0]
        g_ffn = _g[1]
        return (x, ctx_1024, mask_BxSxS2_ik0, g_xattn, g_ffn)
    x, ctx_1024, mask_BxSxS2_ik0, g_xattn, g_ffn = _rec_inputs()

    def _L0_xattn_setup():
        import jax, jax.numpy as jnp
        import numpy as np
        from jax import lax
        BIG = jnp.float32(1e+30)

        def _pairwise_euclidean(a, b):
            aa = jnp.sum(a * a, axis=-1)[:, None]
            bb = jnp.sum(b * b, axis=-1)[None, :]
            ab = a @ b.T
            return jnp.sqrt(jnp.maximum(aa + bb - 2.0 * ab, 0.0))

        def _dtw_cost(D):
            row0 = jnp.cumsum(D[0])

            def row_step(prev_row, d_row):
                first = d_row[0] + prev_row[0]

                def col_step(left, inp):
                    d_ij, up, diag = inp
                    r = d_ij + jnp.minimum(jnp.minimum(up, left), diag)
                    return (r, r)
                _, rest = lax.scan(col_step, first, (d_row[1:], prev_row[1:], prev_row[:-1]))
                row = jnp.concatenate([first[None], rest])
                return (row, row)
            _, rows = lax.scan(row_step, row0, D[1:])
            return jnp.concatenate([row0[None], rows], axis=0)

        def _backtrack(R, T1, T2):
            L = T1 + T2 - 1

            def step(carry, _):
                i, j, done = carry
                valid = jnp.logical_not(done)
                cd = jnp.where((i > 0) & (j > 0), R[jnp.maximum(i - 1, 0), jnp.maximum(j - 1, 0)], BIG)
                cu = jnp.where(i > 0, R[jnp.maximum(i - 1, 0), j], BIG)
                cl = jnp.where(j > 0, R[i, jnp.maximum(j - 1, 0)], BIG)
                choice = jnp.argmin(jnp.stack([cd, cu, cl]))
                ni = jnp.where(choice <= 1, i - 1, i)
                nj = jnp.where((choice == 0) | (choice == 2), j - 1, j)
                at_origin = (i == 0) & (j == 0)
                ni = jnp.where(at_origin, 0, ni)
                nj = jnp.where(at_origin, 0, nj)
                return ((ni, nj, done | at_origin), (i, j, valid))
            init = (jnp.int32(T1 - 1), jnp.int32(T2 - 1), jnp.bool_(False))
            _, (i_idx, j_idx, valid) = lax.scan(step, init, None, length=L)
            return (i_idx, j_idx, valid)

        def _align_one(small, large):
            T_small, d = small.shape
            T_large = large.shape[0]
            D = _pairwise_euclidean(small, large)
            R = _dtw_cost(D)
            i_idx, j_idx, valid = _backtrack(R, T_small, T_large)
            contrib = small[i_idx] * valid[:, None].astype(small.dtype)
            expanded = jnp.zeros((T_large, d), dtype=small.dtype).at[j_idx].add(contrib)
            return expanded
        key = jax.random.key(seed)
        k1, k2 = jax.random.split(key)
        teacher = jax.random.normal(k1, (16, 100, 256), dtype=jnp.float32)
        student = jax.random.normal(k2, (16, 150, 256), dtype=jnp.float32)
        return {'teacher_features': teacher, 'student_features': student}
    _L0_xattn_all = _L0_xattn_setup()
    _L0_xattn_in = {k: v for k, v in _L0_xattn_all.items() if k in ()}
    del _L0_xattn_all

    def _L0_ffn_setup():
        import jax, jax.numpy as jnp
        import numpy as np
        import math
        B, T, D, H, E, TOPK, CAPF = (4, 512, 256, 16, 8, 2, 2.0)
        HD = D // H

        def layernorm(x, g, b, eps=1e-05):
            m = jnp.mean(x, -1, keepdims=True)
            v = jnp.mean(jnp.square(x - m), -1, keepdims=True)
            return (x - m) * jax.lax.rsqrt(v + eps) * g + b

        def block_forward(x, ln1_g, ln1_b, Wqkv, Wproj, ln2_g, ln2_b, Wgate, W1, b1, W2, b2):
            Bb, Tt, d = x.shape
            hd = HD
            half = hd // 2
            h = layernorm(x, ln1_g, ln1_b)
            qkv = (h @ Wqkv).reshape(Bb, Tt, H, 3 * hd)
            q, k, v = (qkv[..., :hd], qkv[..., hd:2 * hd], qkv[..., 2 * hd:])
            inv_freq = 1.0 / 10000.0 ** (jnp.arange(0, hd, 2, dtype=jnp.float32) / hd)
            ang = jnp.arange(Tt, dtype=jnp.float32)[:, None] * inv_freq
            sin = jnp.sin(ang)[None, :, None, :].astype(x.dtype)
            cos = jnp.cos(ang)[None, :, None, :].astype(x.dtype)

            def rope(t):
                t1, t2 = (t[..., :half], t[..., half:])
                return jnp.concatenate([t1 * cos - t2 * sin, t1 * sin + t2 * cos], -1)
            q, k = (rope(q), rope(k))
            scores = jnp.einsum('bqhd,bkhd->bhqk', q, k) / math.sqrt(hd)
            causal = jnp.tril(jnp.ones((Tt, Tt), dtype=bool))
            scores = jnp.where(causal, scores, jnp.asarray(-1000000000.0, scores.dtype))
            probs = jax.nn.softmax(scores, axis=-1)
            attn = jnp.einsum('bhqk,bkhd->bqhd', probs, v).reshape(Bb, Tt, d) @ Wproj
            x = x + attn
            h2 = layernorm(x, ln2_g, ln2_b)
            flat = h2.reshape(-1, d)
            N = flat.shape[0]
            capacity = int(math.ceil(CAPF * N / E))
            gates = jax.nn.softmax((flat @ Wgate).astype(jnp.float32), -1).astype(flat.dtype)
            _, top_inds = jax.lax.top_k(gates, TOPK)
            mask = jnp.zeros((N, E), dtype=bool).at[jnp.arange(N)[:, None], top_inds].set(True)
            pos = jnp.cumsum(mask.astype(jnp.int32), axis=0) * mask - 1
            keep = (pos < capacity) & mask
            t_flat = jnp.repeat(jnp.arange(N), TOPK)
            e_flat = top_inds.reshape(-1)
            p = pos[t_flat, e_flat]
            kp = keep[t_flat, e_flat]
            p_eff = jnp.where(kp, p, capacity)
            exp_in = jnp.zeros((E, capacity, d), flat.dtype).at[e_flat, p_eff].set(flat[t_flat], mode='drop')
            hmid = jax.nn.gelu(jnp.einsum('ecd,edf->ecf', exp_in, W1) + b1[:, None, :], approximate=False)
            exp_out = jnp.einsum('ecf,efd->ecd', hmid, W2) + b2[:, None, :]
            gate = gates[t_flat, e_flat] * kp.astype(flat.dtype)
            p_g = jnp.minimum(p_eff, capacity - 1)
            moe = jnp.zeros((N, d), flat.dtype).at[t_flat].add(exp_out[e_flat, p_g] * gate[:, None])
            return x + moe.reshape(Bb, Tt, d)
        key = jax.random.key(seed)
        ks = jax.random.split(key, 8)
        s = 0.02
        return {'x': jax.random.normal(ks[0], (B, T, D), jnp.float32), 'ln1_g': jnp.ones((D,), jnp.float32), 'ln1_b': jnp.zeros((D,), jnp.float32), 'Wqkv': jax.random.normal(ks[1], (D, 3 * D), jnp.float32) * s, 'Wproj': jax.random.normal(ks[2], (D, D), jnp.float32) * s, 'ln2_g': jnp.ones((D,), jnp.float32), 'ln2_b': jnp.zeros((D,), jnp.float32), 'Wgate': jax.random.normal(ks[3], (D, E), jnp.float32) * s, 'W1': jax.random.normal(ks[4], (E, D, 4 * D), jnp.float32) * s, 'b1': jnp.zeros((E, 4 * D), jnp.float32), 'W2': jax.random.normal(ks[5], (E, 4 * D, D), jnp.float32) * s, 'b2': jnp.zeros((E, D), jnp.float32)}
    _L0_ffn_all = _L0_ffn_setup()
    _L0_ffn_in = {k: v for k, v in _L0_ffn_all.items() if k in ('ln1_g', 'ln1_b', 'Wqkv', 'Wproj', 'ln2_g', 'ln2_b', 'Wgate', 'W1', 'b1', 'W2', 'b2')}
    del _L0_ffn_all

    def _L1_xattn_setup():
        import jax, jax.numpy as jnp
        import numpy as np
        B, S, D, H = (2, 512, 256, 16)
        DK = D // H

        def _split_heads(x):
            b, s, _ = x.shape
            return x.reshape(b, s, H, DK).transpose(0, 2, 1, 3)
        key = jax.random.key(seed)
        ks = jax.random.split(key, 7)
        causal = jnp.tril(jnp.ones((S, S), dtype=jnp.int32))
        mask = jnp.broadcast_to(causal, (B, S, S))
        return {'query': jax.random.normal(ks[0], (B, S, D), dtype=jnp.float32), 'key': jax.random.normal(ks[1], (B, S, D), dtype=jnp.float32), 'value': jax.random.normal(ks[2], (B, S, D), dtype=jnp.float32), 'mask': mask, 'Wq': jax.random.normal(ks[3], (D, D), dtype=jnp.float32) * D ** (-0.5), 'Wk': jax.random.normal(ks[4], (D, D), dtype=jnp.float32) * D ** (-0.5), 'Wv': jax.random.normal(ks[5], (D, D), dtype=jnp.float32) * D ** (-0.5), 'Wo': jax.random.normal(ks[6], (D, D), dtype=jnp.float32) * D ** (-0.5)}
    _L1_xattn_all = _L1_xattn_setup()
    _L1_xattn_in = {k: v for k, v in _L1_xattn_all.items() if k in ('Wq', 'Wk', 'Wv', 'Wo')}
    del _L1_xattn_all

    def _L1_ffn_setup():
        import jax, jax.numpy as jnp
        import numpy as np
        BLOCK = 16
        _GRID = jnp.array([0.0, 0.5, 1.0, 1.5, 2.0, 3.0, 4.0, 6.0], dtype=jnp.float32)
        _MID = jnp.array([0.25, 0.75, 1.25, 1.75, 2.5, 3.5, 5.0], dtype=jnp.float32)

        def fp4_quant_dequant(x):
            shape = x.shape
            xb = x.reshape(shape[:-1] + (shape[-1] // BLOCK, BLOCK))
            scale = jnp.max(jnp.abs(xb), axis=-1, keepdims=True) / 6.0
            scale = jnp.maximum(scale, jnp.float32(1e-12))
            xn = xb / scale
            idx = jnp.searchsorted(_MID, jnp.abs(xn))
            q = _GRID[idx] * jnp.sign(xn) * scale
            return q.reshape(shape)

        def fp4_linear(x, w):
            xq = fp4_quant_dequant(x)
            wq = fp4_quant_dequant(w)
            return jnp.einsum('bsk,nk->bsn', xq, wq)
        key = jax.random.key(seed)
        k1, k2, k3, k4 = jax.random.split(key, 4)
        H, I = (256, 704)
        x = jax.random.normal(k1, (4, 1024, H), dtype=jnp.float32)
        w_gate = jax.random.normal(k2, (I, H), dtype=jnp.float32) * 0.02
        w_up = jax.random.normal(k3, (I, H), dtype=jnp.float32) * 0.02
        w_down = jax.random.normal(k4, (H, I), dtype=jnp.float32) * 0.02
        return {'x': x, 'w_gate': w_gate, 'w_up': w_up, 'w_down': w_down}
    _L1_ffn_all = _L1_ffn_setup()
    _L1_ffn_in = {k: v for k, v in _L1_ffn_all.items() if k in ('w_gate', 'w_up', 'w_down')}
    del _L1_ffn_all
    return {'x': x, 'ctx_1024': ctx_1024, 'mask_BxSxS2_ik0': mask_BxSxS2_ik0, 'g_xattn': g_xattn, 'g_ffn': g_ffn, 'L0_ffn_ln1_g': _L0_ffn_in['ln1_g'], 'L0_ffn_ln1_b': _L0_ffn_in['ln1_b'], 'L0_ffn_Wqkv': _L0_ffn_in['Wqkv'], 'L0_ffn_Wproj': _L0_ffn_in['Wproj'], 'L0_ffn_ln2_g': _L0_ffn_in['ln2_g'], 'L0_ffn_ln2_b': _L0_ffn_in['ln2_b'], 'L0_ffn_Wgate': _L0_ffn_in['Wgate'], 'L0_ffn_W1': _L0_ffn_in['W1'], 'L0_ffn_b1': _L0_ffn_in['b1'], 'L0_ffn_W2': _L0_ffn_in['W2'], 'L0_ffn_b2': _L0_ffn_in['b2'], 'L1_xattn_Wq': _L1_xattn_in['Wq'], 'L1_xattn_Wk': _L1_xattn_in['Wk'], 'L1_xattn_Wv': _L1_xattn_in['Wv'], 'L1_xattn_Wo': _L1_xattn_in['Wo'], 'L1_ffn_w_gate': _L1_ffn_in['w_gate'], 'L1_ffn_w_up': _L1_ffn_in['w_up'], 'L1_ffn_w_down': _L1_ffn_in['w_down']}

def reference(x, ctx_1024, mask_BxSxS2_ik0, g_xattn, g_ffn, L0_ffn_ln1_g, L0_ffn_ln1_b, L0_ffn_Wqkv, L0_ffn_Wproj, L0_ffn_ln2_g, L0_ffn_ln2_b, L0_ffn_Wgate, L0_ffn_W1, L0_ffn_b1, L0_ffn_W2, L0_ffn_b2, L1_xattn_Wq, L1_xattn_Wk, L1_xattn_Wv, L1_xattn_Wo, L1_ffn_w_gate, L1_ffn_w_up, L1_ffn_w_down):
    import jax
    import jax.numpy as jnp

    def _L0_xattn_ref(teacher_features, student_features):
        import jax, jax.numpy as jnp
        import numpy as np
        from jax import lax
        BIG = jnp.float32(1e+30)

        def _pairwise_euclidean(a, b):
            aa = jnp.sum(a * a, axis=-1)[:, None]
            bb = jnp.sum(b * b, axis=-1)[None, :]
            ab = a @ b.T
            return jnp.sqrt(jnp.maximum(aa + bb - 2.0 * ab, 0.0))

        def _dtw_cost(D):
            row0 = jnp.cumsum(D[0])

            def row_step(prev_row, d_row):
                first = d_row[0] + prev_row[0]

                def col_step(left, inp):
                    d_ij, up, diag = inp
                    r = d_ij + jnp.minimum(jnp.minimum(up, left), diag)
                    return (r, r)
                _, rest = lax.scan(col_step, first, (d_row[1:], prev_row[1:], prev_row[:-1]))
                row = jnp.concatenate([first[None], rest])
                return (row, row)
            _, rows = lax.scan(row_step, row0, D[1:])
            return jnp.concatenate([row0[None], rows], axis=0)

        def _backtrack(R, T1, T2):
            L = T1 + T2 - 1

            def step(carry, _):
                i, j, done = carry
                valid = jnp.logical_not(done)
                cd = jnp.where((i > 0) & (j > 0), R[jnp.maximum(i - 1, 0), jnp.maximum(j - 1, 0)], BIG)
                cu = jnp.where(i > 0, R[jnp.maximum(i - 1, 0), j], BIG)
                cl = jnp.where(j > 0, R[i, jnp.maximum(j - 1, 0)], BIG)
                choice = jnp.argmin(jnp.stack([cd, cu, cl]))
                ni = jnp.where(choice <= 1, i - 1, i)
                nj = jnp.where((choice == 0) | (choice == 2), j - 1, j)
                at_origin = (i == 0) & (j == 0)
                ni = jnp.where(at_origin, 0, ni)
                nj = jnp.where(at_origin, 0, nj)
                return ((ni, nj, done | at_origin), (i, j, valid))
            init = (jnp.int32(T1 - 1), jnp.int32(T2 - 1), jnp.bool_(False))
            _, (i_idx, j_idx, valid) = lax.scan(step, init, None, length=L)
            return (i_idx, j_idx, valid)

        def _align_one(small, large):
            T_small, d = small.shape
            T_large = large.shape[0]
            D = _pairwise_euclidean(small, large)
            R = _dtw_cost(D)
            i_idx, j_idx, valid = _backtrack(R, T_small, T_large)
            contrib = small[i_idx] * valid[:, None].astype(small.dtype)
            expanded = jnp.zeros((T_large, d), dtype=small.dtype).at[j_idx].add(contrib)
            return expanded
        return jax.vmap(_align_one)(teacher_features, student_features)

    def _L0_ffn_ref(x, ln1_g, ln1_b, Wqkv, Wproj, ln2_g, ln2_b, Wgate, W1, b1, W2, b2):
        import jax, jax.numpy as jnp
        import numpy as np
        import math
        B, T, D, H, E, TOPK, CAPF = (4, 512, 256, 16, 8, 2, 2.0)
        HD = D // H

        def layernorm(x, g, b, eps=1e-05):
            m = jnp.mean(x, -1, keepdims=True)
            v = jnp.mean(jnp.square(x - m), -1, keepdims=True)
            return (x - m) * jax.lax.rsqrt(v + eps) * g + b

        def block_forward(x, ln1_g, ln1_b, Wqkv, Wproj, ln2_g, ln2_b, Wgate, W1, b1, W2, b2):
            Bb, Tt, d = x.shape
            hd = HD
            half = hd // 2
            h = layernorm(x, ln1_g, ln1_b)
            qkv = (h @ Wqkv).reshape(Bb, Tt, H, 3 * hd)
            q, k, v = (qkv[..., :hd], qkv[..., hd:2 * hd], qkv[..., 2 * hd:])
            inv_freq = 1.0 / 10000.0 ** (jnp.arange(0, hd, 2, dtype=jnp.float32) / hd)
            ang = jnp.arange(Tt, dtype=jnp.float32)[:, None] * inv_freq
            sin = jnp.sin(ang)[None, :, None, :].astype(x.dtype)
            cos = jnp.cos(ang)[None, :, None, :].astype(x.dtype)

            def rope(t):
                t1, t2 = (t[..., :half], t[..., half:])
                return jnp.concatenate([t1 * cos - t2 * sin, t1 * sin + t2 * cos], -1)
            q, k = (rope(q), rope(k))
            scores = jnp.einsum('bqhd,bkhd->bhqk', q, k) / math.sqrt(hd)
            causal = jnp.tril(jnp.ones((Tt, Tt), dtype=bool))
            scores = jnp.where(causal, scores, jnp.asarray(-1000000000.0, scores.dtype))
            probs = jax.nn.softmax(scores, axis=-1)
            attn = jnp.einsum('bhqk,bkhd->bqhd', probs, v).reshape(Bb, Tt, d) @ Wproj
            x = x + attn
            h2 = layernorm(x, ln2_g, ln2_b)
            flat = h2.reshape(-1, d)
            N = flat.shape[0]
            capacity = int(math.ceil(CAPF * N / E))
            gates = jax.nn.softmax((flat @ Wgate).astype(jnp.float32), -1).astype(flat.dtype)
            _, top_inds = jax.lax.top_k(gates, TOPK)
            mask = jnp.zeros((N, E), dtype=bool).at[jnp.arange(N)[:, None], top_inds].set(True)
            pos = jnp.cumsum(mask.astype(jnp.int32), axis=0) * mask - 1
            keep = (pos < capacity) & mask
            t_flat = jnp.repeat(jnp.arange(N), TOPK)
            e_flat = top_inds.reshape(-1)
            p = pos[t_flat, e_flat]
            kp = keep[t_flat, e_flat]
            p_eff = jnp.where(kp, p, capacity)
            exp_in = jnp.zeros((E, capacity, d), flat.dtype).at[e_flat, p_eff].set(flat[t_flat], mode='drop')
            hmid = jax.nn.gelu(jnp.einsum('ecd,edf->ecf', exp_in, W1) + b1[:, None, :], approximate=False)
            exp_out = jnp.einsum('ecf,efd->ecd', hmid, W2) + b2[:, None, :]
            gate = gates[t_flat, e_flat] * kp.astype(flat.dtype)
            p_g = jnp.minimum(p_eff, capacity - 1)
            moe = jnp.zeros((N, d), flat.dtype).at[t_flat].add(exp_out[e_flat, p_g] * gate[:, None])
            return x + moe.reshape(Bb, Tt, d)
        return block_forward(x, ln1_g, ln1_b, Wqkv, Wproj, ln2_g, ln2_b, Wgate, W1, b1, W2, b2)

    def _L1_xattn_ref(query, key, value, mask, Wq, Wk, Wv, Wo):
        import jax, jax.numpy as jnp
        import numpy as np
        B, S, D, H = (2, 512, 256, 16)
        DK = D // H

        def _split_heads(x):
            b, s, _ = x.shape
            return x.reshape(b, s, H, DK).transpose(0, 2, 1, 3)
        q = _split_heads(query @ Wq.T)
        k = _split_heads(key @ Wk.T)
        v = _split_heads(value @ Wv.T)
        inv_scale = jnp.asarray(DK ** 0.5, dtype=q.dtype)
        scores = jnp.einsum('bhqd,bhkd->bhqk', q, k) * inv_scale
        min_val = jnp.finfo(scores.dtype).min
        scores = jnp.where(mask[:, None, :, :] == 0, min_val, scores)
        attn = jax.nn.softmax(scores.astype(jnp.float32), axis=-1).astype(scores.dtype)
        ctx = jnp.einsum('bhqk,bhkd->bhqd', attn, v)
        ctx = ctx.transpose(0, 2, 1, 3).reshape(query.shape[0], -1, D)
        return ctx @ Wo.T

    def _L1_ffn_ref(x, w_gate, w_up, w_down):
        import jax, jax.numpy as jnp
        import numpy as np
        BLOCK = 16
        _GRID = jnp.array([0.0, 0.5, 1.0, 1.5, 2.0, 3.0, 4.0, 6.0], dtype=jnp.float32)
        _MID = jnp.array([0.25, 0.75, 1.25, 1.75, 2.5, 3.5, 5.0], dtype=jnp.float32)

        def fp4_quant_dequant(x):
            shape = x.shape
            xb = x.reshape(shape[:-1] + (shape[-1] // BLOCK, BLOCK))
            scale = jnp.max(jnp.abs(xb), axis=-1, keepdims=True) / 6.0
            scale = jnp.maximum(scale, jnp.float32(1e-12))
            xn = xb / scale
            idx = jnp.searchsorted(_MID, jnp.abs(xn))
            q = _GRID[idx] * jnp.sign(xn) * scale
            return q.reshape(shape)

        def fp4_linear(x, w):
            xq = fp4_quant_dequant(x)
            wq = fp4_quant_dequant(w)
            return jnp.einsum('bsk,nk->bsn', xq, wq)
        gate = fp4_linear(x, w_gate)
        y = fp4_linear(x, w_up)
        h = jax.nn.silu(gate) * y
        return fp4_linear(h, w_down)
    x = x + jnp.tanh(g_xattn[0]) * _L0_xattn_ref(ctx_1024, _layernorm(x, axis=-1))
    x = x + jnp.tanh(g_ffn[0]) * _L0_ffn_ref(_layernorm(x, axis=-1), L0_ffn_ln1_g, L0_ffn_ln1_b, L0_ffn_Wqkv, L0_ffn_Wproj, L0_ffn_ln2_g, L0_ffn_ln2_b, L0_ffn_Wgate, L0_ffn_W1, L0_ffn_b1, L0_ffn_W2, L0_ffn_b2)
    x = x + jnp.tanh(g_xattn[1]) * _L1_xattn_ref(_layernorm(x, axis=-1), ctx_1024, ctx_1024, mask_BxSxS2_ik0, L1_xattn_Wq, L1_xattn_Wk, L1_xattn_Wv, L1_xattn_Wo)
    x = x + jnp.tanh(g_ffn[1]) * _L1_ffn_ref(_layernorm(x, axis=-1), L1_ffn_w_gate, L1_ffn_w_up, L1_ffn_w_down)
    return x

_drawn_inputs = setup_inputs


def setup_inputs(seed=0):
    import zlib

    import numpy as np

    out = dict(_drawn_inputs(seed))
    spreads = {'g_ffn': (-1.0, 0.6),
     'L0_ffn_ln1_g': (1.0, 0.6),
     'L0_ffn_ln1_b': (0.0, 0.666),
     'L0_ffn_ln2_g': (1.0, 0.6),
     'L0_ffn_ln2_b': (0.0, 0.636),
     'L0_ffn_b1': (0.0, 0.8),
     'L0_ffn_b2': (0.0, 0.333)}
    factors = {'L1_ffn_w_gate': 8.0, 'L1_ffn_w_up': 8.0, 'L1_ffn_w_down': 8.0}
    for name, (base, spread) in spreads.items():
        noise = np.random.default_rng([zlib.crc32(name.encode()), seed]).standard_normal(out[name].shape)
        drawn = base * np.exp(spread * noise) if base else spread * noise
        out[name] = jnp.asarray(drawn.astype(out[name].dtype))
    for name, factor in factors.items():
        out[name] = (out[name] * factor).astype(out[name].dtype)
    return out
```

```python
import numpy as np
import concourse.bass as bass
from concourse import mybir
from contextlib import ExitStack

F32, BF16, I32, I8 = mybir.dt.float32, mybir.dt.bfloat16, mybir.dt.int32, mybir.dt.int8
ALU, ACT, AX = mybir.AluOpType, mybir.ActivationFunctionType, mybir.AxisListType
P = 128
B, S, D, SK = 4, 512, 256, 1024
QT = S // P
KT = SK // P
NT = B * QT
DH = D // P
NBLK, RB = 32, 33
PADI = NBLK * RB
PITCH = RB + 1
SLOTS = S + NBLK
CH = 16
NCH = SLOTS // CH
ROW = SLOTS * PITCH
FAR = 1e30
FAR2 = 1e34
EPS = 1e-5


def ap_of(t, offset, dims):
    return bass.AP(tensor=t.tensor, offset=t.offset + offset, ap=dims)


def clear_released(nc):
    nums = sorted(set(nc.released_uncleared_semaphores))
    while nums:
        n = 1
        while n < len(nums) and nums[n] == nums[0] + n:
            n += 1
        nc.gpsimd.sem_clear(range(nums[0], nums[0] + n))
        nums = nums[n:]
    nc.all_engine_barrier()


def layer_norm(nc, es, x_sb, out_sb, name):
    stats = es.enter_context(nc.sbuf_tensor(f"{name}_stats", [P, NT, 6], F32))
    mv = es.enter_context(nc.sbuf_tensor(f"{name}_mv", [P, NT, 2], F32))
    std = es.enter_context(nc.sbuf_tensor(f"{name}_std", [P, NT], F32))
    rstd = es.enter_context(nc.sbuf_tensor(f"{name}_rstd", [P, NT], F32))
    stats_done = es.enter_context(nc.semaphore(f"{name}_stats_done"))
    var_done = es.enter_context(nc.semaphore(f"{name}_var_done"))
    std_done = es.enter_context(nc.semaphore(f"{name}_std_done"))
    rstd_done = es.enter_context(nc.semaphore(f"{name}_rstd_done"))
    with nc.Block() as block:
        @block.vector
        def _(dve):
            for t in range(NT):
                nc.vector.bn_stats(stats[:, t, :], x_sb[:, t, :]).then_inc(stats_done, 1)
            for t in range(NT):
                dve.wait_ge(stats_done, t + 1)
                nc.vector.bn_aggr(mv[:, t, :], stats[:, t, :]).then_inc(var_done, 1)
            dve.wait_ge(var_done, NT)
            nc.vector.tensor_scalar(std[:, :], mv[:, :, 1], EPS, None, ALU.add).then_inc(var_done, 1)
            dve.wait_ge(std_done, 1)
            nc.vector.reciprocal(rstd[:, :], std[:, :]).then_inc(rstd_done, 1)
            dve.wait_ge(rstd_done, 1)
            for t in range(NT):
                nc.vector.tensor_scalar(out_sb[:, t, :], x_sb[:, t, :], mv[:, t, 0:1], rstd[:, t:t + 1],
                                        ALU.subtract, ALU.mult)

        @block.scalar
        def _(act):
            act.wait_ge(var_done, NT + 1)
            nc.scalar.activation(std[:, :], std[:, :], ACT.Sqrt).then_inc(std_done, 1)


def transpose_tokens(nc, es, src, dst, ident, name, scale=None, bias=None, mul=1.0):
    ps = [es.enter_context(nc.psum_tensor(f"{name}_ps{i}", [P, 512], F32)) for i in range(2)]
    turned = es.enter_context(nc.semaphore(f"{name}_turned"))
    copied = es.enter_context(nc.semaphore(f"{name}_copied"))
    groups = src.shape[1] // 4
    with nc.Block() as block:
        @block.tensor
        def _(pe):
            for n in range(groups * DH):
                g, h = n // DH, n % DH
                if n >= 2:
                    pe.wait_ge(copied, n - 1)
                for q in range(4):
                    last = nc.tensor.transpose(ps[n % 2][:, q * P:(q + 1) * P],
                                               src[:, 4 * g + q, h * P:(h + 1) * P], ident[:, :])
                last.then_inc(turned, 1)

        @block.vector
        def _(dve):
            for n in range(groups * DH):
                g, h = n // DH, n % DH
                dve.wait_ge(turned, n + 1)
                out = dst(g, h)
                if scale is not None:
                    i = nc.vector.tensor_scalar(out, ps[n % 2][:, :], scale[:, h:h + 1], bias[:, h:h + 1],
                                                ALU.mult, ALU.add)
                else:
                    i = nc.vector.tensor_scalar(out, ps[n % 2][:, :], float(mul), None, ALU.mult)
                i.then_inc(copied, 1)


def dtw_block(nc, d, x_sb, ident, ctxT):
    dist = nc.dram_tensor("dist", [P, ROW], F32).ap()
    path = nc.dram_tensor("path", [P, ROW], BF16).ap()
    with ExitStack() as es:
        xnT = es.enter_context(nc.sbuf_tensor("xnT", [P, DH, B * S], F32))
        with ExitStack() as es1:
            xn = es1.enter_context(nc.sbuf_tensor("dtw_xn", [P, NT, D], F32))
            layer_norm(nc, es1, x_sb, xn, "ln0")
            transpose_tokens(nc, es1, xn, lambda g, h: xnT[:, h, g * 512:(g + 1) * 512], ident, "xT", mul=-2.0)
        dtw_distances(nc, d, xnT, ctxT, dist)
    dtw_path(nc, d, dist, path)
    dtw_expand(nc, d, x_sb, path)


def dtw_distances(nc, d, xnT, ctxT, dist):
    with ExitStack() as es:
        sq = es.enter_context(nc.sbuf_tensor("sq", [P, 2, 2, 512], F32))
        ones2 = es.enter_context(nc.sbuf_tensor("ones2", [P, 2, 2], F32))
        add2 = es.enter_context(nc.sbuf_tensor("add2", [2, 2], F32))
        rows_i = es.enter_context(nc.sbuf_tensor("rows_i", [2, B, PADI], F32))
        rows_j = es.enter_context(nc.sbuf_tensor("rows_j", [2, B, S], F32))
        stage = es.enter_context(nc.sbuf_tensor("stage", [P, SLOTS, PITCH], F32))
        ps_n = [es.enter_context(nc.psum_tensor(f"ps_n{i}", [P, 512], F32)) for i in range(2)]
        ps_d = [es.enter_context(nc.psum_tensor(f"ps_d{i}", [P, 512], F32)) for i in range(2)]
        consts = es.enter_context(nc.semaphore("d_consts"))
        squared = es.enter_context(nc.semaphore("squared"))
        normed = es.enter_context(nc.semaphore("normed"))
        norm_kept = es.enter_context(nc.semaphore("norm_kept"))
        prod = es.enter_context(nc.semaphore("d_prod"))
        clipped = es.enter_context(nc.semaphore("d_clipped"))
        rooted = es.enter_context(nc.semaphore("d_rooted"))
        filled = es.enter_context(nc.semaphore("d_filled"))
        stored = es.enter_context(nc.semaphore("d_stored"))
        jobs = [(0, b, c, 1.0) for b in range(B) for c in range(0, SK, 512)] + [(1, b, 0, 0.25) for b in range(B)]
        with nc.Block() as block:
            def keep_norm(dve, n):
                w, b, c, f = jobs[n]
                if n == 0:
                    dve.wait_ge(consts, 32)
                    dve.wait_ge(filled, 4)
                dve.wait_ge(normed, n + 1)
                dst = rows_j[:, b, :] if w else rows_i[:, b, c:c + 512]
                nc.vector.tensor_scalar(dst, ps_n[n % 2][0:2, :], add2[:, w:w + 1], None,
                                        ALU.add).then_inc(norm_kept, 1)

            @block.sync
            def _(sp):
                sp.dma_start(ones2[:], d["c_ones2"]).then_inc(consts, 16)
                sp.dma_start(add2[:], d["c_add2"]).then_inc(consts, 16)

            @block.gpsimd
            def _(pool):
                nc.gpsimd.memset(rows_i[:, :, :], 1.0).then_inc(filled, 1)
                pool.wait_ge(filled, 1)
                nc.gpsimd.memset(rows_i[0:1, :, SK:PADI], FAR2).then_inc(filled, 1)
                nc.gpsimd.memset(stage[:, S:SLOTS, :], FAR).then_inc(filled, 1)
                nc.gpsimd.memset(stage[:, 0:S, 0], FAR).then_inc(filled, 1)

            @block.vector
            def _(dve):
                for n, (w, b, c, f) in enumerate(jobs):
                    if n >= 2:
                        dve.wait_ge(normed, n - 1)
                    for h in range(DH):
                        src = xnT[:, h, b * S:(b + 1) * S] if w else ctxT[:, b, h, c:c + 512]
                        i = nc.vector.scalar_tensor_tensor(sq[:, n % 2, h, :], src, f, src, ALU.mult, ALU.mult)
                    i.then_inc(squared, 1)
                    if n >= 1:
                        keep_norm(dve, n - 1)
                keep_norm(dve, len(jobs) - 1)

            @block.tensor
            def _(pe):
                pe.wait_ge(consts, 32)
                for n, (w, b, c, f) in enumerate(jobs):
                    pe.wait_ge(squared, n + 1)
                    if n >= 2:
                        pe.wait_ge(norm_kept, n - 1)
                    for h in range(DH):
                        last = nc.tensor.matmul(ps_n[n % 2][0:2, :], ones2[:, w, :], sq[:, n % 2, h, :],
                                                start=(h == 0), stop=(h == DH - 1))
                    last.then_inc(normed, 1)
        with nc.Block() as block:
            @block.tensor
            def _(pe):
                for k in range(RB):
                    if k >= 2:
                        pe.wait_ge(clipped, k - 1)
                    for b in range(B):
                        o = ps_d[k % 2][32 * b:32 * b + 32, :]
                        for h in range(DH):
                            nc.tensor.matmul(o, ctxT[:, b, h, k:PADI:RB], xnT[:, h, b * S:(b + 1) * S],
                                             start=(h == 0), stop=False, tile_position=(0, 32 * b))
                        last = nc.tensor.matmul(o, rows_i[:, b, k:PADI:RB], rows_j[:, b, :], start=False, stop=True,
                                                tile_position=(0, 32 * b))
                    last.then_inc(prod, 1)

            @block.vector
            def _(dve):
                for k in range(RB):
                    dve.wait_ge(prod, k + 1)
                    nc.vector.tensor_scalar(stage[:, 0:S, 1 + k], ps_d[k % 2][:, :], 0.0, None,
                                            ALU.max).then_inc(clipped, 1)

            @block.scalar
            def _(act):
                for k in range(RB):
                    act.wait_ge(clipped, k + 1)
                    nc.scalar.activation(stage[:, 0:S, 1 + k], stage[:, 0:S, 1 + k], ACT.Sqrt).then_inc(rooted, 1)

            @block.sync
            def _(sp):
                sp.wait_ge(rooted, RB)
                sp.dma_start(dist.rearrange("p (s k) -> p s k", k=PITCH), stage[:, :, :]).then_inc(stored, 16)
                sp.wait_ge(stored, 16)


def dtw_path(nc, d, dist, path):
    with ExitStack() as es:
        def sb(name, shape, dt):
            return es.enter_context(nc.sbuf_tensor(name, shape, dt))

        def sem(name):
            return es.enter_context(nc.semaphore(name))

        code_all = sb("code_all", [P, SLOTS + 1, RB], I8)
        up_all = sb("up_all", [P, SLOTS + 1, RB], I8)
        cost = [sb(f"cost{i}", [P, CH + 1, PITCH], F32) for i in range(2)]
        m = sb("m", [P, CH, RB], F32)
        left_ok = sb("left_ok", [P, CH, RB], BF16)
        best = sb("best", [P, CH, RB], F32)
        diag = sb("diag", [P, CH, RB], BF16)
        up = [sb(f"up{i}", [P, CH, RB], BF16) for i in range(2)]
        code = [sb(f"code{i}", [P, CH, RB], BF16) for i in range(2)]
        loaded = [sem(f"dist_loaded{i}") for i in range(2)]
        freed = [sem(f"dist_freed{i}") for i in range(2)]
        seeded, edge, minned, scanned = sem("seeded"), sem("edge"), sem("minned"), sem("scanned")
        ruled, coded, kept = sem("ruled"), sem("coded"), sem("kept")
        shift_up = [NBLK - 1] + list(range(NBLK - 1))
        with nc.Block() as block:
            @block.sync
            def _(sp):
                sp.dma_start(cost[1][:, CH, :], d["c_corner"]).then_inc(seeded, 16)
                with sp.Fori(0, NCH // 2) as it:
                    for h in range(2):
                        sp.wait_ge(freed[h], it + 1)
                        src = ap_of(dist, (2 * it + h) * (CH * PITCH),
                                    [[NBLK * ROW, B], [ROW - PITCH, NBLK], [PITCH, CH], [1, PITCH]])
                        sp.dma_start(cost[h][:, 1:CH + 1, :], src).then_inc(loaded[h], 16)

            @block.vector
            def _(dve):
                nc.vector.nop().then_inc(freed[0], 1)
                nc.vector.nop().then_inc(coded, 1)
                dve.wait_ge(seeded, 16)
                with dve.Fori(0, NCH // 2) as it:
                    for h in range(2):
                        w, before = cost[h], cost[1 - h]
                        dve.wait_ge(coded, it * 2 + h + 1)
                        dve.wait_ge(loaded[h], it * 16 + 16)
                        nc.vector.tensor_copy(w[:, 0, :], before[:, CH, :]).then_inc(edge, 1)
                        for s in range(CH):
                            n = h * CH + s
                            if s == 0:
                                dve.wait_ge(edge, h + 1)
                                nc.vector.nop().then_inc(freed[1 - h], 1)
                            else:
                                dve.wait_ge(scanned, n)
                            nc.vector.stream_shuffle(w[:, s + 1, 0:1], w[:, s, RB:RB + 1], shift_up)
                            nc.vector.tensor_tensor(m[:, s, :], w[:, s, 0:RB], w[:, s, 1:PITCH],
                                                    ALU.min).then_inc(minned, 1)
                            dve.wait_ge(minned, n + 1)
                            nc.vector.tensor_tensor_scan(w[:, s + 1, 1:PITCH], m[:, s, :], w[:, s + 1, 1:PITCH],
                                                         w[:, s + 1, 0:1], ALU.min, ALU.add).then_inc(scanned, 1)
                        dve.wait_ge(scanned, (h + 1) * CH)
                        cu, cd, cl = w[:, 1:CH + 1, 0:RB], w[:, 0:CH, 0:RB], w[:, 0:CH, 1:PITCH]
                        nc.vector.tensor_tensor(left_ok[:], cu, cl, ALU.is_le)
                        nc.vector.tensor_tensor(best[:], cu, cl, ALU.min).then_inc(ruled, 1)
                        dve.wait_ge(ruled, 3 * h + 1)
                        nc.vector.tensor_tensor(diag[:], cd, best[:], ALU.is_le).then_inc(ruled, 1)
                        dve.wait_ge(ruled, 3 * h + 2)
                        dve.wait_ge(kept, it * 2 + h + 1)
                        nc.vector.tensor_tensor(up[h][:], left_ok[:], diag[:], ALU.is_gt).then_inc(ruled, 1)
                        dve.wait_ge(ruled, 3 * h + 3)
                        nc.vector.scalar_tensor_tensor(code[h][:], diag[:], -2.0, up[h][:], ALU.mult,
                                                       ALU.subtract).then_inc(coded, 1)
                    dve.sem_clear(scanned)
                    dve.sem_clear(minned)
                    dve.sem_clear(edge)
                    dve.sem_clear(ruled)

            @block.scalar
            def _(act):
                nc.scalar.nop().then_inc(kept, 1)
                with act.Fori(0, NCH // 2) as it:
                    for h in range(2):
                        act.wait_ge(coded, it * 2 + h + 2)
                        at = it * (2 * CH) + h * CH
                        nc.scalar.copy(up_all[:, bass.ds(at, CH), :], up[h][:])
                        nc.scalar.copy(code_all[:, bass.ds(at, CH), :], code[h][:]).then_inc(kept, 1)
        backtrack(nc, d, es, code_all, up_all, path)


def backtrack(nc, d, es, code_all, up_all, path):
    def sb(name, shape, dt):
        return es.enter_context(nc.sbuf_tensor(name, shape, dt))

    def sem(name):
        return es.enter_context(nc.semaphore(name))

    on = [sb(f"on{i}", [P, CH, PITCH], BF16) for i in range(2)]
    up = [sb(f"bup{i}", [P, CH + 1, PITCH], BF16) for i in range(2)]
    code = [sb(f"bcode{i}", [P, CH + 1, PITCH], BF16) for i in range(2)]
    leave = sb("leave", [P, CH, PITCH], BF16)
    enter = sb("enter", [P, CH, RB], BF16)
    inner = sb("inner", [P, 2], F32)
    b_end, fetched = sem("b_end"), sem("fetched")
    edges, left, entered, traced = sem("b_edges"), sem("b_left"), sem("b_entered"), sem("b_traced")
    done, saved = sem("b_done"), [sem("b_saved0"), sem("b_saved1")]
    read = [sem("b_read0"), sem("b_read1")]
    shift_down = list(range(1, NBLK)) + [0]
    with nc.Block() as block:
        @block.sync
        def _(sp):
            sp.dma_start(inner[:], d["c_inner"]).then_inc(saved[0], 16)
            sp.dma_start(on[1][:, 0, :], d["c_seed"].bitcast(BF16)).then_inc(saved[1], 16)
            with sp.Fori(0, NCH // 2) as it:
                for h in range(2):
                    sp.wait_ge(done, it * 2 + h + 1)
                    at = (it * (-2 * CH * PITCH)) + (NCH - 1 - h) * CH * PITCH
                    sp.dma_start(path[:, bass.ds(at, CH * PITCH)].rearrange("p (s k) -> p s k", k=PITCH),
                                 on[h][:]).then_inc(saved[h], 16)
            for h in range(2):
                sp.wait_ge(saved[h], 16 * (NCH // 2) + 16)

        @block.gpsimd
        def _(pool):
            nc.gpsimd.memset(code_all[:, SLOTS - 1:SLOTS + 1, :], 0.0).then_inc(b_end, 1)
            nc.gpsimd.memset(up_all[:, SLOTS - 1:SLOTS + 1, :], 0.0).then_inc(b_end, 1)

        @block.scalar
        def _(act):
            act.wait_ge(b_end, 2)
            with act.Fori(0, NCH // 2) as it:
                for h in range(2):
                    at = (it * (-2 * CH)) + (NCH - 1 - h) * CH
                    act.wait_ge(read[h], it + 1)
                    nc.scalar.copy(up[h][:, :, 0:RB], up_all[:, bass.ds(at, CH + 1), :])
                    nc.scalar.copy(code[h][:, :, 0:RB], code_all[:, bass.ds(at, CH + 1), :]).then_inc(fetched, 1)

        @block.vector
        def _(dve):
            nc.vector.memset(code[1][:, 0, RB:PITCH], 0.0).then_inc(read[0], 1)
            dve.wait_ge(read[0], 1)
            nc.vector.nop().then_inc(read[1], 1)
            for h in range(2):
                dve.wait_ge(saved[h], 16)
            with dve.Fori(0, NCH // 2) as it:
                for h in range(2):
                    dve.wait_ge(fetched, it * 2 + h + 1)
                    nc.vector.tensor_copy(code[h][:, CH, RB:PITCH], code[1 - h][:, 0, RB:PITCH]).then_inc(edges, 1)
                    nc.vector.stream_shuffle(up[h][:, 0:CH, RB], up[h][:, 1:CH + 1, 0], shift_down)
                    nc.vector.stream_shuffle(code[h][:, 0:CH, RB], code[h][:, 1:CH + 1, 0],
                                             shift_down).then_inc(edges, 1)
                    dve.wait_ge(edges, 3 * h + 2)
                    nc.vector.tensor_scalar(up[h][:, 0:CH, RB], up[h][:, 0:CH, RB], inner[:, 0:1], None, ALU.mult)
                    nc.vector.tensor_scalar(code[h][:, 0:CH, RB], code[h][:, 0:CH, RB], inner[:, 0:1],
                                            inner[:, 1:2], ALU.mult, ALU.add).then_inc(edges, 1)
                    dve.wait_ge(edges, 3 * h + 3)
                    for s in range(CH - 1, -1, -1):
                        n = h * CH + CH - 1 - s
                        if n:
                            dve.wait_ge(traced, n)
                        if s == CH - 1:
                            dve.wait_ge(saved[h], it * 16 + 16)
                        after = on[h][:, s + 1, :] if s < CH - 1 else on[1 - h][:, 0, :]
                        nc.vector.scalar_tensor_tensor(leave[:, s, :], code[h][:, s + 1, :], 1.0, after,
                                                       ALU.add, ALU.mult).then_inc(left, 1)
                        nc.vector.stream_shuffle(on[h][:, s, RB:PITCH], after[:, 0:1], shift_down)
                        dve.wait_ge(left, n + 1)
                        nc.vector.scalar_tensor_tensor(enter[:, s, :], leave[:, s, 1:PITCH], -1.0,
                                                       leave[:, s, 0:RB], ALU.mult, ALU.max).then_inc(entered, 1)
                        dve.wait_ge(entered, n + 1)
                        nc.vector.tensor_tensor_scan(on[h][:, s, 0:RB][:, ::-1], up[h][:, s, 1:PITCH][:, ::-1],
                                                     enter[:, s, :][:, ::-1], on[h][:, s, RB:PITCH],
                                                     ALU.mult, ALU.add).then_inc(traced, 1)
                    dve.wait_ge(traced, (h + 1) * CH)
                    nc.vector.nop().then_inc(done, 1)
                    if h == 1:
                        nc.vector.nop().then_inc(read[0], 1)
                        nc.vector.nop().then_inc(read[1], 1)
                for s in (edges, left, entered, traced):
                    dve.sem_clear(s)


def dtw_expand(nc, d, x_sb, path):
    with ExitStack() as es:
        def sb(name, shape, dt):
            return es.enter_context(nc.sbuf_tensor(name, shape, dt))

        def sem(name):
            return es.enter_context(nc.semaphore(name))

        onp = sb("onp", [P, S, PITCH], BF16)
        rows = sb("ctx_rows", [P, RB, D], F32)
        rest = sb("ctx_rest", [P, RB, D], F32)
        part = [sb(f"ctx_part{i}", [P, RB, D], BF16) for i in range(3)]
        gate = sb("x_gate", [P, 2], F32)
        ps = [es.enter_context(nc.psum_tensor(f"ps_e{i}", [P, 512], F32)) for i in range(4)]
        got_path, got_rows, zeroed, split = sem("got_path"), sem("got_rows"), sem("zeroed"), sem("split")
        gated, summed, added = sem("gated"), sem("summed"), sem("e_added")
        with nc.Block() as block:
            @block.sync
            def _(sp):
                src = ap_of(path, 0, [[NBLK * ROW, B], [ROW + PITCH, NBLK], [1, S * PITCH]])
                sp.dma_start(onp[:, :, :].rearrange("p s k -> p (s k)"), src).then_inc(got_path, 16)
                sp.wait_ge(zeroed, 1)
                for b in range(B):
                    c = d["ctx_1024"][b]
                    full = (SK // RB)
                    sp.dma_start(rows[32 * b:32 * b + full, :, :],
                                 c[0:full * RB, :].rearrange("(c k) d -> c k d", k=RB)).then_inc(got_rows, 16)
                    sp.dma_start(rows[32 * b + full:32 * b + full + 1, 0:SK - full * RB, :],
                                 c[full * RB:SK, :].rearrange("(c k) d -> c k d", c=1)).then_inc(got_rows, 16)
                sp.dma_start(gate[:], ap_of(d["g_xattn"], 0, [[0, P], [1, 2]])).then_inc(gated, 16)

            @block.gpsimd
            def _(pool):
                nc.gpsimd.memset(rows[:, :, :], 0.0).then_inc(zeroed, 1)

            @block.scalar
            def _(act):
                act.wait_ge(gated, 16)
                nc.scalar.activation(gate[:], gate[:], ACT.Tanh).then_inc(gated, 1)

            @block.vector
            def _(dve):
                dve.wait_ge(got_rows, 16 * 2 * B)
                nc.vector.tensor_copy(part[0][:], rows[:]).then_inc(split, 1)
                dve.wait_ge(split, 1)
                nc.vector.tensor_tensor(rest[:], rows[:], part[0][:], ALU.subtract).then_inc(split, 1)
                dve.wait_ge(split, 2)
                nc.vector.tensor_copy(part[1][:], rest[:]).then_inc(split, 1)
                dve.wait_ge(split, 3)
                nc.vector.tensor_tensor(part[2][:], rest[:], part[1][:], ALU.subtract).then_inc(split, 1)
                dve.wait_ge(gated, 17)
                for jt in range(QT):
                    dve.wait_ge(summed, jt + 1)
                    for b in range(B):
                        t = b * QT + jt
                        i = nc.vector.scalar_tensor_tensor(x_sb[:, t, :], ps[b][:, 256 * (jt % 2):256 * (jt % 2) + D],
                                                           gate[:, 0:1], x_sb[:, t, :], ALU.mult, ALU.add)
                    i.then_inc(added, 1)

            @block.tensor
            def _(pe):
                pe.wait_ge(got_path, 16)
                pe.wait_ge(split, 4)
                for jt in range(QT):
                    if jt >= 1:
                        pe.wait_ge(added, jt)
                    for k in range(RB):
                        for q in range(3):
                            for b in range(B):
                                r = slice(32 * b, 32 * b + 32)
                                last = nc.tensor.matmul(ps[b][:, 256 * (jt % 2):256 * (jt % 2) + D],
                                                        onp[r, jt * P:(jt + 1) * P, k], part[q][r, k, :],
                                                        start=(k == 0 and q == 0), stop=(k == RB - 1 and q == 2),
                                                        tile_position=(32 * b, 0))
                    last.then_inc(summed, 1)


NH, HD = 16, 16
HG = 4
NG = NH // HG
NPART = 6
STK = NPART * HD
MAXR = 3
VW = 32
NEG = -1e30
K_SLOTS = ((0, 1, 2), (3, 4), (5,))
Q_SLOTS = ((0, 3, 5), (1, 4), (2,))


class Names:

    def __init__(self, nc, es, stage):
        self.nc, self.es, self.stage = nc, es, stage
        self.sems = []

    def sb(self, name, shape, dt=F32):
        return self.es.enter_context(self.nc.sbuf_tensor(f"{self.stage}_{name}", shape, dt))

    def ps(self, name, shape, dt=F32):
        return self.es.enter_context(self.nc.psum_tensor(f"{self.stage}_{name}", shape, dt))

    def sem(self, name):
        s = self.es.enter_context(self.nc.semaphore(f"{self.stage}_{name}"))
        self.sems.append(s)
        return s

    def clear(self):
        for s in self.sems:
            self.nc.gpsimd.sem_clear(s)
        self.nc.all_engine_barrier()


def project_tokens(nc, nm, jobs):
    ps = [nm.ps(f"proj{i}", [P, 512]) for i in range(2)]
    done, kept = nm.sem("proj_done"), [nm.sem("proj_kept0"), nm.sem("proj_kept1")]
    static = nm.sem("proj_in")

    def run(copies):
        with nc.Block() as block:
            @block.scalar
            def _(act):
                for dst, src in copies:
                    last = nc.scalar.copy(dst, src)
                last.then_inc(static, 1)
                for n, (out, lhs, rhs, view) in enumerate(jobs):
                    if n % 2:
                        act.wait_ge(done, n + 1)
                        nc.scalar.copy(out, view(ps[n % 2])).then_inc(kept[1], 1)

            @block.vector
            def _(dve):
                for n, (out, lhs, rhs, view) in enumerate(jobs):
                    if n % 2 == 0:
                        dve.wait_ge(done, n + 1)
                        nc.vector.tensor_copy(out, view(ps[n % 2])).then_inc(kept[0], 1)

            @block.tensor
            def _(pe):
                pe.wait_ge(static, 1)
                for n, (out, lhs, rhs, view) in enumerate(jobs):
                    if n >= 2:
                        pe.wait_ge(kept[n % 2], n // 2)
                    for h in range(DH):
                        last = nc.tensor.matmul(ps[n % 2][:, 0:rhs[h].shape[1]], lhs[h], rhs[h],
                                                start=(h == 0), stop=(h == DH - 1))
                    last.then_inc(done, 1)
    return run


def split_stacks(nc, nm, jobs):
    first, rest1, second, third = nm.sem("sp_first"), nm.sem("sp_rest"), nm.sem("sp_second"), nm.sem("sp_third")
    with nc.Block() as block:
        @block.vector
        def _(dve):
            for n, (src, stk, slots, scale, rest) in enumerate(jobs):
                def at(part, i=0):
                    s = slots[part][i]
                    return stk[:, :, s * HD:(s + 1) * HD]
                nc.vector.tensor_scalar(at(0), src, scale, None, ALU.mult).then_inc(first, 1)
                dve.wait_ge(first, n + 1)
                nc.vector.scalar_tensor_tensor(rest, src, scale, at(0), ALU.mult, ALU.subtract).then_inc(rest1, 1)
                dve.wait_ge(rest1, n + 1)
                nc.vector.tensor_copy(at(1), rest).then_inc(second, 1)
                dve.wait_ge(second, n + 1)
                nc.vector.tensor_tensor(at(2), rest, at(1), ALU.subtract).then_inc(third, 1)

        @block.gpsimd
        def _(pool):
            for n, (src, stk, slots, scale, rest) in enumerate(jobs):
                pool.wait_ge(second, n + 1)
                a, b = slots[1]
                nc.gpsimd.tensor_copy(stk[:, :, b * HD:(b + 1) * HD], stk[:, :, a * HD:(a + 1) * HD])

        @block.scalar
        def _(act):
            for n, (src, stk, slots, scale, rest) in enumerate(jobs):
                act.wait_ge(first, n + 1)
                a = slots[0][0]
                for b in slots[0][1:]:
                    nc.scalar.copy(stk[:, :, b * HD:(b + 1) * HD], stk[:, :, a * HD:(a + 1) * HD])


def turn_stacks(nc, nm, identb, jobs):
    ps = [nm.ps(f"turn{i}", [STK, 1024], BF16) for i in range(2)]
    turned, kept = nm.sem("turn_done"), [nm.sem("turn_kept0"), nm.sem("turn_kept1")]
    units = []
    for stk, tiles, out in jobs:
        per = 1024 // (tiles * P)
        units += [(stk, tiles, out, h0, per) for h0 in range(0, NH, per)]
    with nc.Block() as block:
        @block.tensor
        def _(pe):
            for n, (stk, tiles, out, h0, per) in enumerate(units):
                if n >= 2:
                    pe.wait_ge(kept[n % 2], n // 2)
                for i in range(per):
                    for t in range(tiles):
                        c = (i * tiles + t) * P
                        last = nc.tensor.transpose(ps[n % 2][:, c:c + P], stk[:, t, h0 + i, :], identb[:, :])
                last.then_inc(turned, 1)

        def copies(eng, parity, copy):
            for n, (stk, tiles, out, h0, per) in enumerate(units):
                if n % 2 == parity:
                    eng.wait_ge(turned, n + 1)
                    copy(out[0:STK, h0:h0 + per, :], ps[n % 2][:, :].rearrange("p (h s) -> p h s", h=per)).then_inc(
                        kept[parity], 1)

        @block.vector
        def _(dve):
            copies(dve, 0, nc.vector.tensor_copy)

        @block.scalar
        def _(act):
            copies(act, 1, nc.scalar.copy)


def attend(nc, nm, ident, identb, qT, kT, vt, attn, keys, causal, bias_q, bias_k):
    kt_n = keys // P
    halves = max(1, keys // 512)
    ps1 = [nm.ps(f"s1_{i}", [P, 512]) for i in range(2)]
    ps2 = [nm.ps(f"s2_{i}", [P, 512]) for i in range(3)]
    psm = nm.ps("mx", [MAXR, 1024], BF16)
    pso = nm.ps("o", [P, 512])
    pst = nm.ps("ot", [P, 512])
    NE = 4
    ebuf = [nm.sb(f"exp{i}", [P, 512]) for i in range(NE)]
    NJ = 4
    junk = nm.sb("junk", [P, NJ, 512], BF16)
    mx = nm.sb("max", [P, 2, HG, QT, halves])
    neg = nm.sb("neg", [P, HG * QT])
    negr = nm.sb("negr", [P, HG * QT])
    parts = nm.sb("parts", [P, 2, HG * QT, MAXR], BF16)
    osb = nm.sb("osb", [P, 2, 512])
    rden = nm.sb("rden", [P, HG * QT])
    scored, maxed = nm.sem("scored"), nm.sem("maxed")
    negated, parted = nm.sem("negated"), nm.sem("parted")
    mturned, mkept = nm.sem("mturned"), nm.sem("mkept")
    scored2, exped, weighed = nm.sem("scored2"), nm.sem("exped"), nm.sem("weighed")
    okept, oturned, inverted, normed = nm.sem("okept"), nm.sem("oturned"), nm.sem("inverted"), nm.sem("normed")
    u1 = [(h, qt, f) for h in range(HG) for qt in range(QT) for f in range(halves)]
    u2 = [(kt, h) for kt in range(kt_n) for h in range(HG)]
    n1, n2 = len(u1), len(u2)
    LAG = 2

    def width1(qt):
        return (qt + 1) * P if causal else 512

    with nc.Block() as block:
        @block.tensor
        def _(pe):
            def first(g, u):
                h, qt, f = u1[u]
                n = g * n1 + u
                if n >= 2:
                    pe.wait_ge(maxed, n - 1)
                w = width1(qt)
                nc.tensor.matmul(ps1[n % 2][:, 0:w], qT[0:STK, g * HG + h, qt * P:(qt + 1) * P],
                                 kT[0:STK, g * HG + h, f * 512:f * 512 + w], start=True, stop=True).then_inc(scored, 1)

            def turn_max(g):
                for pair in range(HG // 2):
                    pe.wait_ge(parted, 3 * (g + 1))
                    if g or pair:
                        pe.wait_ge(mkept, g * (HG // 2) + pair)
                    for i in range(2):
                        for qt in range(QT):
                            c = (i * QT + qt) * P
                            last = nc.tensor.transpose(psm[:, c:c + P], parts[:, g % 2, (2 * pair + i) * QT + qt, :],
                                                       identb[:, :])
                    last.then_inc(mturned, 1)

            def second(g, u):
                kt, h = u2[u]
                n = g * n2 + u
                if u == 0:
                    pe.wait_ge(mkept, (g + 1) * (HG // 2))
                if n >= 3:
                    pe.wait_ge(exped, n - 2)
                q0 = kt * P if causal else 0
                o = ps2[n % 3]
                nc.tensor.matmul(o[:, q0:512], kT[:, g * HG + h, kt * P:(kt + 1) * P], qT[:, g * HG + h, q0:512],
                                 start=True, stop=False)
                w = P if causal else 512
                nc.tensor.matmul(o[:, q0:q0 + w], identb[:, :], bias_k(kt), start=False,
                                 stop=True).then_inc(scored2, 1)

            def weigh(g, u):
                kt, h = u2[u]
                n = g * n2 + u
                pe.wait_ge(exped, n + 1)
                if u == 0 and g:
                    pe.wait_ge(okept, g)
                q0 = kt * P if causal else 0
                nc.tensor.matmul(pso[32 * h:32 * h + 32, q0:512], vt[:, kt, g * HG + h, :], ebuf[n % NE][:, q0:512],
                                 start=(kt == 0), stop=(kt == kt_n - 1), tile_position=(0, 32 * h),
                                 skip_group_check=True).then_inc(weighed, 1)

            def turn_out(g):
                pe.wait_ge(okept, g + 1)
                if g:
                    pe.wait_ge(normed, g)
                for qt in range(QT):
                    last = nc.tensor.transpose(pst[:, qt * P:(qt + 1) * P], osb[:, g % 2, qt * P:(qt + 1) * P],
                                               ident[:, :])
                last.then_inc(oturned, 1)

            for u in range(n1):
                first(0, u)
            turn_max(0)
            for g in range(NG):
                for u in range(n2):
                    second(g, u)
                    if g + 1 < NG and u < n1:
                        first(g + 1, u)
                    if u >= LAG:
                        weigh(g, u - LAG)
                    if u == LAG + 2 and g:
                        turn_out(g - 1)
                for u in range(n2 - LAG, n2):
                    weigh(g, u)
                if g + 1 < NG:
                    turn_max(g + 1)
            turn_out(NG - 1)

        @block.vector
        def _(dve):
            def take_max(g, u):
                h, qt, f = u1[u]
                n = g * n1 + u
                dve.wait_ge(scored, n + 1)
                w = width1(qt)
                if n >= NJ:
                    dve.wait_ge(maxed, n - NJ + 1)
                nc.vector.tensor_tensor_reduce(junk[:, n % NJ, 0:w], ps1[n % 2][:, 0:w], bias_q(qt, f), 1.0, NEG * 4,
                                               ALU.add, ALU.max, mx[:, g % 2, h, qt, f:f + 1]).then_inc(maxed, 1)

            def negate(g):
                dve.wait_ge(maxed, (g + 1) * n1)
                if g:
                    dve.wait_ge(parted, 3 * g)
                m = mx[:, g % 2, :, :, :].rearrange("p h t f -> p (h t) f")
                nc.vector.tensor_reduce(neg[:, :], m, AX.X, ALU.max, negate=True).then_inc(negated, 1)
                dve.wait_ge(negated, 3 * g + 1)
                p3 = parts[:, g % 2, :, :]
                nc.vector.tensor_copy(p3[:, :, 0], neg[:, :]).then_inc(parted, 1)
                dve.wait_ge(parted, 3 * g + 1)
                nc.vector.tensor_tensor(negr[:, :], neg[:, :], p3[:, :, 0], ALU.subtract).then_inc(negated, 1)
                dve.wait_ge(negated, 3 * g + 2)
                nc.vector.tensor_copy(p3[:, :, 1], negr[:, :]).then_inc(parted, 1)
                dve.wait_ge(parted, 3 * g + 2)
                nc.vector.tensor_tensor(neg[:, :], negr[:, :], p3[:, :, 1], ALU.subtract).then_inc(negated, 1)
                dve.wait_ge(negated, 3 * g + 3)
                nc.vector.tensor_copy(p3[:, :, 2], neg[:, :]).then_inc(parted, 1)

            def normalise(g):
                dve.wait_ge(oturned, g + 1)
                if g:
                    dve.wait_ge(normed, g)
                t = pst[:, :].rearrange("p (t h e) -> p t h e", t=QT, h=HG)
                r = rden[:, :].rearrange("p (t h) -> p t h", t=QT)
                nc.vector.reciprocal(r, t[:, :, :, HD]).then_inc(inverted, 1)
                dve.wait_ge(inverted, g + 1)
                for qt in range(QT):
                    o = attn[:, qt, g * HG * HD:(g + 1) * HG * HD].rearrange("p (h e) -> p h e", h=HG)
                    rb = ap_of(rden[:, qt * HG:(qt + 1) * HG], 0, [rden[:, :].ap[0], [1, HG], [0, HD]])
                    i = nc.vector.tensor_tensor(o, t[:, qt, :, 0:HD], rb, ALU.mult)
                i.then_inc(normed, 1)

            for u in range(n1):
                take_max(0, u)
            negate(0)
            for g in range(NG):
                for u in range(n1):
                    if g + 1 < NG:
                        take_max(g + 1, u)
                    if u == LAG + 3 and g:
                        normalise(g - 1)
                if g + 1 < NG:
                    negate(g + 1)
            normalise(NG - 1)

        @block.scalar
        def _(act):
            def keep_max(g):
                for pair in range(HG // 2):
                    act.wait_ge(mturned, g * (HG // 2) + pair + 1)
                    h0 = g * HG + 2 * pair
                    nc.scalar.copy(qT[STK:STK + MAXR, h0:h0 + 2, :],
                                   psm[:, :].rearrange("p (h s) -> p h s", h=2)).then_inc(mkept, 1)

            keep_max(0)
            for g in range(NG):
                for u in range(n2):
                    n = g * n2 + u
                    kt, h = u2[u]
                    q0 = kt * P if causal else 0
                    act.wait_ge(scored2, n + 1)
                    if n >= NE:
                        act.wait_ge(weighed, n - NE + 1)
                    nc.scalar.activation(ebuf[n % NE][:, q0:512], ps2[n % 3][:, q0:512], ACT.Exp).then_inc(exped, 1)
                act.wait_ge(weighed, (g + 1) * n2)
                if g >= 2:
                    act.wait_ge(oturned, g - 1)
                nc.scalar.copy(osb[:, g % 2, :], pso[:, :]).then_inc(okept, 1)
                if g + 1 < NG:
                    keep_max(g + 1)


def project_out(nc, nm, ident, attn, w, add):
    ps = [nm.ps(f"at{i}", [P, 512]) for i in range(2)]
    py = [nm.ps(f"ay{i}", [P, 512]) for i in range(2)]
    aT = nm.sb("attnT", [P, DH, QT * P])
    turned, kept, done, added = nm.sem("at_turned"), nm.sem("at_kept"), nm.sem("at_done"), nm.sem("at_added")
    with nc.Block() as block:
        @block.tensor
        def _(pe):
            for h in range(DH):
                for t in range(QT):
                    last = nc.tensor.transpose(ps[h][:, t * P:(t + 1) * P], attn[:, t, h * P:(h + 1) * P], ident[:, :])
                last.then_inc(turned, 1)
            pe.wait_ge(kept, DH)
            for t in range(QT):
                if t >= 2:
                    pe.wait_ge(added, t - 1)
                for h in range(DH):
                    last = nc.tensor.matmul(py[t % 2][:, 0:D], aT[:, h, t * P:(t + 1) * P], w[:, h, :],
                                            start=(h == 0), stop=(h == DH - 1))
                last.then_inc(done, 1)

        @block.scalar
        def _(act):
            for h in range(DH):
                act.wait_ge(turned, h + 1)
                nc.scalar.copy(aT[:, h, :], ps[h][:, :]).then_inc(kept, 1)

        @block.vector
        def _(dve):
            for t in range(QT):
                dve.wait_ge(done, t + 1)
                add(t, py[t % 2][:, 0:D]).then_inc(added, 1)


def self_attention(nc, d, x_sb, y_sb, ident, identb):
    with ExitStack() as es:
        hT = es.enter_context(nc.sbuf_tensor("l0_hT", [P, DH, B * S], F32))
        vecs = es.enter_context(nc.sbuf_tensor("l0_vecs", [P, 2, DH], F32))
        wqkv = es.enter_context(nc.sbuf_tensor("l0_wqkv", [P, DH, 3 * D], F32))
        wproj = es.enter_context(nc.sbuf_tensor("l0_wproj", [P, DH, D], F32))
        rope = es.enter_context(nc.sbuf_tensor("l0_rope", [P, 2, QT * NH, HD // 2], F32))
        tri_q = es.enter_context(nc.sbuf_tensor("l0_tri_q", [P, 512], BF16))
        tri_k = es.enter_context(nc.sbuf_tensor("l0_tri_k", [P, P], BF16))
        got = es.enter_context(nc.semaphore("l0_got"))
        with nc.Block() as block:
            @block.sync
            def _(sp):
                sp.dma_start(wqkv[:], d["L0_ffn_Wqkv"].rearrange("(h p) n -> p h n", p=P)).then_inc(got, 16)
                sp.dma_start(wproj[:], d["L0_ffn_Wproj"].rearrange("(h p) n -> p h n", p=P)).then_inc(got, 16)
                for i, n in enumerate(("L0_ffn_ln1_g", "L0_ffn_ln1_b")):
                    for h in range(DH):
                        sp.dma_start(vecs[:, i, h:h + 1],
                                     d[n][h * P:(h + 1) * P].rearrange("(p o) -> p o", o=1)).then_inc(got, 16)
                sp.dma_start(rope[:], d["c_rope"]).then_inc(got, 16)
                sp.dma_start(tri_q[:], d["c_tri_q"].bitcast(BF16)).then_inc(got, 16)
                sp.dma_start(tri_k[:], d["c_tri_k"].bitcast(BF16)).then_inc(got, 16)
                sp.wait_ge(got, 16 * 9)
        with ExitStack() as es1:
            layer_norm(nc, es1, x_sb, y_sb, "l0a")
            hn = es1.enter_context(nc.sbuf_tensor("l0_hn", [P, NT, D], F32))
            layer_norm(nc, es1, y_sb, hn, "l0b")
            transpose_tokens(nc, es1, hn, lambda g, h: hT[:, h, g * 512:(g + 1) * 512], ident, "l0T",
                             scale=vecs[:, 0, :], bias=vecs[:, 1, :])
        sb = Names(nc, es, "l0")
        hTb = sb.sb("hTb", [P, DH, S])
        qkv = sb.sb("qkv", [P, QT, 3 * D])
        qT = sb.sb("qT", [STK + MAXR, NH, S], BF16)
        kT = sb.sb("kT", [STK + MAXR, NH, S], BF16)
        vt = sb.sb("vt", [P, QT, NH, VW])
        attn = sb.sb("attn", [P, QT, D])
        with nc.Block() as block:
            @block.vector
            def _(dve):
                nc.vector.memset(kT[STK:STK + MAXR, :, :], 1.0)
                nc.vector.memset(vt[:, :, :, HD:HD + 1], 1.0)
                nc.vector.memset(vt[:, :, :, HD + 1:VW], 0.0)
        with nc.Fori(0, B) as b:
            with ExitStack() as e1:
                nm = Names(nc, e1, "l0p")
                jobs = [(qkv[:, t, c:c + 384], [hTb[:, h, t * P:(t + 1) * P] for h in range(DH)],
                         [wqkv[:, h, c:c + 384] for h in range(DH)], lambda ps: ps[:, 0:384])
                        for t in range(QT) for c in (0, 384)]
                project_tokens(nc, nm, jobs)([(hTb[:, :, :], hT[:, :, bass.ds(b * S, S)])])
                nm.clear()
            with ExitStack() as e1:
                nm = Names(nc, e1, "l0s")
                qr = nm.sb("qr", [P, QT * NH, 2, HD])
                tmp = nm.sb("ropetmp", [P, 4, QT * NH, 2, HD // 2])
                stk = [nm.sb(f"stk{i}", [P, QT * NH, STK], BF16) for i in range(2)]
                rest = nm.sb("rest", [P, QT * NH, HD])
                rotated, summed = nm.sem("rotated"), nm.sem("rsummed")
                src = qkv[:, :, :].rearrange("p t (h c e) -> p (t h) c e", h=NH, c=3)
                half = HD // 2
                with nc.Block() as block:
                    @block.vector
                    def _(dve):
                        for i, (part, table) in enumerate(((0, 1), (1, 0), (0, 0), (1, 1))):
                            for c in range(2):
                                a = src[:, :, c, part * half:(part + 1) * half]
                                j = nc.vector.tensor_tensor(tmp[:, i, :, c, :], a, rope[:, table, :, :], ALU.mult)
                        j.then_inc(rotated, 1)
                        dve.wait_ge(rotated, 1)
                        for c in range(2):
                            nc.vector.tensor_tensor(qr[:, :, c, 0:half], tmp[:, 0, :, c, :], tmp[:, 1, :, c, :],
                                                    ALU.subtract)
                            nc.vector.tensor_tensor(qr[:, :, c, half:HD], tmp[:, 2, :, c, :], tmp[:, 3, :, c, :],
                                                    ALU.add)

                    @block.scalar
                    def _(act):
                        nc.scalar.copy(vt[:, :, :, 0:HD].rearrange("p t h e -> p (t h) e"), src[:, :, 2, :])
                split_stacks(nc, nm, [(qr[:, :, 0, :], stk[0], Q_SLOTS, HD ** -0.5, rest[:, :, :]),
                                      (qr[:, :, 1, :], stk[1], K_SLOTS, 1.0, rest[:, :, :])])
                v = [s[:, :, :].rearrange("p (t h) e -> p t h e", t=QT) for s in stk]
                turn_stacks(nc, nm, identb, [(v[0], QT, qT), (v[1], QT, kT)])
                nm.clear()
            with ExitStack() as e1:
                nm = Names(nc, e1, "l0a")
                attend(nc, nm, ident, identb, qT, kT, vt, attn, S, True,
                       lambda qt, f: tri_q[:, 512 - (qt + 1) * P:512], lambda kt: tri_k[:, :])
                nm.clear()
            with ExitStack() as e1:
                nm = Names(nc, e1, "l0o")

                def add(t, prod):
                    y = y_sb[:, bass.ds(b * QT + t, 1), :].rearrange("p o d -> p (o d)")
                    return nc.vector.tensor_tensor(y, prod, y, ALU.add)
                project_out(nc, nm, ident, attn, wproj, add)
                nm.clear()


NEXP, FF = 8, 4 * D
CAP = -(-2 * B * S // NEXP)
FC = FF // P


def route(nc, es, d, y_sb, h2T, gatew):
    with ExitStack() as es1:
        nm = Names(nc, es1, "rt")
        wg = nm.sb("wg", [P, DH, NEXP])
        tri = nm.sb("tri", [P, P])
        ones = nm.sb("ones", [P, P])
        ident = nm.sb("ident", [P, P])
        rank = nm.sb("rank", [P, NT, NEXP])
        b2 = nm.sb("b2", [NEXP, D])
        g = nm.sb("g", [P, NT, NEXP])
        e = nm.sb("e", [P, NT, NEXP])
        eq = nm.sb("eq", [P, NT, NEXP])
        hot = [nm.sb(f"hot{i}", [P, NT, NEXP]) for i in range(2)]
        mask = nm.sb("mask", [P, NT, NEXP])
        before = nm.sb("before", [P, NT, NEXP])
        m = nm.sb("m", [P, NT])
        s = nm.sb("s", [P, NT])
        gwT = nm.sb("gwT", [NEXP, NT * P])
        ps = nm.ps("lg", [P, 512])
        pc = nm.ps("cum", [P, 512])
        pt = [nm.ps(f"gT{i}", [NEXP, 512]) for i in range(2)]
        pb = [nm.ps(f"gb{i}", [P, 512]) for i in range(2)]
        got, scored, lowered, exped = nm.sem("got"), nm.sem("scored"), nm.sem("lowered"), nm.sem("exped")
        step, masked, counted, weighted = nm.sem("step"), nm.sem("masked"), nm.sem("counted"), nm.sem("weighted")
        turned, kept, biased, added = nm.sem("turned"), nm.sem("kept"), nm.sem("biased"), nm.sem("added")

        def per_token(t):
            return ap_of(t[:, :], 0, [t[:, :].ap[0], [1, NT], [0, NEXP]])

        with nc.Block() as block:
            @block.sync
            def _(sp):
                sp.dma_start(wg[:], d["L0_ffn_Wgate"].rearrange("(h p) n -> p h n", p=P)).then_inc(got, 16)
                sp.dma_start(tri[:], d["c_tri"]).then_inc(got, 16)
                sp.dma_start(ones[:], d["c_ones"]).then_inc(got, 16)
                sp.dma_start(ident[:], d["c_ident"]).then_inc(got, 16)
                sp.dma_start(rank[:], d["c_rank"]).then_inc(got, 16)
                sp.dma_start(b2[:], d["L0_ffn_b2"]).then_inc(got, 16)

            @block.tensor
            def _(pe):
                pe.wait_ge(got, 96)
                for t in range(NT):
                    for h in range(DH):
                        last = nc.tensor.matmul(ps[:, t * NEXP:(t + 1) * NEXP], h2T[:, h, t * P:(t + 1) * P],
                                                wg[:, h, :], start=(h == 0), stop=(h == DH - 1))
                last.then_inc(scored, 1)
                pe.wait_ge(masked, 1)
                n = NT * NEXP
                nc.tensor.matmul(pc[:, 0:n], tri[:, :], mask[:, :, :].rearrange("p t e -> p (t e)"), start=True,
                                 stop=False)
                nc.tensor.matmul(pc[:, 0:n], ones[:, :], before[:, :, :].rearrange("p t e -> p (t e)"), start=False,
                                 stop=True).then_inc(counted, 1)
                pe.wait_ge(weighted, 1)
                for q in range(NT // 4):
                    if q >= 2:
                        pe.wait_ge(kept, q - 1)
                    for i in range(4):
                        last = nc.tensor.transpose(pt[q % 2][:, i * P:(i + 1) * P], gatew[:, 4 * q + i, :], ident[:, :])
                    last.then_inc(turned, 1)
                for t in range(NT):
                    pe.wait_ge(kept, t // 4 + 1)
                    if t >= 2:
                        pe.wait_ge(added, t - 1)
                    nc.tensor.matmul(pb[t % 2][:, 0:D], gwT[:, t * P:(t + 1) * P], b2[:, :], start=True,
                                     stop=True).then_inc(biased, 1)

            @block.scalar
            def _(act):
                act.wait_ge(lowered, 1)
                nc.scalar.activation(e[:, :, :], g[:, :, :], ACT.Exp).then_inc(exped, 1)

            @block.vector
            def _(dve):
                count = [0]

                def then(i):
                    count[0] += 1
                    i.then_inc(step, 1)
                    dve.wait_ge(step, count[0])

                tt, ts = nc.vector.tensor_tensor, nc.vector.tensor_scalar
                dve.wait_ge(scored, 1)
                lg = ps[:, 0:NT * NEXP].rearrange("p (t e) -> p t e", e=NEXP)
                then(nc.vector.tensor_reduce(m[:, :], lg, AX.X, ALU.max))
                tt(g[:, :, :], lg, per_token(m), ALU.subtract).then_inc(lowered, 1)
                dve.wait_ge(exped, 1)
                then(nc.vector.tensor_reduce(s[:, :], e[:, :, :], AX.X, ALU.add))
                then(nc.vector.reciprocal(s[:, :], s[:, :]))
                then(tt(g[:, :, :], e[:, :, :], per_token(s), ALU.mult))
                then(nc.vector.tensor_copy(e[:, :, :], g[:, :, :]))
                dve.wait_ge(got, 96)
                for i in range(2):
                    then(nc.vector.tensor_reduce(m[:, :], e[:, :, :], AX.X, ALU.max))
                    then(tt(eq[:, :, :], e[:, :, :], per_token(m), ALU.is_equal))
                    then(tt(eq[:, :, :], eq[:, :, :], rank[:, :, :], ALU.mult))
                    then(nc.vector.tensor_reduce(m[:, :], eq[:, :, :], AX.X, ALU.max))
                    then(tt(hot[i][:, :, :], eq[:, :, :], per_token(m), ALU.is_equal))
                    if i == 0:
                        then(nc.vector.scalar_tensor_tensor(e[:, :, :], hot[0][:, :, :], -2.0, e[:, :, :], ALU.mult,
                                                            ALU.add))
                then(tt(mask[:, :, :], hot[0][:, :, :], hot[1][:, :, :], ALU.add))
                then(nc.vector.memset(before[:, 0, :], 0.0))
                for t in range(1, NT):
                    i = tt(before[:, t, :], before[:, t - 1, :], mask[:, t - 1, :], ALU.add)
                    if t < NT - 1:
                        then(i)
                i.then_inc(masked, 1)
                dve.wait_ge(counted, 1)
                cum = pc[:, 0:NT * NEXP].rearrange("p (t e) -> p t e", e=NEXP)
                then(ts(eq[:, :, :], cum, float(CAP), None, ALU.is_le))
                then(tt(mask[:, :, :], mask[:, :, :], eq[:, :, :], ALU.mult))
                tt(gatew[:, :, :], g[:, :, :], mask[:, :, :], ALU.mult).then_inc(weighted, 1)
                for q in range(NT // 4):
                    dve.wait_ge(turned, q + 1)
                    nc.vector.tensor_copy(gwT[:, q * 512:(q + 1) * 512], pt[q % 2][:, :]).then_inc(kept, 1)
                for t in range(NT):
                    dve.wait_ge(biased, t + 1)
                    tt(y_sb[:, t, :], pb[t % 2][:, 0:D], y_sb[:, t, :], ALU.add).then_inc(added, 1)


def experts(nc, d, y_sb, h2T, gatew):
    with ExitStack() as es:
        nm = Names(nc, es, "ex")
        w1 = [nm.sb(f"w1_{i}", [P, DH, FF]) for i in range(2)]
        w2 = [nm.sb(f"w2_{i}", [P, FC, D]) for i in range(2)]
        b1 = [nm.sb(f"b1_{i}", [P, FC]) for i in range(2)]
        hm = [nm.sb(f"hm{i}", [P, FC, 512]) for i in range(2)]
        pu = [nm.ps(f"up{i}", [P, 512]) for i in range(4)]
        pd = [nm.ps(f"dn{i}", [P, 512]) for i in range(2)]
        got = [nm.sem("got0"), nm.sem("got1")]
        up, act_done, down, added = nm.sem("up"), nm.sem("act"), nm.sem("down"), nm.sem("added")
        units = [(i, tb) for i in range(2) for tb in range(B)]
        with nc.Fori(0, NEXP // 2) as pair:
            with nc.Block() as block:
                @block.sync
                def _(sp):
                    for i in range(2):
                        ex = pair * 2 + i
                        sp.dma_start(w1[i][:, :, :], d["L0_ffn_W1"][bass.ds(ex, 1)].rearrange(
                            "o (h p) n -> p (o h) n", p=P)).then_inc(got[i], 16)
                        sp.dma_start(b1[i][:, :], d["b1_epc"][bass.ds(ex, 1)].rearrange(
                            "o p c -> p (o c)")).then_inc(got[i], 16)
                        sp.dma_start(w2[i][:, :, :], d["L0_ffn_W2"][bass.ds(ex, 1)].rearrange(
                            "o (c p) n -> p (o c) n", p=P)).then_inc(got[i], 16)

                @block.tensor
                def _(pe):
                    def ups(n):
                        i, tb = units[n]
                        if tb == 0:
                            pe.wait_ge(got[i], 48)
                        for c in range(FC):
                            k = n * FC + c
                            if k >= 4:
                                pe.wait_ge(act_done, k - 3)
                            for h in range(DH):
                                last = nc.tensor.matmul(pu[k % 4][:, :], w1[i][:, h, c * P:(c + 1) * P],
                                                        h2T[:, h, tb * 512:(tb + 1) * 512], start=(h == 0),
                                                        stop=(h == DH - 1))
                            last.then_inc(up, 1)

                    def downs(n):
                        i, tb = units[n]
                        pe.wait_ge(act_done, (n + 1) * FC)
                        for q in range(4):
                            k = n * 4 + q
                            if k >= 2:
                                pe.wait_ge(added, k - 1)
                            for c in range(FC):
                                last = nc.tensor.matmul(pd[k % 2][:, 0:D], hm[n % 2][:, c, q * P:(q + 1) * P],
                                                        w2[i][:, c, :], start=(c == 0), stop=(c == FC - 1))
                            last.then_inc(down, 1)

                    ups(0)
                    for n in range(1, len(units)):
                        ups(n)
                        downs(n - 1)
                    downs(len(units) - 1)

                @block.scalar
                def _(act):
                    for n, (i, tb) in enumerate(units):
                        if tb == 0:
                            act.wait_ge(got[i], 48)
                        if n >= 2:
                            act.wait_ge(down, (n - 1) * 4)
                        for c in range(FC):
                            k = n * FC + c
                            act.wait_ge(up, k + 1)
                            nc.scalar.activation(hm[n % 2][:, c, :], pu[k % 4][:, :], ACT.Gelu,
                                                 bias=b1[i][:, c:c + 1]).then_inc(act_done, 1)

                @block.vector
                def _(dve):
                    for n, (i, tb) in enumerate(units):
                        for q in range(4):
                            k, t = n * 4 + q, tb * 4 + q
                            dve.wait_ge(down, k + 1)
                            if n >= 4:
                                dve.wait_ge(added, k - 15)
                            gs = gatew[:, t, bass.ds(pair * 2 + i, 1)]
                            nc.vector.scalar_tensor_tensor(y_sb[:, t, :], pd[k % 2][:, 0:D], gs, y_sb[:, t, :],
                                                           ALU.mult, ALU.add).then_inc(added, 1)
            nm.clear()


def gated_add(nc, d, name, layer, x_sb, y_sb):
    with ExitStack() as es:
        nm = Names(nc, es, f"ga_{name}{layer}")
        gate = nm.sb("gate", [P, 2])
        got, gated = nm.sem("got"), nm.sem("gated")
        with nc.Block() as block:
            @block.sync
            def _(sp):
                sp.dma_start(gate[:], ap_of(d[name], 0, [[0, P], [1, 2]])).then_inc(got, 16)

            @block.scalar
            def _(act):
                act.wait_ge(got, 16)
                nc.scalar.activation(gate[:], gate[:], ACT.Tanh).then_inc(gated, 1)

            @block.vector
            def _(dve):
                dve.wait_ge(gated, 1)
                nc.vector.scalar_tensor_tensor(x_sb[:, :, :], y_sb[:, :, :], gate[:, layer:layer + 1], x_sb[:, :, :],
                                               ALU.mult, ALU.add)


def moe(nc, d, x_sb, y_sb, ident):
    with ExitStack() as es:
        h2T = es.enter_context(nc.sbuf_tensor("moe_hT", [P, DH, B * S], F32))
        gatew = es.enter_context(nc.sbuf_tensor("moe_gate", [P, NT, NEXP], F32))
        with ExitStack() as es1:
            vecs = es1.enter_context(nc.sbuf_tensor("moe_vecs", [P, 2, DH], F32))
            got = es1.enter_context(nc.semaphore("moe_got"))
            with nc.Block() as block:
                @block.sync
                def _(sp):
                    for i, n in enumerate(("L0_ffn_ln2_g", "L0_ffn_ln2_b")):
                        for h in range(DH):
                            sp.dma_start(vecs[:, i, h:h + 1],
                                         d[n][h * P:(h + 1) * P].rearrange("(p o) -> p o", o=1)).then_inc(got, 16)
                    sp.wait_ge(got, 64)
            hn = es1.enter_context(nc.sbuf_tensor("moe_hn", [P, NT, D], F32))
            layer_norm(nc, es1, y_sb, hn, "lnm")
            transpose_tokens(nc, es1, hn, lambda g, h: h2T[:, h, g * 512:(g + 1) * 512], ident, "mT",
                             scale=vecs[:, 0, :], bias=vecs[:, 1, :])
        route(nc, es, d, y_sb, h2T, gatew)
        experts(nc, d, y_sb, h2T, gatew)
    gated_add(nc, d, "g_ffn", 0, x_sb, y_sb)


def cross_attention(nc, d, x_sb, ident, identb, ctxT):
    with ExitStack() as es:
        hT = es.enter_context(nc.sbuf_tensor("xa_hT", [P, DH, B * S], F32))
        w = {n: es.enter_context(nc.sbuf_tensor(f"xa_{n}", [P, DH, D], F32)) for n in ("wqT", "wkT", "wvT", "woT")}
        gate = es.enter_context(nc.sbuf_tensor("xa_gate", [P, 2], F32))
        got, gated = es.enter_context(nc.semaphore("xa_got")), es.enter_context(nc.semaphore("xa_gated"))
        with nc.Block() as block:
            @block.sync
            def _(sp):
                for n, t in w.items():
                    sp.dma_start(t[:], d[n].rearrange("(h p) n -> p h n", p=P)).then_inc(got, 16)
                sp.dma_start(gate[:], ap_of(d["g_xattn"], 0, [[0, P], [1, 2]])).then_inc(got, 16)
                sp.wait_ge(got, 80)

            @block.scalar
            def _(act):
                act.wait_ge(got, 80)
                nc.scalar.activation(gate[:], gate[:], ACT.Tanh)
        with ExitStack() as es1:
            xn = es1.enter_context(nc.sbuf_tensor("xa_xn", [P, NT, D], F32))
            layer_norm(nc, es1, x_sb, xn, "xa")
            transpose_tokens(nc, es1, xn, lambda g, h: hT[:, h, g * 512:(g + 1) * 512], ident, "xaT")
        sb = Names(nc, es, "xa")
        qT = sb.sb("qT", [STK + MAXR, NH, S], BF16)
        kT = sb.sb("kT", [STK + MAXR, NH, SK], BF16)
        vt = sb.sb("vt", [P, KT, NH, VW])
        bias_q = sb.sb("bias_q", [P, QT, SK], BF16)
        bias_k = sb.sb("bias_k", [P, KT, S], BF16)
        attn = sb.sb("attn", [P, QT, D])
        with nc.Block() as block:
            @block.vector
            def _(dve):
                nc.vector.memset(kT[STK:STK + MAXR, :, :], 1.0)
                nc.vector.memset(vt[:, :, :, HD:HD + 1], 1.0)
                nc.vector.memset(vt[:, :, :, HD + 1:VW], 0.0)
        with nc.Fori(0, B) as b:
            with ExitStack() as e0:
                mask = e0.enter_context(nc.sbuf_tensor("xa_mask", [P, QT, SK], I32))
                nm = Names(nc, e0, "xam")
                pm = [nm.ps(f"mt{i}", [P, 1024], BF16) for i in range(2)]
                mgot, biased, turned, kept = nm.sem("got"), nm.sem("biased"), nm.sem("turned"), nm.sem("kept")
                with nc.Block() as block:
                    @block.sync
                    def _(sp):
                        sp.dma_start(mask[:, :, :], d["mask_BxSxS2_ik0"][bass.ds(b, 1)].rearrange(
                            "o (t p) k -> p (o t) k", p=P)).then_inc(mgot, 16)

                    @block.vector
                    def _(dve):
                        dve.wait_ge(mgot, 16)
                        for t in range(QT):
                            nc.vector.tensor_scalar(bias_q[:, t, :], mask[:, t, :], 0.0, NEG, ALU.is_equal,
                                                    ALU.mult).then_inc(biased, 1)

                    @block.tensor
                    def _(pe):
                        pe.wait_ge(biased, QT)
                        for n in range(KT // 2):
                            if n >= 2:
                                pe.wait_ge(kept, n - 1)
                            for i in range(2):
                                for t in range(QT):
                                    kt = 2 * n + i
                                    last = nc.tensor.transpose(pm[n % 2][:, (i * QT + t) * P:(i * QT + t + 1) * P],
                                                               bias_q[:, t, kt * P:(kt + 1) * P], identb[:, :])
                            last.then_inc(turned, 1)

                    @block.scalar
                    def _(act):
                        for n in range(KT // 2):
                            act.wait_ge(turned, n + 1)
                            nc.scalar.copy(bias_k[:, 2 * n:2 * n + 2, :],
                                           pm[n % 2][:, :].rearrange("p (i s) -> p i s", i=2)).then_inc(kept, 1)
                nm.clear()
            with ExitStack() as e0:
                q = e0.enter_context(nc.sbuf_tensor("xa_q", [P, QT, D], F32))
                k = e0.enter_context(nc.sbuf_tensor("xa_k", [P, KT, D], F32))
                with ExitStack() as e1:
                    nm = Names(nc, e1, "xap")
                    hTb = nm.sb("hTb", [P, DH, S])
                    cTb = nm.sb("cTb", [P, DH, SK])

                    def lhs(t, src):
                        return [src[:, h, t * P:(t + 1) * P] for h in range(DH)]

                    def whole(ps):
                        return ps[:, 0:D]
                    jobs = [(q[:, t, :], lhs(t, hTb), [w["wqT"][:, h, :] for h in range(DH)], whole) for t in range(QT)]
                    for t in range(KT):
                        jobs.append((k[:, t, :], lhs(t, cTb), [w["wkT"][:, h, :] for h in range(DH)], whole))
                        jobs.append((vt[:, t, :, 0:HD], lhs(t, cTb), [w["wvT"][:, h, :] for h in range(DH)],
                                     lambda ps: ps[:, 0:D].rearrange("p (h e) -> p h e", h=NH)))
                    cv = ctxT[:, :, :, :].rearrange("p b h s -> p (b h) s")
                    project_tokens(nc, nm, jobs)([(hTb[:, :, :], hT[:, :, bass.ds(b * S, S)]),
                                                  (cTb[:, :, :], cv[:, bass.ds(b * DH, DH), 0:SK])])
                    nm.clear()
                with ExitStack() as e1:
                    nm = Names(nc, e1, "xas")
                    stk = [nm.sb(f"stk{i}", [P, QT * NH, STK], BF16) for i in range(2)]
                    rest = nm.sb("rest", [P, QT * NH, HD])
                    v = [s[:, :, :].rearrange("p (t h) e -> p t h e", t=QT) for s in stk]

                    def heads(x, t0):
                        return x[:, t0:t0 + QT, :].rearrange("p t (h e) -> p (t h) e", h=NH)
                    split_stacks(nc, nm, [(heads(q, 0), stk[0], Q_SLOTS, float(HD) ** 0.5, rest[:, :, :]),
                                          (heads(k, 0), stk[1], K_SLOTS, 1.0, rest[:, :, :])])
                    turn_stacks(nc, nm, identb, [(v[0], QT, qT), (v[1], QT, kT[:, :, 0:S])])
                    nm.clear()
                with ExitStack() as e1:
                    nm = Names(nc, e1, "xau")
                    stk = nm.sb("stk", [P, QT * NH, STK], BF16)
                    rest = nm.sb("rest", [P, QT * NH, HD])
                    split_stacks(nc, nm, [(heads(k, QT), stk, K_SLOTS, 1.0, rest[:, :, :])])
                    turn_stacks(nc, nm, identb, [(stk[:, :, :].rearrange("p (t h) e -> p t h e", t=QT), QT,
                                                  kT[:, :, S:SK])])
                    nm.clear()
            with ExitStack() as e1:
                nm = Names(nc, e1, "xaa")
                attend(nc, nm, ident, identb, qT, kT, vt, attn, SK, False,
                       lambda qt, f: bias_q[:, qt, f * 512:(f + 1) * 512], lambda kt: bias_k[:, kt, :])
                nm.clear()
            with ExitStack() as e1:
                nm = Names(nc, e1, "xao")

                def add(t, prod):
                    x = x_sb[:, bass.ds(b * QT + t, 1), :].rearrange("p o d -> p (o d)")
                    return nc.vector.scalar_tensor_tensor(x, prod, gate[:, 1:2], x, ALU.mult, ALU.add)
                project_out(nc, nm, ident, attn, w["woT"], add)
                nm.clear()


FI = 704
QB = 16
FPAD = -(-FI // P)
STEPS_HALF, STEPS_ONE, STEP_TWO = (0.25, 0.75, 1.25, 1.75), (2.5, 3.5), 5.0


def quantize(nc, nm, jobs, width):
    n_blk = width // QB
    amax = nm.sb("amax", [P, 2, n_blk])
    inv = nm.sb("inv", [P, 2, n_blk])
    v = nm.sb("v", [P, 2, width])
    sgn = nm.sb("sgn", [P, 2, width])
    hi = nm.sb("hi", [P, 2, width])
    lo = nm.sb("lo", [P, 2, width])
    maxed, scaled, inverted, divided = nm.sem("maxed"), nm.sem("scaled"), nm.sem("inverted"), nm.sem("divided")
    signed, absed, step, graded, done = nm.sem("signed"), nm.sem("absed"), nm.sem("step"), nm.sem("graded"), nm.sem("done")
    sscaled = nm.sem("sscaled")

    def blocks(ap):
        return ap.rearrange("p (n e) -> p n e", e=QB)

    def wide(t, r, i):
        a = t[0:r, i, :]
        return ap_of(a, 0, [a.ap[0], [1, n_blk], [0, QB]])

    with nc.Block() as block:
        @block.vector
        def _(dve):
            count = [0]

            def then(i):
                count[0] += 1
                i.then_inc(step, 1)
                dve.wait_ge(step, count[0])

            def scale(n):
                src, dst = jobs[n]
                r, i = src.shape[0], n % 2
                if n >= 2:
                    dve.wait_ge(done, n - 1)
                then(nc.vector.tensor_reduce(amax[0:r, i, :], blocks(src), AX.X, ALU.max,
                                             apply_absolute_value=True))
                nc.vector.tensor_scalar(amax[0:r, i, :], amax[0:r, i, :], 1.0 / 6.0, 1e-12, ALU.mult,
                                        ALU.max).then_inc(scaled, 1)
                dve.wait_ge(scaled, n + 1)
                nc.vector.reciprocal(inv[0:r, i, :], amax[0:r, i, :]).then_inc(inverted, 1)

            def grade(n):
                src, dst = jobs[n]
                r, i = src.shape[0], n % 2
                a, h, l = v[0:r, i, :], hi[0:r, i, :], lo[0:r, i, :]
                dve.wait_ge(absed, n + 1)
                stt, ts = nc.vector.scalar_tensor_tensor, nc.vector.tensor_scalar
                ts(h, a, STEP_TWO, 2.0, ALU.is_gt, ALU.mult)
                then(ts(l, a, STEPS_HALF[0], None, ALU.is_gt))
                stt(h, a, STEPS_ONE[0], h, ALU.is_gt, ALU.add)
                then(stt(l, a, STEPS_HALF[1], l, ALU.is_gt, ALU.add))
                stt(h, a, STEPS_ONE[1], h, ALU.is_gt, ALU.add)
                then(stt(l, a, STEPS_HALF[2], l, ALU.is_gt, ALU.add))
                then(stt(l, a, STEPS_HALF[3], l, ALU.is_gt, ALU.add))
                stt(h, l, 0.5, h, ALU.mult, ALU.add).then_inc(graded, 1)

            scale(0)
            for n in range(len(jobs)):
                if n + 1 < len(jobs):
                    scale(n + 1)
                grade(n)

        @block.scalar
        def _(act):
            for n, (src, dst) in enumerate(jobs):
                r, i = src.shape[0], n % 2
                if n >= 2:
                    act.wait_ge(done, n - 1)
                nc.scalar.activation(sgn[0:r, i, :], src, ACT.Sign).then_inc(signed, 1)
                act.wait_ge(divided, n + 1)
                nc.scalar.activation(v[0:r, i, :], v[0:r, i, :], ACT.Abs).then_inc(absed, 1)

        @block.gpsimd
        def _(pool):
            def divide(n):
                src, dst = jobs[n]
                r, i = src.shape[0], n % 2
                pool.wait_ge(inverted, n + 1)
                nc.gpsimd.tensor_tensor(blocks(v[0:r, i, :]), blocks(src), wide(inv, r, i), ALU.mult).then_inc(divided, 1)
                pool.wait_ge(signed, n + 1)
                nc.gpsimd.tensor_tensor(blocks(sgn[0:r, i, :]), blocks(sgn[0:r, i, :]), wide(amax, r, i),
                                        ALU.mult).then_inc(sscaled, 1)

            divide(0)
            for n, (src, dst) in enumerate(jobs):
                r, i = src.shape[0], n % 2
                if n + 1 < len(jobs):
                    divide(n + 1)
                pool.wait_ge(graded, n + 1)
                pool.wait_ge(sscaled, n + 1)
                nc.gpsimd.tensor_tensor(dst, hi[0:r, i, :], sgn[0:r, i, :], ALU.mult).then_inc(done, 1)


def turn_rows(nc, nm, ident, jobs):
    ps = [nm.ps(f"tr{i}", [P, 512]) for i in range(4)]
    turned, kept = nm.sem("tr_turned"), [nm.sem("tr_kept0"), nm.sem("tr_kept1")]
    with nc.Block() as block:
        @block.tensor
        def _(pe):
            for n, (src, dst) in enumerate(jobs):
                r, c = src.shape
                if n >= 4:
                    pe.wait_ge(kept[n % 2], (n - 4) // 2 + 1)
                nc.tensor.transpose(ps[n % 4][0:c, 0:r], src, ident[0:r, 0:r]).then_inc(turned, 1)

        def copies(eng, parity, copy):
            for n, (src, dst) in enumerate(jobs):
                r, c = src.shape
                if n % 2 == parity:
                    eng.wait_ge(turned, n + 1)
                    copy(dst, ps[n % 4][0:c, 0:r]).then_inc(kept[parity], 1)

        @block.vector
        def _(dve):
            copies(dve, 0, nc.vector.tensor_copy)

        @block.scalar
        def _(act):
            copies(act, 1, nc.scalar.copy)


def fp4_ffn(nc, d, x_sb, ident):
    with ExitStack() as es:
        wgu = es.enter_context(nc.sbuf_tensor("ff_wguT", [P, DH, 2, FI], F32))
        wd = es.enter_context(nc.sbuf_tensor("ff_wdT", [P, FPAD, D], F32))
        xqT = es.enter_context(nc.sbuf_tensor("ff_xqT", [P, DH, B * S], F32))
        gate = es.enter_context(nc.sbuf_tensor("ff_gate", [P, 2], F32))
        with ExitStack() as e1:
            nm = Names(nc, e1, "ffw")
            wr = nm.sb("rows", [P, 2, FPAD, D])
            wq = nm.sb("rowsq", [P, 2, FPAD, D])
            dr = nm.sb("down", [P, DH, FI])
            dq = nm.sb("downq", [P, DH, FI])
            got = nm.sem("got")
            last_rows = FI - (FPAD - 1) * P
            with nc.Block() as block:
                @block.sync
                def _(sp):
                    for i, n in enumerate(("L1_ffn_w_gate", "L1_ffn_w_up")):
                        full = (FPAD - 1) * P
                        sp.dma_start(wr[:, i, 0:FPAD - 1, :],
                                     d[n][0:full, :].rearrange("(c p) k -> p c k", p=P)).then_inc(got, 16)
                        sp.dma_start(wr[0:last_rows, i, FPAD - 1, :], d[n][full:FI, :]).then_inc(got, 16)
                    sp.dma_start(dr[:], d["L1_ffn_w_down"].rearrange("(h p) k -> p h k", p=P)).then_inc(got, 16)
                    sp.dma_start(gate[:], ap_of(d["g_ffn"], 0, [[0, P], [1, 2]])).then_inc(got, 16)
                    sp.wait_ge(got, 96)

                @block.scalar
                def _(act):
                    act.wait_ge(got, 96)
                    nc.scalar.activation(gate[:], gate[:], ACT.Tanh)
            with ExitStack() as e2:
                nq = Names(nc, e2, "ffq1")
                jobs = []
                for i in range(2):
                    for c in range(FPAD):
                        r = P if c < FPAD - 1 else last_rows
                        jobs.append((wr[0:r, i, c, :], wq[0:r, i, c, :]))
                quantize(nc, nq, jobs, D)
            with ExitStack() as e2:
                nq = Names(nc, e2, "ffq2")
                quantize(nc, nq, [(dr[:, h, :], dq[:, h, :]) for h in range(DH)], FI)
            jobs = []
            for i in range(2):
                for c in range(FPAD):
                    r = P if c < FPAD - 1 else last_rows
                    for h in range(DH):
                        jobs.append((wq[0:r, i, c, h * P:(h + 1) * P], wgu[:, h, i, c * P:c * P + r]))
            for c in range(FPAD):
                r = P if c < FPAD - 1 else last_rows
                for h in range(DH):
                    jobs.append((dq[:, h, c * P:c * P + r], wd[0:r, c, h * P:(h + 1) * P]))
            turn_rows(nc, nm, ident, jobs)
        with ExitStack() as e1:
            xn = e1.enter_context(nc.sbuf_tensor("ff_xn", [P, NT, D], F32))
            layer_norm(nc, e1, x_sb, xn, "ff")
            nm = Names(nc, e1, "ffx")
            quantize(nc, nm, [(xn[:, 4 * g:4 * g + 4, :].rearrange("p t d -> p (t d)"),
                               xn[:, 4 * g:4 * g + 4, :].rearrange("p t d -> p (t d)")) for g in range(NT // 4)], 4 * D)
            transpose_tokens(nc, e1, xn, lambda g, h: xqT[:, h, g * 512:(g + 1) * 512], ident, "ffT")
        with nc.Fori(0, B) as b, ExitStack() as e0:
            hid = e0.enter_context(nc.sbuf_tensor("ff_hid", [P, QT, FI], F32))
            hq = e0.enter_context(nc.sbuf_tensor("ff_hq", [P, QT, FI], F32))
            with ExitStack() as e1:
                nm = Names(nc, e1, "ffg")
                xb = nm.sb("xb", [P, DH, S])
                sg = nm.sb("sg", [P, 2, FI])
                HALF = FI // 2
                pg = [nm.ps(f"g{i}", [P, 512]) for i in range(4)]
                pu = [nm.ps(f"u{i}", [P, 512]) for i in range(4)]
                static, prod, silued, mixed = nm.sem("static"), nm.sem("prod"), nm.sem("silued"), nm.sem("mixed")
                units = [(t, f) for t in range(QT) for f in range(2)]
                with nc.Block() as block:
                    @block.tensor
                    def _(pe):
                        pe.wait_ge(static, 1)
                        for n, (t, f) in enumerate(units):
                            if n >= 4:
                                pe.wait_ge(mixed, n - 3)
                            for i, ps in enumerate((pg, pu)):
                                for h in range(DH):
                                    last = nc.tensor.matmul(ps[n % 4][:, 0:HALF], xb[:, h, t * P:(t + 1) * P],
                                                            wgu[:, h, i, f * HALF:(f + 1) * HALF], start=(h == 0),
                                                            stop=(h == DH - 1))
                            last.then_inc(prod, 1)

                    @block.scalar
                    def _(act):
                        nc.scalar.copy(xb[:, :, :], xqT[:, :, bass.ds(b * S, S)]).then_inc(static, 1)
                        for n, (t, f) in enumerate(units):
                            act.wait_ge(prod, n + 1)
                            if n >= 4:
                                act.wait_ge(mixed, n - 3)
                            nc.scalar.activation(sg[:, (n // 2) % 2, f * HALF:(f + 1) * HALF], pg[n % 4][:, 0:HALF],
                                                 ACT.Silu).then_inc(silued, 1)

                    @block.vector
                    def _(dve):
                        for n, (t, f) in enumerate(units):
                            dve.wait_ge(silued, n + 1)
                            nc.vector.tensor_tensor(hid[:, t, f * HALF:(f + 1) * HALF], pu[n % 4][:, 0:HALF],
                                                    sg[:, (n // 2) % 2, f * HALF:(f + 1) * HALF],
                                                    ALU.mult).then_inc(mixed, 1)
                nm.clear()
            with ExitStack() as e1:
                nm = Names(nc, e1, "ffh")
                quantize(nc, nm, [(hid[:, t, :], hq[:, t, :]) for t in range(QT)], FI)
                nm.clear()
            with ExitStack() as e1:
                nm = Names(nc, e1, "ffd")
                hqT = nm.sb("hqT", [P, 2, FPAD, P])
                pt = [nm.ps(f"t{i}", [P, 1024]) for i in range(2)]
                py = [nm.ps(f"y{i}", [P, 512]) for i in range(2)]
                turned, kept, down, added = nm.sem("turned"), nm.sem("kept"), nm.sem("down"), nm.sem("added")
                last_rows = FI - (FPAD - 1) * P
                with nc.Block() as block:
                    @block.tensor
                    def _(pe):
                        def turn(t):
                            if t >= 2:
                                pe.wait_ge(kept, 2 * (t - 1))
                            for c in range(FPAD):
                                r = P if c < FPAD - 1 else last_rows
                                last = nc.tensor.transpose(pt[t % 2][0:r, c * P:(c + 1) * P], hq[:, t, c * P:c * P + r],
                                                           ident[:, :])
                            last.then_inc(turned, 1)

                        def product(t):
                            pe.wait_ge(kept, 2 * (t + 1))
                            if t >= 2:
                                pe.wait_ge(added, t - 1)
                            for c in range(FPAD):
                                r = P if c < FPAD - 1 else last_rows
                                last = nc.tensor.matmul(py[t % 2][:, 0:D], hqT[0:r, t % 2, c, :], wd[0:r, c, :],
                                                        start=(c == 0), stop=(c == FPAD - 1))
                            last.then_inc(down, 1)

                        turn(0)
                        for t in range(1, QT):
                            turn(t)
                            product(t - 1)
                        product(QT - 1)

                    @block.scalar
                    def _(act):
                        for t in range(QT):
                            act.wait_ge(turned, t + 1)
                            if t >= 2:
                                act.wait_ge(down, t - 1)
                            n = FPAD - 1
                            nc.scalar.copy(hqT[:, t % 2, 0:n, :],
                                           pt[t % 2][:, 0:n * P].rearrange("p (c s) -> p c s", s=P)).then_inc(kept, 1)
                            nc.scalar.copy(hqT[0:last_rows, t % 2, n, :],
                                           pt[t % 2][0:last_rows, n * P:(n + 1) * P]).then_inc(kept, 1)

                    @block.vector
                    def _(dve):
                        for t in range(QT):
                            dve.wait_ge(down, t + 1)
                            x = x_sb[:, bass.ds(b * QT + t, 1), :].rearrange("p o d -> p (o d)")
                            nc.vector.scalar_tensor_tensor(x, py[t % 2][:, 0:D], gate[:, 1:2], x, ALU.mult,
                                                           ALU.add).then_inc(added, 1)
                nm.clear()


def layouts(a):
    return {
        "b1_epc": np.ascontiguousarray(np.asarray(a["L0_ffn_b1"]).reshape(NEXP, FC, P).transpose(0, 2, 1)),
        "wqT": np.ascontiguousarray(np.asarray(a["L1_xattn_Wq"]).T),
        "wkT": np.ascontiguousarray(np.asarray(a["L1_xattn_Wk"]).T),
        "wvT": np.ascontiguousarray(np.asarray(a["L1_xattn_Wv"]).T),
        "woT": np.ascontiguousarray(np.asarray(a["L1_xattn_Wo"]).T),
    }


def bf16_bits(a):
    return np.ascontiguousarray((np.ascontiguousarray(a, np.float32).view(np.uint32) >> 16).astype(np.uint16))


def constants():
    c = {}
    c["c_ident"] = np.eye(P, dtype=np.float32)
    ones2 = np.zeros((P, 2, 2), np.float32)
    ones2[:, 0, 0] = 1
    ones2[:, 1, 1] = 1
    c["c_ones2"] = ones2
    c["c_add2"] = np.array([[0, 1], [1, 0]], np.float32)
    corner = np.full((P, PITCH), FAR, np.float32)
    corner[::NBLK, 0] = 0
    c["c_corner"] = corner
    inner = np.tile(np.array([[1, 0]], np.float32), (P, 1))
    inner[NBLK - 1::NBLK] = (0, -1)
    c["c_inner"] = inner
    seed = np.zeros((P, PITCH), np.float32)
    seed[NBLK - 1::NBLK, 0] = 1
    c["c_seed"] = bf16_bits(seed)
    c["c_identb"] = bf16_bits(np.eye(P, dtype=np.float32))
    inv = 1.0 / 10000.0 ** (np.arange(0, HD, 2, dtype=np.float32) / np.float32(HD))
    ang = np.arange(S, dtype=np.float32)[:, None] * inv.astype(np.float32)
    tab = np.stack([np.sin(ang), np.cos(ang)]).astype(np.float32)
    tab = tab.reshape(2, QT, P, 1, HD // 2).transpose(2, 0, 1, 3, 4)
    c["c_rope"] = np.ascontiguousarray(np.broadcast_to(tab, (P, 2, QT, NH, HD // 2)).reshape(P, 2, QT * NH, HD // 2))
    tri = np.where(np.arange(P)[None, :] <= np.arange(P)[:, None], 0, NEG).astype(np.float32)
    c["c_tri_q"] = bf16_bits(np.concatenate([np.zeros((P, 512 - P), np.float32), tri], 1))
    c["c_tri_k"] = bf16_bits(tri.T)
    c["c_tri"] = np.ascontiguousarray(np.tri(P, dtype=np.float32).T)
    c["c_ones"] = np.ones((P, P), np.float32)
    c["c_rank"] = np.ascontiguousarray(np.broadcast_to(np.arange(NEXP, 0, -1, dtype=np.float32), (P, NT, NEXP)))
    return c


def load_all(nc, d, x_sb, ident, identb, ctxT, x_src):
    with ExitStack() as es:
        ctx_nat = es.enter_context(nc.sbuf_tensor("ctx_nat", [P, B * KT, D], F32))
        came = es.enter_context(nc.semaphore("inputs_came"))
        with nc.Block() as block:
            @block.sync
            def _(sp):
                sp.dma_start(x_sb[:], x_src.rearrange("b (t p) d -> p (b t) d", p=P)).then_inc(came, 16)
                sp.dma_start(ident[:], d["c_ident"]).then_inc(came, 16)
                sp.dma_start(identb[:], d["c_identb"].bitcast(BF16)).then_inc(came, 16)
                sp.wait_ge(came, 64)

            @block.scalar
            def _(act):
                act.dma_start(ctx_nat[:], d["ctx_1024"].rearrange("b (t p) d -> p (b t) d", p=P)).then_inc(came, 16)

            @block.gpsimd
            def _(pool):
                nc.gpsimd.memset(ctxT[:, :, :, SK:PADI], 0.0)
        transpose_tokens(nc, es, ctx_nat, lambda g, h: ctxT[:, g // 2, h, (g % 2) * 512:(g % 2) * 512 + 512],
                         ident, "cT")


def build(nc, d, out, phases=("dtw", "l0", "xa", "ffn")):
    with ExitStack() as es:
        x_sb = es.enter_context(nc.sbuf_tensor("x_sb", [P, NT, D], F32))
        ident = es.enter_context(nc.sbuf_tensor("ident", [P, P], F32))
        identb = es.enter_context(nc.sbuf_tensor("identb", [P, P], BF16))
        ctxT = es.enter_context(nc.sbuf_tensor("ctxT", [P, B, DH, PADI], F32))
        load_all(nc, d, x_sb, ident, identb, ctxT, d["x"])
        clear_released(nc)
        if "dtw" in phases:
            dtw_block(nc, d, x_sb, ident, ctxT)
            clear_released(nc)
        if "l0" in phases:
            with ExitStack() as es1:
                y_sb = es1.enter_context(nc.sbuf_tensor("y_sb", [P, NT, D], F32))
                self_attention(nc, d, x_sb, y_sb, ident, identb)
                clear_released(nc)
                moe(nc, d, x_sb, y_sb, ident)
                clear_released(nc)
        if "xa" in phases:
            cross_attention(nc, d, x_sb, ident, identb, ctxT)
            clear_released(nc)
        if "ffn" in phases:
            fp4_ffn(nc, d, x_sb, ident)
            clear_released(nc)
        stored = es.enter_context(nc.semaphore("out_stored"))
        with nc.Block() as block:
            @block.sync
            def _(sp):
                sp.dma_start(out.rearrange("b (t p) d -> p (b t) d", p=P), x_sb[:]).then_inc(stored, 16)
                sp.wait_ge(stored, 16)


_INS = ("x", "ctx_1024", "mask_BxSxS2_ik0", "g_xattn", "g_ffn", "L0_ffn_ln1_g", "L0_ffn_ln1_b", "L0_ffn_Wqkv",
        "L0_ffn_Wproj", "L0_ffn_ln2_g", "L0_ffn_ln2_b", "L0_ffn_Wgate", "L0_ffn_W1", "L0_ffn_W2", "L0_ffn_b2",
        "L1_ffn_w_gate", "L1_ffn_w_up", "L1_ffn_w_down")


def kernel(**inputs):
    import concourse.bacc as bacc
    from concourse.bass_utils import run_bass_kernel_spmd

    nc = bacc.Bacc("TRN2", target_bir_lowering=False, num_devices=1)
    arrays = {n: np.ascontiguousarray(inputs[n]) for n in _INS}
    arrays.update(layouts(inputs))
    arrays.update(constants())
    d = {n: nc.dram_tensor(n, a.shape, mybir.dt.from_np(a.dtype), kind="ExternalInput").ap()
         for n, a in arrays.items()}
    out = nc.dram_tensor("out", (B, S, D), F32, kind="ExternalOutput").ap()
    build(nc, d, out)
    r = run_bass_kernel_spmd(nc, [arrays], core_ids=[0])
    return r.results[0]["out"]
```

```python
import numpy as np
import concourse.bass as bass
from concourse import mybir
from contextlib import ExitStack

F32, BF16, I32, U32, I8 = mybir.dt.float32, mybir.dt.bfloat16, mybir.dt.int32, mybir.dt.uint32, mybir.dt.int8
ALU, ACT, AX = mybir.AluOpType, mybir.ActivationFunctionType, mybir.AxisListType
P = 128
B, S, D, SK = 4, 512, 256, 1024
QT = S // P
KT = SK // P
NT = B * QT
DH = D // P
NBLK, RB = 32, 33
PADI = NBLK * RB
PITCH = RB + 1
SLOTS = S + NBLK
CH = 16
NCH = SLOTS // CH
ROW = SLOTS * PITCH
FAR = 1e30
FAR2 = 1e34
EPS = 1e-5


def ap_of(t, offset, dims):
    return bass.AP(tensor=t.tensor, offset=t.offset + offset, ap=dims)


def clear_released(nc):
    nums = sorted(set(nc.released_uncleared_semaphores))
    while nums:
        n = 1
        while n < len(nums) and nums[n] == nums[0] + n:
            n += 1
        nc.gpsimd.sem_clear(range(nums[0], nums[0] + n))
        nums = nums[n:]
    nc.all_engine_barrier()


def layer_norm(nc, es, x_sb, out_sb, name):
    stats = es.enter_context(nc.sbuf_tensor(f"{name}_stats", [P, NT, 6], F32))
    mv = es.enter_context(nc.sbuf_tensor(f"{name}_mv", [P, NT, 2], F32))
    std = es.enter_context(nc.sbuf_tensor(f"{name}_std", [P, NT], F32))
    rstd = es.enter_context(nc.sbuf_tensor(f"{name}_rstd", [P, NT], F32))
    stats_done = es.enter_context(nc.semaphore(f"{name}_stats_done"))
    var_done = es.enter_context(nc.semaphore(f"{name}_var_done"))
    std_done = es.enter_context(nc.semaphore(f"{name}_std_done"))
    rstd_done = es.enter_context(nc.semaphore(f"{name}_rstd_done"))
    with nc.Block() as block:
        @block.vector
        def _(dve):
            for t in range(NT):
                nc.vector.bn_stats(stats[:, t, :], x_sb[:, t, :]).then_inc(stats_done, 1)
            for t in range(NT):
                dve.wait_ge(stats_done, t + 1)
                nc.vector.bn_aggr(mv[:, t, :], stats[:, t, :]).then_inc(var_done, 1)
            dve.wait_ge(var_done, NT)
            nc.vector.tensor_scalar(std[:, :], mv[:, :, 1], EPS, None, ALU.add).then_inc(var_done, 1)
            dve.wait_ge(std_done, 1)
            nc.vector.reciprocal(rstd[:, :], std[:, :]).then_inc(rstd_done, 1)
            dve.wait_ge(rstd_done, 1)
            for t in range(NT):
                nc.vector.tensor_scalar(out_sb[:, t, :], x_sb[:, t, :], mv[:, t, 0:1], rstd[:, t:t + 1],
                                        ALU.subtract, ALU.mult)

        @block.scalar
        def _(act):
            act.wait_ge(var_done, NT + 1)
            nc.scalar.activation(std[:, :], std[:, :], ACT.Sqrt).then_inc(std_done, 1)


def transpose_tokens(nc, es, src, dst, ident, name, scale=None, bias=None, mul=1.0):
    ps = [es.enter_context(nc.psum_tensor(f"{name}_ps{i}", [P, 512], F32)) for i in range(2)]
    turned = es.enter_context(nc.semaphore(f"{name}_turned"))
    copied = es.enter_context(nc.semaphore(f"{name}_copied"))
    groups = src.shape[1] // 4
    with nc.Block() as block:
        @block.tensor
        def _(pe):
            for n in range(groups * DH):
                g, h = n // DH, n % DH
                if n >= 2:
                    pe.wait_ge(copied, n - 1)
                for q in range(4):
                    last = nc.tensor.transpose(ps[n % 2][:, q * P:(q + 1) * P],
                                               src[:, 4 * g + q, h * P:(h + 1) * P], ident[:, :])
                last.then_inc(turned, 1)

        @block.vector
        def _(dve):
            for n in range(groups * DH):
                g, h = n // DH, n % DH
                dve.wait_ge(turned, n + 1)
                out = dst(g, h)
                if scale is not None:
                    i = nc.vector.tensor_scalar(out, ps[n % 2][:, :], scale[:, h:h + 1], bias[:, h:h + 1],
                                                ALU.mult, ALU.add)
                else:
                    i = nc.vector.tensor_scalar(out, ps[n % 2][:, :], float(mul), None, ALU.mult)
                i.then_inc(copied, 1)


def tanh_gate(nc, es, g, name):
    gate = es.enter_context(nc.sbuf_tensor(f"{name}_gate", [P, 2], F32))
    got = es.enter_context(nc.semaphore(f"{name}_gate_got"))
    with nc.Block() as block:
        @block.sync
        def _(sp):
            sp.dma_start(gate[:], ap_of(g, 0, [[0, P], [1, 2]])).then_inc(got, 16)

        @block.scalar
        def _(act):
            act.wait_ge(got, 16)
            nc.scalar.activation(gate[:], gate[:], ACT.Tanh)
    return gate


def dtw_block(nc, d, x_sb, ident, ctxT, rows_came):
    dist = nc.dram_tensor("dist", [P, ROW], F32).ap()
    path = nc.dram_tensor("path", [P, SLOTS * RB], BF16).ap()
    with ExitStack() as es:
        xnT = es.enter_context(nc.sbuf_tensor("xnT", [P, DH, B * S], F32))
        with ExitStack() as es1:
            xn = es1.enter_context(nc.sbuf_tensor("dtw_xn", [P, NT, D], F32))
            layer_norm(nc, es1, x_sb, xn, "ln0")
            transpose_tokens(nc, es1, xn, lambda g, h: xnT[:, h, g * 512:(g + 1) * 512], ident, "xT", mul=-2.0)
        dtw_distances(nc, d, xnT, ctxT, dist)
    with ExitStack() as es:
        part = [es.enter_context(nc.sbuf_tensor(f"ctx_part{i}", [P, RB, D], BF16)) for i in range(3)]
        ways = [es.enter_context(nc.sbuf_tensor(f"way_{n}", [P, CH + SLOTS + 2, RB], I8))
                for n in ("diag", "up", "left")]
        gate = tanh_gate(nc, es, d["g_xattn"], "dtw")
        dtw_costs(nc, d, dist, ways, part, rows_came)
        backtrack(nc, d, ways, path, part, x_sb, gate)


def dtw_distances(nc, d, xnT, ctxT, dist):
    with ExitStack() as es:
        sq = es.enter_context(nc.sbuf_tensor("sq", [P, 2, 2, 512], F32))
        ones2 = es.enter_context(nc.sbuf_tensor("ones2", [P, 2, 2], F32))
        add2 = es.enter_context(nc.sbuf_tensor("add2", [2, 2], F32))
        rows_i = es.enter_context(nc.sbuf_tensor("rows_i", [2, B, PADI], F32))
        rows_j = es.enter_context(nc.sbuf_tensor("rows_j", [2, B, S], F32))
        stage = es.enter_context(nc.sbuf_tensor("stage", [P, SLOTS, PITCH], F32))
        ps_n = [es.enter_context(nc.psum_tensor(f"ps_n{i}", [P, 512], F32)) for i in range(2)]
        ps_d = [es.enter_context(nc.psum_tensor(f"ps_d{i}", [P, 512], F32)) for i in range(2)]
        consts = es.enter_context(nc.semaphore("d_consts"))
        squared = es.enter_context(nc.semaphore("squared"))
        normed = es.enter_context(nc.semaphore("normed"))
        norm_kept = es.enter_context(nc.semaphore("norm_kept"))
        prod = es.enter_context(nc.semaphore("d_prod"))
        clipped = es.enter_context(nc.semaphore("d_clipped"))
        rooted = es.enter_context(nc.semaphore("d_rooted"))
        filled = es.enter_context(nc.semaphore("d_filled"))
        stored = es.enter_context(nc.semaphore("d_stored"))
        jobs = [(0, b, c, 1.0) for b in range(B) for c in range(0, SK, 512)] + [(1, b, 0, 0.25) for b in range(B)]
        with nc.Block() as block:
            def keep_norm(dve, n):
                w, b, c, f = jobs[n]
                if n == 0:
                    dve.wait_ge(consts, 32)
                    dve.wait_ge(filled, 4)
                dve.wait_ge(normed, n + 1)
                dst = rows_j[:, b, :] if w else rows_i[:, b, c:c + 512]
                nc.vector.tensor_scalar(dst, ps_n[n % 2][0:2, :], add2[:, w:w + 1], None,
                                        ALU.add).then_inc(norm_kept, 1)

            @block.sync
            def _(sp):
                sp.dma_start(ones2[:], d["c_ones2"]).then_inc(consts, 16)
                sp.dma_start(add2[:], d["c_add2"]).then_inc(consts, 16)

            @block.gpsimd
            def _(pool):
                nc.gpsimd.memset(rows_i[:, :, :], 1.0).then_inc(filled, 1)
                pool.wait_ge(filled, 1)
                nc.gpsimd.memset(rows_i[0:1, :, SK:PADI], FAR2).then_inc(filled, 1)
                nc.gpsimd.memset(stage[:, S:SLOTS, :], FAR).then_inc(filled, 1)
                nc.gpsimd.memset(stage[:, 0:S, 0], FAR).then_inc(filled, 1)

            @block.vector
            def _(dve):
                for n, (w, b, c, f) in enumerate(jobs):
                    if n >= 2:
                        dve.wait_ge(normed, n - 1)
                    for h in range(DH):
                        src = xnT[:, h, b * S:(b + 1) * S] if w else ctxT[:, b, h, c:c + 512]
                        i = nc.vector.scalar_tensor_tensor(sq[:, n % 2, h, :], src, f, src, ALU.mult, ALU.mult)
                    i.then_inc(squared, 1)
                    if n >= 1:
                        keep_norm(dve, n - 1)
                keep_norm(dve, len(jobs) - 1)

            @block.tensor
            def _(pe):
                pe.wait_ge(consts, 32)
                for n, (w, b, c, f) in enumerate(jobs):
                    pe.wait_ge(squared, n + 1)
                    if n >= 2:
                        pe.wait_ge(norm_kept, n - 1)
                    for h in range(DH):
                        last = nc.tensor.matmul(ps_n[n % 2][0:2, :], ones2[:, w, :], sq[:, n % 2, h, :],
                                                start=(h == 0), stop=(h == DH - 1))
                    last.then_inc(normed, 1)
        with nc.Block() as block:
            @block.tensor
            def _(pe):
                for k in range(RB):
                    if k >= 2:
                        pe.wait_ge(clipped, k - 1)
                    for b in range(B):
                        o = ps_d[k % 2][32 * b:32 * b + 32, :]
                        for h in range(DH):
                            nc.tensor.matmul(o, ctxT[:, b, h, k:PADI:RB], xnT[:, h, b * S:(b + 1) * S],
                                             start=(h == 0), stop=False, tile_position=(0, 32 * b))
                        last = nc.tensor.matmul(o, rows_i[:, b, k:PADI:RB], rows_j[:, b, :], start=False, stop=True,
                                                tile_position=(0, 32 * b))
                    last.then_inc(prod, 1)

            @block.vector
            def _(dve):
                for k in range(RB):
                    dve.wait_ge(prod, k + 1)
                    nc.vector.tensor_scalar(stage[:, 0:S, 1 + k], ps_d[k % 2][:, :], 0.0, None,
                                            ALU.max).then_inc(clipped, 1)

            @block.scalar
            def _(act):
                for k in range(RB):
                    act.wait_ge(clipped, k + 1)
                    nc.scalar.activation(stage[:, 0:S, 1 + k], stage[:, 0:S, 1 + k], ACT.Sqrt).then_inc(rooted, 1)

            @block.sync
            def _(sp):
                sp.wait_ge(rooted, RB)
                sp.dma_start(dist.rearrange("p (s k) -> p s k", k=PITCH), stage[:, :, :]).then_inc(stored, 16)
                sp.wait_ge(stored, 16)


def dtw_costs(nc, d, dist, ways, part, rows_came):
    with ExitStack() as es:
        def sb(name, shape, dt):
            return es.enter_context(nc.sbuf_tensor(name, shape, dt))

        def sem(name):
            return es.enter_context(nc.semaphore(name))

        cost = [sb(f"cost{i}", [P, CH + 1, PITCH], F32) for i in range(2)]
        m = sb("m", [P, CH, RB], F32)
        up_ok = sb("up_ok", [P, CH, RB], BF16)
        best = sb("best", [P, CH, RB], F32)
        way = [[sb(f"chunk_{n}{i}", [P, CH, RB], BF16) for n in ("diag", "up", "left")] for i in range(2)]
        KP = RB // 3
        rows = sb("ctx_rows", [P, KP, D], F32)
        loaded = [sem(f"dist_loaded{i}") for i in range(2)]
        freed = [sem(f"dist_freed{i}") for i in range(2)]
        seeded, edge, minned, scanned = sem("seeded"), sem("edge"), sem("minned"), sem("scanned")
        coded, kept, blank = sem("coded"), sem("kept"), sem("blank")
        zeroed, split, tail = sem("zeroed"), sem("split"), sem("tail")
        shift_up = [NBLK - 1] + list(range(NBLK - 1))
        full = SK // RB
        G = 4
        pieces = [(op, s0) for op in range(5) for s0 in range(0, CH, G)]
        with nc.Block() as block:
            @block.sync
            def _(sp):
                sp.wait_ge(blank, 1)
                sp.dma_start(cost[1][:, CH, :], d["c_corner"]).then_inc(seeded, 16)
                with sp.Fori(0, NCH // 2) as it:
                    for h in range(2):
                        sp.wait_ge(freed[h], it + 1)
                        src = ap_of(dist, (2 * it + h) * (CH * PITCH),
                                    [[NBLK * ROW, B], [ROW - PITCH, NBLK], [PITCH, CH], [1, PITCH]])
                        sp.dma_start(cost[h][:, 1:CH + 1, :], src).then_inc(loaded[h], 16)

            @block.vector
            def _(dve):
                def rule(h, op, s0, n=G):
                    w = cost[h]
                    s = slice(s0, s0 + n)
                    cu, cd, cl = w[:, s0 + 1:s0 + n + 1, 0:RB], w[:, s, 0:RB], w[:, s, 1:PITCH]
                    dg, up, lf = (x[:, s, :] for x in way[h])
                    if op == 0:
                        return nc.vector.tensor_tensor(up_ok[:, s, :], cu, cl, ALU.is_le)
                    if op == 1:
                        return nc.vector.tensor_tensor(best[:, s, :], cu, cl, ALU.min)
                    if op == 2:
                        return nc.vector.tensor_tensor(dg, cd, best[:, s, :], ALU.is_le)
                    if op == 3:
                        return nc.vector.tensor_tensor(up, up_ok[:, s, :], dg, ALU.is_gt)
                    return nc.vector.scalar_tensor_tensor(lf, up_ok[:, s, :], 0.0, dg, ALU.is_equal, ALU.is_gt)

                nc.vector.memset(cost[1][:, :, :], FAR).then_inc(blank, 1)
                nc.vector.nop().then_inc(freed[0], 1)
                dve.wait_ge(seeded, 16)
                with dve.Fori(0, NCH // 2) as it:
                    for h in range(2):
                        w, before = cost[h], cost[1 - h]
                        dve.wait_ge(loaded[h], it * 16 + 16)
                        if h == 1:
                            dve.wait_ge(scanned, CH)
                        nc.vector.tensor_copy(w[:, 0, :], before[:, CH, :]).then_inc(edge, 1)
                        todo = list(pieces)
                        for s in range(CH):
                            n = h * CH + s
                            dve.wait_ge(*((edge, h + 1) if s == 0 else (scanned, n)))
                            nc.vector.stream_shuffle(w[:, s + 1, 0:1], w[:, s, RB:RB + 1], shift_up)
                            nc.vector.tensor_tensor(m[:, s, :], w[:, s, 0:RB], w[:, s, 1:PITCH],
                                                    ALU.min).then_inc(minned, 1)
                            if s == 1:
                                dve.wait_ge(kept, it * 2 + h + 1)
                            if s >= 1 and todo:
                                rule(1 - h, *todo.pop(0))
                            dve.wait_ge(minned, n + 1)
                            nc.vector.tensor_tensor_scan(w[:, s + 1, 1:PITCH], m[:, s, :], w[:, s + 1, 1:PITCH],
                                                         w[:, s + 1, 0:1], ALU.min, ALU.add).then_inc(scanned, 1)
                            if s >= 1 and todo:
                                i = rule(1 - h, *todo.pop(0))
                                if not todo:
                                    i.then_inc(coded, 1)
                                    dve.wait_ge(coded, it * 2 + h + 1)
                                    nc.vector.nop().then_inc(freed[1 - h], 1)
                        assert not todo
                    dve.wait_ge(scanned, 2 * CH)
                    dve.sem_clear(scanned)
                    dve.sem_clear(minned)
                    dve.sem_clear(edge)
                dve.wait_ge(kept, NCH)
                for op in range(5):
                    rule(1, op, 0, CH).then_inc(coded if op == 4 else tail, 1)
                    if op < 4:
                        dve.wait_ge(tail, op + 1)

            @block.scalar
            def _(act):
                nc.scalar.nop().then_inc(kept, 1)

                def keep(buf, at):
                    for a, w in zip(ways, way[buf]):
                        last = nc.scalar.copy(a[:, bass.ds(at, CH), :], w[:, :, ::-1])
                    last.then_inc(kept, 1)

                with act.Fori(0, NCH // 2) as it:
                    for h in range(2):
                        act.wait_ge(coded, it * 2 + h + 1)
                        keep(1 - h, it * (2 * CH) + h * CH)
                act.wait_ge(coded, NCH + 1)
                keep(1, NCH * CH)

            @block.gpsimd
            def _(pool):
                for q in range(3):
                    nc.gpsimd.memset(rows[:, :, :], 0.0).then_inc(zeroed, 1)
                    pool.wait_ge(zeroed, q + 1)
                    for b in range(B):
                        c = d["ctx_1024"][b]
                        pool.dma_start(rows[32 * b:32 * b + full, :, :],
                                       c[0:full * RB, :].rearrange("(c k) d -> c k d", k=RB)[:, q * KP:(q + 1) * KP, :]
                                       ).then_inc(rows_came, 16)
                        if q == 0:
                            pool.dma_start(rows[32 * b + full:32 * b + full + 1, 0:SK - full * RB, :],
                                           c[full * RB:SK, :].rearrange("(c k) d -> c k d", c=1)).then_inc(rows_came, 16)
                    pool.wait_ge(rows_came, 16 * B * (q + 2))
                    p0, p1, p2 = (x[:, q * KP:(q + 1) * KP, :] for x in part)
                    nc.gpsimd.tensor_copy(p0, rows[:]).then_inc(split, 1)
                    pool.wait_ge(split, 4 * q + 1)
                    nc.gpsimd.tensor_tensor(rows[:], rows[:], p0, ALU.subtract).then_inc(split, 1)
                    pool.wait_ge(split, 4 * q + 2)
                    nc.gpsimd.tensor_copy(p1, rows[:]).then_inc(split, 1)
                    pool.wait_ge(split, 4 * q + 3)
                    nc.gpsimd.tensor_tensor(p2, rows[:], p1, ALU.subtract).then_inc(split, 1)
                    pool.wait_ge(split, 4 * q + 4)


def backtrack(nc, d, ways, path, part, x_sb, gate):
    with ExitStack() as es:
        def sb(name, shape, dt):
            return es.enter_context(nc.sbuf_tensor(name, shape, dt))

        def sem(name):
            return es.enter_context(nc.semaphore(name))

        W2 = 2 * RB
        on = [sb(f"on{i}", [P, CH, W2 + 2], BF16) for i in range(2)]
        packed = [sb(f"packed{i}", [P, CH, RB], BF16) for i in range(2)]
        came = [sb(f"came{i}", [P, CH + 1, W2 + 2], BF16) for i in range(2)]
        went = [sb(f"went{i}", [P, CH + 1, W2 + 2], BF16) for i in range(2)]
        enter = sb("enter", [P, 2, W2], BF16)
        inner = sb("inner", [P, 1], F32)
        first = sb("first", [P, 2, CH], BF16)
        onp = sb("onp", [P, P, RB], BF16)
        ps = [es.enter_context(nc.psum_tensor(f"ps_e{i}", [P, 512], F32)) for i in range(2 * B)]
        b_end, ones_in, fetched = sem("b_end"), sem("b_ones"), sem("fetched")
        edges, entered, traced, done = sem("b_edges"), sem("b_entered"), sem("b_traced"), sem("b_done")
        pack, saved = sem("b_pack"), [sem("b_saved0"), sem("b_saved1")]
        taken, summed, added = sem("b_taken"), sem("b_summed"), sem("b_added")
        shift_down = list(range(1, NBLK)) + [0]
        turns = [NCH // 2 - jt * (P // CH) // 2 for jt in range(QT - 1, -1, -1)]
        with nc.Block() as block:
            @block.sync
            def _(sp):
                sp.dma_start(inner[:], d["c_inner"]).then_inc(saved[0], 16)
                sp.dma_start(on[1][:, 0, :], d["c_seed"].bitcast(BF16)).then_inc(saved[1], 16)
                start = 0
                for q, end in enumerate(turns):
                    with sp.Fori(start, end) as it:
                        for h in range(2):
                            sp.wait_ge(pack, it * 2 + h + 3)
                            at = (it * (-2 * CH * RB)) + (NCH - 1 - h) * CH * RB
                            sp.dma_start(path[:, bass.ds(at, CH * RB)].rearrange("p (s k) -> p s k", k=RB),
                                         packed[h][:]).then_inc(saved[h], 16)
                    start = end
                    for h in range(2):
                        sp.wait_ge(saved[h], 16 * end + 16)
                    if q:
                        sp.wait_ge(summed, q)
                    src = ap_of(path, (QT - 1 - q) * P * RB,
                                [[NBLK * SLOTS * RB, B], [SLOTS * RB + RB, NBLK], [1, P * RB]])
                    sp.dma_start(onp[:, :, :].rearrange("p s k -> p (s k)"), src).then_inc(taken, 16)

            @block.gpsimd
            def _(pool):
                end = CH + SLOTS
                for n, (a, v) in enumerate(zip(ways, (0.0, 0.0, 1.0))):
                    nc.gpsimd.memset(a[:, end - 1:end + 2, :], v).then_inc(b_end, 1)
                    pool.wait_ge(b_end, n + 1)

            @block.scalar
            def _(act):
                def fetch(h, at):
                    nc.scalar.copy(went[h][:, :, 2:W2 + 2:2], ways[1][:, bass.ds(at, CH + 1), :])
                    nc.scalar.copy(came[h][:, :, 2:W2 + 2:2], ways[0][:, bass.ds(at + 1, CH + 1), :])
                    nc.scalar.copy(came[h][:, :, 1:W2 + 1:2],
                                   ways[2][:, bass.ds(at + 1, CH + 1), :]).then_inc(fetched, 1)

                def keep(h):
                    nc.scalar.copy(packed[h][:], on[h][:, :, 3:W2 + 2:2]).then_inc(pack, 1)

                nc.scalar.nop().then_inc(pack, 2)
                act.wait_ge(b_end, 3)
                for h in range(2):
                    fetch(h, (NCH - 1 - h) * CH + CH)
                with act.Fori(0, NCH // 2 - 1) as it:
                    for h in range(2):
                        act.wait_ge(done, it * 2 + h + 1)
                        act.wait_ge(saved[h], it * 16 + 16)
                        keep(h)
                        fetch(h, (it * (-2 * CH)) + (NCH - 3 - h) * CH + CH)
                for h in range(2):
                    act.wait_ge(done, NCH - 1 + h)
                    act.wait_ge(saved[h], 8 * NCH)
                    keep(h)

            @block.tensor
            def _(pe):
                for q in range(QT):
                    jt = QT - 1 - q
                    pe.wait_ge(taken, 16 * (q + 1))
                    if q >= 2:
                        pe.wait_ge(added, q - 1)
                    for k in range(RB):
                        for i in range(3):
                            for b in range(B):
                                r = slice(32 * b, 32 * b + 32)
                                last = nc.tensor.matmul(ps[2 * b + q % 2][:, 0:D], onp[r, :, RB - 1 - k], part[i][r, k, :],
                                                        start=(k == 0 and i == 0), stop=(k == RB - 1 and i == 2),
                                                        tile_position=(32 * b, 0))
                    last.then_inc(summed, 1)

            @block.vector
            def _(dve):
                def add(q):
                    dve.wait_ge(summed, q + 1)
                    for b in range(B):
                        t = b * QT + QT - 1 - q
                        i = nc.vector.scalar_tensor_tensor(x_sb[:, t, :], ps[2 * b + q % 2][:, 0:D], gate[:, 0:1], x_sb[:, t, :],
                                                           ALU.mult, ALU.add)
                    i.then_inc(added, 1)

                for i in range(2):
                    nc.vector.memset(went[i][:, :, 1:W2 + 2:2], 1.0).then_inc(ones_in, 1)
                dve.wait_ge(ones_in, 2)
                for h in range(2):
                    dve.wait_ge(saved[h], 16)
                start = 0
                for q, end in enumerate(turns):
                    if q >= 2:
                        add(q - 2)
                    with dve.Fori(start, end) as it:
                        for h in range(2):
                            dve.wait_ge(fetched, it * 2 + h + 1)
                            dve.wait_ge(pack, it * 2 + h + 1)
                            for n, a in enumerate((went, came)):
                                nc.vector.tensor_scalar(first[:, n, :], a[h][:, 1:CH + 1, W2], inner[:, 0:1], None,
                                                        ALU.mult).then_inc(edges, 1)
                            dve.wait_ge(edges, 4 * h + 2)
                            for n, a in enumerate((went, came)):
                                nc.vector.stream_shuffle(a[h][:, 0:CH, 0], first[:, n, :], shift_down).then_inc(edges, 1)
                            dve.wait_ge(edges, 4 * h + 4)
                            for s in range(CH - 1, -1, -1):
                                n = h * CH + CH - 1 - s
                                if n:
                                    dve.wait_ge(traced, n)
                                after = on[h][:, s + 1, :] if s < CH - 1 else on[1 - h][:, 0, :]
                                nc.vector.stream_shuffle(on[h][:, s, 1:2], after[:, W2 + 1:W2 + 2], shift_down)
                                pair = ap_of(after, 1, [after.ap[0], [2, RB], [2, 2]])
                                nc.vector.tensor_tensor(
                                    enter[:, s % 2, :].rearrange("p (r e) -> p r e", e=2), pair,
                                    came[h][:, s, 0:W2].rearrange("p (r e) -> p r e", e=2), ALU.mult).then_inc(entered, 1)
                                dve.wait_ge(entered, n + 1)
                                nc.vector.tensor_tensor_scan(on[h][:, s, 2:W2 + 2], went[h][:, s, 0:W2],
                                                             enter[:, s % 2, :], on[h][:, s, 1:2],
                                                             ALU.mult, ALU.add).then_inc(traced, 1)
                            dve.wait_ge(traced, (h + 1) * CH)
                            nc.vector.nop().then_inc(done, 1)
                        for s in (edges, entered, traced):
                            dve.sem_clear(s)
                    start = end
                add(QT - 2)
                add(QT - 1)


NH, HD = 16, 16
HG = 4
NG = NH // HG
NPART = 6
STK = NPART * HD
MAXR = 3
VW = 32
NEG = -1e30
K_SLOTS = ((0, 1, 2), (3, 4), (5,))
Q_SLOTS = ((0, 3, 5), (1, 4), (2,))


class Names:

    def __init__(self, nc, es, stage):
        self.nc, self.es, self.stage = nc, es, stage
        self.sems = []

    def sb(self, name, shape, dt=F32):
        return self.es.enter_context(self.nc.sbuf_tensor(f"{self.stage}_{name}", shape, dt))

    def ps(self, name, shape, dt=F32):
        return self.es.enter_context(self.nc.psum_tensor(f"{self.stage}_{name}", shape, dt))

    def sem(self, name):
        s = self.es.enter_context(self.nc.semaphore(f"{self.stage}_{name}"))
        self.sems.append(s)
        return s

    def clear(self):
        for s in self.sems:
            self.nc.gpsimd.sem_clear(s)
        self.nc.all_engine_barrier()


def project_tokens(nc, nm, jobs):
    ps = [nm.ps(f"proj{i}", [P, 512]) for i in range(2)]
    done, kept = nm.sem("proj_done"), [nm.sem("proj_kept0"), nm.sem("proj_kept1")]
    static = nm.sem("proj_in")

    def run(copies):
        with nc.Block() as block:
            @block.scalar
            def _(act):
                for dst, src in copies:
                    last = nc.scalar.copy(dst, src)
                last.then_inc(static, 1)
                for n, (out, lhs, rhs, view) in enumerate(jobs):
                    if n % 2:
                        act.wait_ge(done, n + 1)
                        nc.scalar.copy(out, view(ps[n % 2])).then_inc(kept[1], 1)

            @block.vector
            def _(dve):
                for n, (out, lhs, rhs, view) in enumerate(jobs):
                    if n % 2 == 0:
                        dve.wait_ge(done, n + 1)
                        nc.vector.tensor_copy(out, view(ps[n % 2])).then_inc(kept[0], 1)

            @block.tensor
            def _(pe):
                pe.wait_ge(static, 1)
                for n, (out, lhs, rhs, view) in enumerate(jobs):
                    if n >= 2:
                        pe.wait_ge(kept[n % 2], n // 2)
                    for h in range(DH):
                        last = nc.tensor.matmul(ps[n % 2][:, 0:rhs[h].shape[1]], lhs[h], rhs[h],
                                                start=(h == 0), stop=(h == DH - 1))
                    last.then_inc(done, 1)
    return run


def split_stacks(nc, nm, jobs):
    first, rest1, second, third = nm.sem("sp_first"), nm.sem("sp_rest"), nm.sem("sp_second"), nm.sem("sp_third")
    with nc.Block() as block:
        @block.vector
        def _(dve):
            for n, (src, stk, slots, scale, rest) in enumerate(jobs):
                def at(part, i=0):
                    s = slots[part][i]
                    return stk[:, :, s * HD:(s + 1) * HD]
                nc.vector.tensor_scalar(at(0), src, scale, None, ALU.mult).then_inc(first, 1)
                dve.wait_ge(first, n + 1)
                nc.vector.scalar_tensor_tensor(rest, src, scale, at(0), ALU.mult, ALU.subtract).then_inc(rest1, 1)
                dve.wait_ge(rest1, n + 1)
                nc.vector.tensor_copy(at(1), rest).then_inc(second, 1)
                dve.wait_ge(second, n + 1)
                nc.vector.tensor_tensor(at(2), rest, at(1), ALU.subtract).then_inc(third, 1)

        @block.gpsimd
        def _(pool):
            for n, (src, stk, slots, scale, rest) in enumerate(jobs):
                pool.wait_ge(second, n + 1)
                a, b = slots[1]
                nc.gpsimd.tensor_copy(stk[:, :, b * HD:(b + 1) * HD], stk[:, :, a * HD:(a + 1) * HD])

        @block.scalar
        def _(act):
            for n, (src, stk, slots, scale, rest) in enumerate(jobs):
                act.wait_ge(first, n + 1)
                a = slots[0][0]
                for b in slots[0][1:]:
                    nc.scalar.copy(stk[:, :, b * HD:(b + 1) * HD], stk[:, :, a * HD:(a + 1) * HD])


def turn_stacks(nc, nm, identb, jobs):
    ps = [nm.ps(f"turn{i}", [STK, 1024], BF16) for i in range(2)]
    turned, kept = nm.sem("turn_done"), [nm.sem("turn_kept0"), nm.sem("turn_kept1")]
    units = []
    for stk, tiles, out in jobs:
        per = 1024 // (tiles * P)
        units += [(stk, tiles, out, h0, per) for h0 in range(0, NH, per)]
    with nc.Block() as block:
        @block.tensor
        def _(pe):
            for n, (stk, tiles, out, h0, per) in enumerate(units):
                if n >= 2:
                    pe.wait_ge(kept[n % 2], n // 2)
                for i in range(per):
                    for t in range(tiles):
                        c = (i * tiles + t) * P
                        last = nc.tensor.transpose(ps[n % 2][:, c:c + P], stk[:, t, h0 + i, :], identb[:, :])
                last.then_inc(turned, 1)

        def copies(eng, parity, copy):
            for n, (stk, tiles, out, h0, per) in enumerate(units):
                if n % 2 == parity:
                    eng.wait_ge(turned, n + 1)
                    copy(out[0:STK, h0:h0 + per, :], ps[n % 2][:, :].rearrange("p (h s) -> p h s", h=per)).then_inc(
                        kept[parity], 1)

        @block.vector
        def _(dve):
            copies(dve, 0, nc.vector.tensor_copy)

        @block.scalar
        def _(act):
            copies(act, 1, nc.scalar.copy)


def attend(nc, nm, ident, identb, qT, kT, vt, attn, keys, causal, bias_q, bias_k):
    kt_n = keys // P
    halves = max(1, keys // 512)
    ps1 = [nm.ps(f"s1_{i}", [P, 512]) for i in range(2)]
    ps2 = [nm.ps(f"s2_{i}", [P, 512]) for i in range(3)]
    psm = nm.ps("mx", [MAXR, 1024], BF16)
    pso = nm.ps("o", [P, 512])
    pst = nm.ps("ot", [P, 512])
    NE = 4
    ebuf = [nm.sb(f"exp{i}", [P, 512]) for i in range(NE)]
    NJ = 4
    junk = nm.sb("junk", [P, NJ, 512], BF16)
    mx = nm.sb("max", [P, 2, HG, QT, halves])
    neg = nm.sb("neg", [P, HG * QT])
    negr = nm.sb("negr", [P, HG * QT])
    parts = nm.sb("parts", [P, 2, HG * QT, MAXR], BF16)
    osb = nm.sb("osb", [P, 2, 512])
    rden = nm.sb("rden", [P, HG * QT])
    scored, maxed = nm.sem("scored"), nm.sem("maxed")
    negated, parted = nm.sem("negated"), nm.sem("parted")
    mturned, mkept = nm.sem("mturned"), nm.sem("mkept")
    scored2, exped, weighed = nm.sem("scored2"), nm.sem("exped"), nm.sem("weighed")
    okept, oturned, inverted, normed = nm.sem("okept"), nm.sem("oturned"), nm.sem("inverted"), nm.sem("normed")
    u1 = [(h, qt, f) for h in range(HG) for qt in range(QT) for f in range(halves)]
    u2 = [(kt, h) for kt in range(kt_n) for h in range(HG)]
    n1, n2 = len(u1), len(u2)
    LAG = 2

    def width1(qt):
        return (qt + 1) * P if causal else 512

    with nc.Block() as block:
        @block.tensor
        def _(pe):
            def first(g, u):
                h, qt, f = u1[u]
                n = g * n1 + u
                if n >= 2:
                    pe.wait_ge(maxed, n - 1)
                w = width1(qt)
                nc.tensor.matmul(ps1[n % 2][:, 0:w], qT[0:STK, g * HG + h, qt * P:(qt + 1) * P],
                                 kT[0:STK, g * HG + h, f * 512:f * 512 + w], start=True, stop=True).then_inc(scored, 1)

            def turn_max(g):
                for pair in range(HG // 2):
                    pe.wait_ge(parted, 3 * (g + 1))
                    if g or pair:
                        pe.wait_ge(mkept, g * (HG // 2) + pair)
                    for i in range(2):
                        for qt in range(QT):
                            c = (i * QT + qt) * P
                            last = nc.tensor.transpose(psm[:, c:c + P], parts[:, g % 2, (2 * pair + i) * QT + qt, :],
                                                       identb[:, :])
                    last.then_inc(mturned, 1)

            def second(g, u):
                kt, h = u2[u]
                n = g * n2 + u
                if u == 0:
                    pe.wait_ge(mkept, (g + 1) * (HG // 2))
                if n >= 3:
                    pe.wait_ge(exped, n - 2)
                q0 = kt * P if causal else 0
                o = ps2[n % 3]
                nc.tensor.matmul(o[:, q0:512], kT[:, g * HG + h, kt * P:(kt + 1) * P], qT[:, g * HG + h, q0:512],
                                 start=True, stop=False)
                w = P if causal else 512
                nc.tensor.matmul(o[:, q0:q0 + w], identb[:, :], bias_k(kt), start=False,
                                 stop=True).then_inc(scored2, 1)

            def weigh(g, u):
                kt, h = u2[u]
                n = g * n2 + u
                pe.wait_ge(exped, n + 1)
                if u == 0 and g:
                    pe.wait_ge(okept, g)
                q0 = kt * P if causal else 0
                nc.tensor.matmul(pso[32 * h:32 * h + 32, q0:512], vt[:, kt, g * HG + h, :], ebuf[n % NE][:, q0:512],
                                 start=(kt == 0), stop=(kt == kt_n - 1), tile_position=(0, 32 * h),
                                 skip_group_check=True).then_inc(weighed, 1)

            def turn_out(g):
                pe.wait_ge(okept, g + 1)
                if g:
                    pe.wait_ge(normed, g)
                for qt in range(QT):
                    last = nc.tensor.transpose(pst[:, qt * P:(qt + 1) * P], osb[:, g % 2, qt * P:(qt + 1) * P],
                                               ident[:, :])
                last.then_inc(oturned, 1)

            for u in range(n1):
                first(0, u)
            turn_max(0)
            for g in range(NG):
                for u in range(n2):
                    second(g, u)
                    if g + 1 < NG and u < n1:
                        first(g + 1, u)
                    if u >= LAG:
                        weigh(g, u - LAG)
                    if u == LAG + 2 and g:
                        turn_out(g - 1)
                for u in range(n2 - LAG, n2):
                    weigh(g, u)
                if g + 1 < NG:
                    turn_max(g + 1)
            turn_out(NG - 1)

        @block.vector
        def _(dve):
            def take_max(g, u):
                h, qt, f = u1[u]
                n = g * n1 + u
                dve.wait_ge(scored, n + 1)
                w = width1(qt)
                if n >= NJ:
                    dve.wait_ge(maxed, n - NJ + 1)
                nc.vector.tensor_tensor_reduce(junk[:, n % NJ, 0:w], ps1[n % 2][:, 0:w], bias_q(qt, f), 1.0, NEG * 4,
                                               ALU.add, ALU.max, mx[:, g % 2, h, qt, f:f + 1]).then_inc(maxed, 1)

            def negate(g):
                dve.wait_ge(maxed, (g + 1) * n1)
                if g:
                    dve.wait_ge(parted, 3 * g)
                m = mx[:, g % 2, :, :, :].rearrange("p h t f -> p (h t) f")
                nc.vector.tensor_reduce(neg[:, :], m, AX.X, ALU.max, negate=True).then_inc(negated, 1)
                dve.wait_ge(negated, 3 * g + 1)
                p3 = parts[:, g % 2, :, :]
                nc.vector.tensor_copy(p3[:, :, 0], neg[:, :]).then_inc(parted, 1)
                dve.wait_ge(parted, 3 * g + 1)
                nc.vector.tensor_tensor(negr[:, :], neg[:, :], p3[:, :, 0], ALU.subtract).then_inc(negated, 1)
                dve.wait_ge(negated, 3 * g + 2)
                nc.vector.tensor_copy(p3[:, :, 1], negr[:, :]).then_inc(parted, 1)
                dve.wait_ge(parted, 3 * g + 2)
                nc.vector.tensor_tensor(neg[:, :], negr[:, :], p3[:, :, 1], ALU.subtract).then_inc(negated, 1)
                dve.wait_ge(negated, 3 * g + 3)
                nc.vector.tensor_copy(p3[:, :, 2], neg[:, :]).then_inc(parted, 1)

            def normalise(g):
                dve.wait_ge(oturned, g + 1)
                if g:
                    dve.wait_ge(normed, g)
                t = pst[:, :].rearrange("p (t h e) -> p t h e", t=QT, h=HG)
                r = rden[:, :].rearrange("p (t h) -> p t h", t=QT)
                nc.vector.reciprocal(r, t[:, :, :, HD]).then_inc(inverted, 1)
                dve.wait_ge(inverted, g + 1)
                for qt in range(QT):
                    o = attn[:, qt, g * HG * HD:(g + 1) * HG * HD].rearrange("p (h e) -> p h e", h=HG)
                    rb = ap_of(rden[:, qt * HG:(qt + 1) * HG], 0, [rden[:, :].ap[0], [1, HG], [0, HD]])
                    i = nc.vector.tensor_tensor(o, t[:, qt, :, 0:HD], rb, ALU.mult)
                i.then_inc(normed, 1)

            for u in range(n1):
                take_max(0, u)
            negate(0)
            for g in range(NG):
                for u in range(n1):
                    if g + 1 < NG:
                        take_max(g + 1, u)
                    if u == LAG + 3 and g:
                        normalise(g - 1)
                if g + 1 < NG:
                    negate(g + 1)
            normalise(NG - 1)

        @block.scalar
        def _(act):
            def keep_max(g):
                for pair in range(HG // 2):
                    act.wait_ge(mturned, g * (HG // 2) + pair + 1)
                    h0 = g * HG + 2 * pair
                    nc.scalar.copy(qT[STK:STK + MAXR, h0:h0 + 2, :],
                                   psm[:, :].rearrange("p (h s) -> p h s", h=2)).then_inc(mkept, 1)

            keep_max(0)
            for g in range(NG):
                for u in range(n2):
                    n = g * n2 + u
                    kt, h = u2[u]
                    q0 = kt * P if causal else 0
                    act.wait_ge(scored2, n + 1)
                    if n >= NE:
                        act.wait_ge(weighed, n - NE + 1)
                    nc.scalar.activation(ebuf[n % NE][:, q0:512], ps2[n % 3][:, q0:512], ACT.Exp).then_inc(exped, 1)
                act.wait_ge(weighed, (g + 1) * n2)
                if g >= 2:
                    act.wait_ge(oturned, g - 1)
                nc.scalar.copy(osb[:, g % 2, :], pso[:, :]).then_inc(okept, 1)
                if g + 1 < NG:
                    keep_max(g + 1)


def project_out(nc, nm, ident, attn, w, add):
    ps = [nm.ps(f"at{i}", [P, 512]) for i in range(2)]
    py = [nm.ps(f"ay{i}", [P, 512]) for i in range(2)]
    aT = nm.sb("attnT", [P, DH, QT * P])
    turned, kept, done, added = nm.sem("at_turned"), nm.sem("at_kept"), nm.sem("at_done"), nm.sem("at_added")
    with nc.Block() as block:
        @block.tensor
        def _(pe):
            for h in range(DH):
                for t in range(QT):
                    last = nc.tensor.transpose(ps[h][:, t * P:(t + 1) * P], attn[:, t, h * P:(h + 1) * P], ident[:, :])
                last.then_inc(turned, 1)
            pe.wait_ge(kept, DH)
            for t in range(QT):
                if t >= 2:
                    pe.wait_ge(added, t - 1)
                for h in range(DH):
                    last = nc.tensor.matmul(py[t % 2][:, 0:D], aT[:, h, t * P:(t + 1) * P], w[:, h, :],
                                            start=(h == 0), stop=(h == DH - 1))
                last.then_inc(done, 1)

        @block.scalar
        def _(act):
            for h in range(DH):
                act.wait_ge(turned, h + 1)
                nc.scalar.copy(aT[:, h, :], ps[h][:, :]).then_inc(kept, 1)

        @block.vector
        def _(dve):
            for t in range(QT):
                dve.wait_ge(done, t + 1)
                add(t, py[t % 2][:, 0:D]).then_inc(added, 1)


def self_attention(nc, d, x_sb, y_sb, ident, identb):
    with ExitStack() as es:
        hT = es.enter_context(nc.sbuf_tensor("l0_hT", [P, DH, B * S], F32))
        vecs = es.enter_context(nc.sbuf_tensor("l0_vecs", [P, 2, DH], F32))
        wqkv = es.enter_context(nc.sbuf_tensor("l0_wqkv", [P, DH, 3 * D], F32))
        wproj = es.enter_context(nc.sbuf_tensor("l0_wproj", [P, DH, D], F32))
        rope = es.enter_context(nc.sbuf_tensor("l0_rope", [P, 2, QT * NH, HD // 2], F32))
        tri_q = es.enter_context(nc.sbuf_tensor("l0_tri_q", [P, 512], BF16))
        tri_k = es.enter_context(nc.sbuf_tensor("l0_tri_k", [P, P], BF16))
        got = es.enter_context(nc.semaphore("l0_got"))
        with nc.Block() as block:
            @block.sync
            def _(sp):
                sp.dma_start(wqkv[:], d["L0_ffn_Wqkv"].rearrange("(h p) n -> p h n", p=P)).then_inc(got, 16)
                sp.dma_start(wproj[:], d["L0_ffn_Wproj"].rearrange("(h p) n -> p h n", p=P)).then_inc(got, 16)
                for i, n in enumerate(("L0_ffn_ln1_g", "L0_ffn_ln1_b")):
                    for h in range(DH):
                        sp.dma_start(vecs[:, i, h:h + 1],
                                     d[n][h * P:(h + 1) * P].rearrange("(p o) -> p o", o=1)).then_inc(got, 16)
                sp.dma_start(rope[:], d["c_rope"]).then_inc(got, 16)
                sp.dma_start(tri_q[:], d["c_tri_q"].bitcast(BF16)).then_inc(got, 16)
                sp.dma_start(tri_k[:], d["c_tri_k"].bitcast(BF16)).then_inc(got, 16)
                sp.wait_ge(got, 16 * 9)
        with ExitStack() as es1:
            layer_norm(nc, es1, x_sb, y_sb, "l0a")
            hn = es1.enter_context(nc.sbuf_tensor("l0_hn", [P, NT, D], F32))
            layer_norm(nc, es1, y_sb, hn, "l0b")
            transpose_tokens(nc, es1, hn, lambda g, h: hT[:, h, g * 512:(g + 1) * 512], ident, "l0T",
                             scale=vecs[:, 0, :], bias=vecs[:, 1, :])
        sb = Names(nc, es, "l0")
        hTb = sb.sb("hTb", [P, DH, S])
        qkv = sb.sb("qkv", [P, QT, 3 * D])
        qT = sb.sb("qT", [STK + MAXR, NH, S], BF16)
        kT = sb.sb("kT", [STK + MAXR, NH, S], BF16)
        vt = sb.sb("vt", [P, QT, NH, VW])
        attn = sb.sb("attn", [P, QT, D])
        with nc.Block() as block:
            @block.vector
            def _(dve):
                nc.vector.memset(kT[STK:STK + MAXR, :, :], 1.0)
                nc.vector.memset(vt[:, :, :, HD:HD + 1], 1.0)
                nc.vector.memset(vt[:, :, :, HD + 1:VW], 0.0)
        with nc.Fori(0, B) as b:
            with ExitStack() as e1:
                nm = Names(nc, e1, "l0p")
                jobs = [(qkv[:, t, c:c + 384], [hTb[:, h, t * P:(t + 1) * P] for h in range(DH)],
                         [wqkv[:, h, c:c + 384] for h in range(DH)], lambda ps: ps[:, 0:384])
                        for t in range(QT) for c in (0, 384)]
                project_tokens(nc, nm, jobs)([(hTb[:, :, :], hT[:, :, bass.ds(b * S, S)])])
                nm.clear()
            with ExitStack() as e1:
                nm = Names(nc, e1, "l0s")
                qr = nm.sb("qr", [P, QT * NH, 2, HD])
                tmp = nm.sb("ropetmp", [P, 4, QT * NH, 2, HD // 2])
                stk = [nm.sb(f"stk{i}", [P, QT * NH, STK], BF16) for i in range(2)]
                rest = nm.sb("rest", [P, QT * NH, HD])
                rotated, summed = nm.sem("rotated"), nm.sem("rsummed")
                src = qkv[:, :, :].rearrange("p t (h c e) -> p (t h) c e", h=NH, c=3)
                half = HD // 2
                with nc.Block() as block:
                    @block.vector
                    def _(dve):
                        for i, (part, table) in enumerate(((0, 1), (1, 0), (0, 0), (1, 1))):
                            for c in range(2):
                                a = src[:, :, c, part * half:(part + 1) * half]
                                j = nc.vector.tensor_tensor(tmp[:, i, :, c, :], a, rope[:, table, :, :], ALU.mult)
                        j.then_inc(rotated, 1)
                        dve.wait_ge(rotated, 1)
                        for c in range(2):
                            nc.vector.tensor_tensor(qr[:, :, c, 0:half], tmp[:, 0, :, c, :], tmp[:, 1, :, c, :],
                                                    ALU.subtract)
                            nc.vector.tensor_tensor(qr[:, :, c, half:HD], tmp[:, 2, :, c, :], tmp[:, 3, :, c, :],
                                                    ALU.add)

                    @block.scalar
                    def _(act):
                        nc.scalar.copy(vt[:, :, :, 0:HD].rearrange("p t h e -> p (t h) e"), src[:, :, 2, :])
                split_stacks(nc, nm, [(qr[:, :, 0, :], stk[0], Q_SLOTS, HD ** -0.5, rest[:, :, :]),
                                      (qr[:, :, 1, :], stk[1], K_SLOTS, 1.0, rest[:, :, :])])
                v = [s[:, :, :].rearrange("p (t h) e -> p t h e", t=QT) for s in stk]
                turn_stacks(nc, nm, identb, [(v[0], QT, qT), (v[1], QT, kT)])
                nm.clear()
            with ExitStack() as e1:
                nm = Names(nc, e1, "l0a")
                attend(nc, nm, ident, identb, qT, kT, vt, attn, S, True,
                       lambda qt, f: tri_q[:, 512 - (qt + 1) * P:512], lambda kt: tri_k[:, :])
                nm.clear()
            with ExitStack() as e1:
                nm = Names(nc, e1, "l0o")

                def add(t, prod):
                    y = y_sb[:, bass.ds(b * QT + t, 1), :].rearrange("p o d -> p (o d)")
                    return nc.vector.tensor_tensor(y, prod, y, ALU.add)
                project_out(nc, nm, ident, attn, wproj, add)
                nm.clear()


NEXP, FF = 8, 4 * D
CAP = -(-2 * B * S // NEXP)
FC = FF // P
FULL = 1 << 16


def route(nc, d, h2T, hn, xs, slots, gates, sent):
    with ExitStack() as es1:
        nm = Names(nc, es1, "rt")
        wg = nm.sb("wg", [P, DH, NEXP])
        tri = nm.sb("tri", [P, P])
        ones = nm.sb("ones", [P, P])
        rank = nm.sb("rank", [P, NT, NEXP])
        base = nm.sb("base", [P, NT, NEXP])
        zeros = nm.sb("zeros", [P, 8, D])
        g = nm.sb("g", [P, NT, NEXP])
        e = nm.sb("e", [P, NT, NEXP])
        eq = nm.sb("eq", [P, NT, NEXP])
        hot = nm.sb("hot", [P, 2, NT, NEXP])
        mask = nm.sb("mask", [P, NT, NEXP])
        before = nm.sb("before", [P, NT, NEXP])
        val = nm.sb("val", [P, 3, NT, NEXP])
        pick = nm.sb("pick", [P, 2, 3, NT, NEXP])
        got_f = nm.sb("slotf", [P, 2, 2, NT])
        m = nm.sb("m", [P, NT])
        s = nm.sb("s", [P, NT])
        ps = nm.ps("lg", [P, 512])
        pc = nm.ps("cum", [P, 512])
        got, scored, lowered, exped = nm.sem("got"), nm.sem("scored"), nm.sem("lowered"), nm.sem("exped")
        step, masked, counted, indexed = nm.sem("step"), nm.sem("masked"), nm.sem("counted"), nm.sem("indexed")
        zeroed, cleared = nm.sem("zeroed"), nm.sem("cleared")

        def per_token(t):
            return ap_of(t[:, :], 0, [t[:, :].ap[0], [1, NT], [0, NEXP]])

        with nc.Block() as block:
            @block.sync
            def _(sp):
                sp.dma_start(wg[:], d["L0_ffn_Wgate"].rearrange("(h p) n -> p h n", p=P)).then_inc(got, 16)
                sp.dma_start(tri[:], d["c_tri"]).then_inc(got, 16)
                sp.dma_start(ones[:], d["c_ones"]).then_inc(got, 16)
                sp.dma_start(rank[:], d["c_rank"]).then_inc(got, 16)
                sp.dma_start(base[:], d["c_base"]).then_inc(got, 16)
                sp.wait_ge(zeroed, 1)
                for q in range(NEXP * CAP // (8 * P)):
                    sp.dma_start(xs[q * 8 * P:(q + 1) * 8 * P, :].rearrange("(p r) k -> p r k", p=P),
                                 zeros[:, :, :]).then_inc(cleared, 16)

            @block.gpsimd
            def _(pool):
                nc.gpsimd.memset(zeros[:, :, :], 0.0).then_inc(zeroed, 1)
                pool.wait_ge(cleared, 16 * (NEXP * CAP // (8 * P)))
                pool.wait_ge(indexed, 1)
                for t in range(NT):
                    for c in range(2):
                        nc.gpsimd.indirect_dma_start(
                            xs[:, :], bass.IndirectOffsetOnAxis(slots[:, c, 0, t:t + 1], 0), hn[:, t, :], None,
                            bounds_check=NEXP * CAP - 1, oob_is_err=False).then_inc(sent, 16)
                pool.wait_ge(sent, 16 * 2 * NT)

            @block.tensor
            def _(pe):
                pe.wait_ge(got, 80)
                for t in range(NT):
                    for h in range(DH):
                        last = nc.tensor.matmul(ps[:, t * NEXP:(t + 1) * NEXP], h2T[:, h, t * P:(t + 1) * P],
                                                wg[:, h, :], start=(h == 0), stop=(h == DH - 1))
                last.then_inc(scored, 1)
                pe.wait_ge(masked, 1)
                n = NT * NEXP
                nc.tensor.matmul(pc[:, 0:n], tri[:, :], mask[:, :, :].rearrange("p t e -> p (t e)"), start=True,
                                 stop=False)
                nc.tensor.matmul(pc[:, 0:n], ones[:, :], before[:, :, :].rearrange("p t e -> p (t e)"), start=False,
                                 stop=True).then_inc(counted, 1)

            @block.scalar
            def _(act):
                act.wait_ge(lowered, 1)
                nc.scalar.activation(e[:, :, :], g[:, :, :], ACT.Exp).then_inc(exped, 1)

            @block.vector
            def _(dve):
                count = [0]

                def then(i):
                    count[0] += 1
                    i.then_inc(step, 1)
                    dve.wait_ge(step, count[0])

                tt, ts = nc.vector.tensor_tensor, nc.vector.tensor_scalar
                dve.wait_ge(scored, 1)
                lg = ps[:, 0:NT * NEXP].rearrange("p (t e) -> p t e", e=NEXP)
                then(nc.vector.tensor_reduce(m[:, :], lg, AX.X, ALU.max))
                tt(g[:, :, :], lg, per_token(m), ALU.subtract).then_inc(lowered, 1)
                dve.wait_ge(exped, 1)
                then(nc.vector.tensor_reduce(s[:, :], e[:, :, :], AX.X, ALU.add))
                then(nc.vector.reciprocal(s[:, :], s[:, :]))
                then(tt(g[:, :, :], e[:, :, :], per_token(s), ALU.mult))
                then(nc.vector.tensor_copy(e[:, :, :], g[:, :, :]))
                dve.wait_ge(got, 80)
                for i in range(2):
                    then(nc.vector.tensor_reduce(m[:, :], e[:, :, :], AX.X, ALU.max))
                    then(tt(eq[:, :, :], e[:, :, :], per_token(m), ALU.is_equal))
                    then(tt(eq[:, :, :], eq[:, :, :], rank[:, :, :], ALU.mult))
                    then(nc.vector.tensor_reduce(m[:, :], eq[:, :, :], AX.X, ALU.max))
                    then(tt(hot[:, i, :, :], eq[:, :, :], per_token(m), ALU.is_equal))
                    if i == 0:
                        then(nc.vector.scalar_tensor_tensor(e[:, :, :], hot[:, 0, :, :], -2.0, e[:, :, :], ALU.mult,
                                                            ALU.add))
                then(tt(mask[:, :, :], hot[:, 0, :, :], hot[:, 1, :, :], ALU.add))
                then(nc.vector.memset(before[:, 0, :], 0.0))
                for t in range(1, NT):
                    i = tt(before[:, t, :], before[:, t - 1, :], mask[:, t - 1, :], ALU.add)
                    if t < NT - 1:
                        then(i)
                i.then_inc(masked, 1)
                dve.wait_ge(counted, 1)
                cum = pc[:, 0:NT * NEXP].rearrange("p (t e) -> p t e", e=NEXP)
                ts(val[:, 0, :, :], cum, float(CAP), float(FULL), ALU.is_gt, ALU.mult)
                ts(val[:, 1, :, :], cum, float(CAP), None, ALU.min)
                then(ts(val[:, 2, :, :], cum, float(CAP), None, ALU.is_le))
                then(tt(val[:, 0, :, :], val[:, 0, :, :], cum, ALU.add))
                tt(val[:, 2, :, :], val[:, 2, :, :], g[:, :, :], ALU.mult)
                tt(val[:, 0, :, :], val[:, 0, :, :], base[:, :, :], ALU.add)
                then(tt(val[:, 1, :, :], val[:, 1, :, :], base[:, :, :], ALU.add))
                for c in range(2):
                    for v in range(3):
                        i = tt(pick[:, c, v, :, :], val[:, v, :, :], hot[:, c, :, :], ALU.mult)
                then(i)
                for c in range(2):
                    for v in range(2):
                        i = nc.vector.tensor_reduce(got_f[:, c, v, :], pick[:, c, v, :, :], AX.X, ALU.add)
                    nc.vector.tensor_reduce(gates[:, c, :], pick[:, c, 2, :, :], AX.X, ALU.add)
                then(i)
                nc.vector.tensor_copy(slots[:, :, :, :], got_f[:, :, :, :]).then_inc(indexed, 1)
        nm.clear()


def experts(nc, d, y_sb, ident, vecs, xs, ys, slots, gates, came):
    NE = 4
    ST = CAP // P
    with ExitStack() as es:
        nm = Names(nc, es, "ex")
        w1 = [nm.sb(f"w1_{i}", [P, DH, FF]) for i in range(NE)]
        w2 = [nm.sb(f"w2_{i}", [P, FC, D]) for i in range(NE)]
        b1 = [nm.sb(f"b1_{i}", [P, FC]) for i in range(NE)]
        b2 = [nm.sb(f"b2_{i}", [P, D]) for i in range(NE)]
        xr = [nm.sb(f"xr{i}", [P, ST, D]) for i in range(2)]
        xT = [nm.sb(f"xT{i}", [P, DH, CAP]) for i in range(2)]
        hm = [nm.sb(f"hm{i}", [P, FC, CAP]) for i in range(2)]
        yr = nm.sb("yr", [P, 2, ST, D])
        pt = [nm.ps(f"t{i}", [P, CAP]) for i in range(2)]
        pu = [nm.ps(f"up{i}", [P, CAP]) for i in range(4)]
        pd = [nm.ps(f"dn{i}", [P, 512]) for i in range(2)]
        got = [nm.sem(f"got{i}") for i in range(NE)]
        rows = [nm.sem(f"rows{i}") for i in range(2)]
        turned, kept = nm.sem("turned"), nm.sem("kept")
        up, gelued, down, summed = nm.sem("up"), nm.sem("gelued"), nm.sem("down"), nm.sem("summed")
        stored = [nm.sem(f"stored{i}") for i in range(2)]
        with nc.Fori(0, NEXP // NE) as turn:
            with nc.Block() as block:
                @block.sync
                def _(sp):
                    def load_rows(i):
                        if i >= 2:
                            sp.wait_ge(turned, DH * (i - 1))
                        sp.dma_start(xr[i % 2][:, :, :], xs[bass.ds((turn * NE + i) * CAP, CAP), :].rearrange(
                            "(t p) k -> p t k", p=P)).then_inc(rows[i % 2], 16)

                    load_rows(0)
                    for i in range(NE):
                        ex = turn * NE + i
                        sp.dma_start(w1[i][:, :, :], d["L0_ffn_W1"][bass.ds(ex, 1)].rearrange(
                            "o (h p) n -> p (o h) n", p=P)).then_inc(got[i], 16)
                        sp.dma_start(b1[i][:, :], d["b1_epc"][bass.ds(ex, 1)].rearrange(
                            "o p c -> p (o c)", p=P)).then_inc(got[i], 16)
                        if i == 0:
                            load_rows(1)
                    for i in range(2, NE):
                        load_rows(i)
                    for i in range(NE):
                        sp.wait_ge(summed, (i + 1) * ST)
                        sp.dma_start(ys[bass.ds((turn * NE + i) * CAP, CAP), :].rearrange("(t p) k -> p t k", p=P),
                                       yr[:, i % 2, :, :]).then_inc(stored[i % 2], 16)
                    for i in range(2):
                        sp.wait_ge(stored[i], 16 * NE // 2)


                @block.scalar
                def _(act):
                    for i in range(NE):
                        ex = turn * NE + i
                        act.dma_start(w2[i][:, :, :], d["L0_ffn_W2"][bass.ds(ex, 1)].rearrange(
                            "o (c p) n -> p (o c) n", p=P)).then_inc(got[i], 16)
                        src = d["L0_ffn_b2"][bass.ds(ex, 1), :].rearrange("o n -> (o n)").partition_broadcast(P)
                        act.dma_start(b2[i][:, :], src).then_inc(got[i], 16)
                    for i in range(NE):
                        act.wait_ge(got[i], 64)
                        if i >= 2:
                            act.wait_ge(down, (i - 1) * ST)
                        for c in range(FC):
                            k = i * FC + c
                            act.wait_ge(up, k + 1)
                            nc.scalar.activation(hm[i % 2][:, c, :], pu[k % 4][:, :], ACT.Gelu,
                                                 bias=b1[i][:, c:c + 1]).then_inc(gelued, 1)

                @block.tensor
                def _(pe):
                    def turns(i):
                        pe.wait_ge(rows[i % 2], 16 * (i // 2 + 1))
                        for h in range(DH):
                            if i >= 1:
                                pe.wait_ge(kept, DH * (i - 1) + h + 1)
                            for t in range(ST):
                                last = nc.tensor.transpose(pt[h][:, t * P:(t + 1) * P],
                                                           xr[i % 2][:, t, h * P:(h + 1) * P], ident[:, :])
                            last.then_inc(turned, 1)

                    def ups(i):
                        pe.wait_ge(kept, DH * (i + 1))
                        pe.wait_ge(got[i], 64)
                        for c in range(FC):
                            k = i * FC + c
                            if k >= 4:
                                pe.wait_ge(gelued, k - 3)
                            for h in range(DH):
                                last = nc.tensor.matmul(pu[k % 4][:, :], w1[i][:, h, c * P:(c + 1) * P],
                                                        xT[i % 2][:, h, :], start=(h == 0), stop=(h == DH - 1))
                            last.then_inc(up, 1)

                    def downs(i):
                        pe.wait_ge(gelued, (i + 1) * FC)
                        for t in range(ST):
                            k = i * ST + t
                            if k >= 2:
                                pe.wait_ge(summed, k - 1)
                            for c in range(FC):
                                last = nc.tensor.matmul(pd[k % 2][:, 0:D], hm[i % 2][:, c, t * P:(t + 1) * P],
                                                        w2[i][:, c, :], start=(c == 0), stop=(c == FC - 1))
                            last.then_inc(down, 1)

                    turns(0)
                    for i in range(NE):
                        ups(i)
                        if i + 1 < NE:
                            turns(i + 1)
                        if i:
                            downs(i - 1)
                    downs(NE - 1)

                @block.vector
                def _(dve):
                    def keep(i):
                        for h in range(DH):
                            dve.wait_ge(turned, DH * i + h + 1)
                            if i >= 2:
                                dve.wait_ge(up, (i - 1) * FC)
                            nc.vector.tensor_scalar(xT[i % 2][:, h, :], pt[h][:, :], vecs[:, 0, h:h + 1],
                                                    vecs[:, 1, h:h + 1], ALU.mult, ALU.add).then_inc(kept, 1)

                    def sums(i):
                        for t in range(ST):
                            k = i * ST + t
                            dve.wait_ge(down, k + 1)
                            if i >= 2 and t == 0:
                                dve.wait_ge(stored[i % 2], 16 * (i // 2))
                            nc.vector.tensor_tensor(yr[:, i % 2, t, :], pd[k % 2][:, 0:D], b2[i][:, :],
                                                    ALU.add).then_inc(summed, 1)

                    dve.wait_ge(got[0], 64)
                    keep(0)
                    for i in range(NE):
                        if i + 1 < NE:
                            keep(i + 1)
                        if i:
                            sums(i - 1)
                    for j in range(1, NE):
                        dve.wait_ge(got[j], 64)
                    sums(NE - 1)
            nm.clear()
    with ExitStack() as es:
        nm = Names(nc, es, "gb")
        NR = len(came)
        back = nm.sb("back", [P, NR, D])
        added = nm.sem("added")
        units = [(t, c) for c in range(2) for t in range(NT)]
        with nc.Block() as block:
            @block.gpsimd
            def _(pool):
                for n, (t, c) in enumerate(units):
                    if n >= NR:
                        pool.wait_ge(added, n - NR + 1)
                    nc.gpsimd.indirect_dma_start(back[:, n % NR, :], None, ys[:, :],
                                                 bass.IndirectOffsetOnAxis(slots[:, c, 1, t:t + 1], 0),
                                                 bounds_check=NEXP * CAP - 1,
                                                 oob_is_err=False).then_inc(came[n % NR], 16)

            @block.vector
            def _(dve):
                for n, (t, c) in enumerate(units):
                    dve.wait_ge(came[n % NR], 16 * (n // NR + 1))
                    if n >= NT:
                        dve.wait_ge(added, n - NT + 1)
                    nc.vector.scalar_tensor_tensor(y_sb[:, t, :], back[:, n % NR, :], gates[:, c, t:t + 1],
                                                   y_sb[:, t, :], ALU.mult, ALU.add).then_inc(added, 1)
        nm.clear()


def gated_add(nc, d, name, layer, x_sb, y_sb):
    with ExitStack() as es:
        nm = Names(nc, es, f"ga_{name}{layer}")
        gate = nm.sb("gate", [P, 2])
        got, gated = nm.sem("got"), nm.sem("gated")
        with nc.Block() as block:
            @block.sync
            def _(sp):
                sp.dma_start(gate[:], ap_of(d[name], 0, [[0, P], [1, 2]])).then_inc(got, 16)

            @block.scalar
            def _(act):
                act.wait_ge(got, 16)
                nc.scalar.activation(gate[:], gate[:], ACT.Tanh).then_inc(gated, 1)

            @block.vector
            def _(dve):
                dve.wait_ge(gated, 1)
                nc.vector.scalar_tensor_tensor(x_sb[:, :, :], y_sb[:, :, :], gate[:, layer:layer + 1], x_sb[:, :, :],
                                               ALU.mult, ALU.add)


def moe(nc, d, x_sb, y_sb, ident, sent, came):
    xs = nc.dram_tensor("expert_in", [NEXP * CAP, D], F32).ap()
    ys = nc.dram_tensor("expert_out", [NEXP * CAP, D], F32).ap()
    with ExitStack() as es:
        slots = es.enter_context(nc.sbuf_tensor("moe_slots", [P, 2, 2, NT], U32))
        gates = es.enter_context(nc.sbuf_tensor("moe_gates", [P, 2, NT], F32))
        vecs = es.enter_context(nc.sbuf_tensor("moe_vecs", [P, 2, DH], F32))
        with ExitStack() as es1:
            h2T = es1.enter_context(nc.sbuf_tensor("moe_hT", [P, DH, B * S], F32))
            got = es1.enter_context(nc.semaphore("moe_got"))
            with nc.Block() as block:
                @block.sync
                def _(sp):
                    for i, n in enumerate(("L0_ffn_ln2_g", "L0_ffn_ln2_b")):
                        for h in range(DH):
                            sp.dma_start(vecs[:, i, h:h + 1],
                                         d[n][h * P:(h + 1) * P].rearrange("(p o) -> p o", o=1)).then_inc(got, 16)
                    sp.wait_ge(got, 64)
            hn = es1.enter_context(nc.sbuf_tensor("moe_hn", [P, NT, D], F32))
            layer_norm(nc, es1, y_sb, hn, "lnm")
            transpose_tokens(nc, es1, hn, lambda g, h: h2T[:, h, g * 512:(g + 1) * 512], ident, "mT",
                             scale=vecs[:, 0, :], bias=vecs[:, 1, :])
            route(nc, d, h2T, hn, xs, slots, gates, sent)
        experts(nc, d, y_sb, ident, vecs, xs, ys, slots, gates, came)
    gated_add(nc, d, "g_ffn", 0, x_sb, y_sb)


def cross_attention(nc, d, x_sb, ident, identb, ctxT):
    with ExitStack() as es:
        hT = es.enter_context(nc.sbuf_tensor("xa_hT", [P, DH, B * S], F32))
        w = {n: es.enter_context(nc.sbuf_tensor(f"xa_{n}", [P, DH, D], F32)) for n in ("wqT", "wkT", "wvT", "woT")}
        gate = es.enter_context(nc.sbuf_tensor("xa_gate", [P, 2], F32))
        got, gated = es.enter_context(nc.semaphore("xa_got")), es.enter_context(nc.semaphore("xa_gated"))
        with nc.Block() as block:
            @block.sync
            def _(sp):
                for n, t in w.items():
                    sp.dma_start(t[:], d[n].rearrange("(h p) n -> p h n", p=P)).then_inc(got, 16)
                sp.dma_start(gate[:], ap_of(d["g_xattn"], 0, [[0, P], [1, 2]])).then_inc(got, 16)
                sp.wait_ge(got, 80)

            @block.scalar
            def _(act):
                act.wait_ge(got, 80)
                nc.scalar.activation(gate[:], gate[:], ACT.Tanh)
        with ExitStack() as es1:
            xn = es1.enter_context(nc.sbuf_tensor("xa_xn", [P, NT, D], F32))
            layer_norm(nc, es1, x_sb, xn, "xa")
            transpose_tokens(nc, es1, xn, lambda g, h: hT[:, h, g * 512:(g + 1) * 512], ident, "xaT")
        sb = Names(nc, es, "xa")
        qT = sb.sb("qT", [STK + MAXR, NH, S], BF16)
        kT = sb.sb("kT", [STK + MAXR, NH, SK], BF16)
        vt = sb.sb("vt", [P, KT, NH, VW])
        bias_q = sb.sb("bias_q", [P, QT, SK], BF16)
        bias_k = sb.sb("bias_k", [P, KT, S], BF16)
        attn = sb.sb("attn", [P, QT, D])
        with nc.Block() as block:
            @block.vector
            def _(dve):
                nc.vector.memset(kT[STK:STK + MAXR, :, :], 1.0)
                nc.vector.memset(vt[:, :, :, HD:HD + 1], 1.0)
                nc.vector.memset(vt[:, :, :, HD + 1:VW], 0.0)
        with nc.Fori(0, B) as b:
            with ExitStack() as e0:
                mask = e0.enter_context(nc.sbuf_tensor("xa_mask", [P, QT, SK], I32))
                nm = Names(nc, e0, "xam")
                pm = [nm.ps(f"mt{i}", [P, 1024], BF16) for i in range(2)]
                mgot, biased, turned, kept = nm.sem("got"), nm.sem("biased"), nm.sem("turned"), nm.sem("kept")
                with nc.Block() as block:
                    @block.sync
                    def _(sp):
                        sp.dma_start(mask[:, :, :], d["mask_BxSxS2_ik0"][bass.ds(b, 1)].rearrange(
                            "o (t p) k -> p (o t) k", p=P)).then_inc(mgot, 16)

                    @block.vector
                    def _(dve):
                        dve.wait_ge(mgot, 16)
                        for t in range(QT):
                            nc.vector.tensor_scalar(bias_q[:, t, :], mask[:, t, :], 0.0, NEG, ALU.is_equal,
                                                    ALU.mult).then_inc(biased, 1)

                    @block.tensor
                    def _(pe):
                        pe.wait_ge(biased, QT)
                        for n in range(KT // 2):
                            if n >= 2:
                                pe.wait_ge(kept, n - 1)
                            for i in range(2):
                                for t in range(QT):
                                    kt = 2 * n + i
                                    last = nc.tensor.transpose(pm[n % 2][:, (i * QT + t) * P:(i * QT + t + 1) * P],
                                                               bias_q[:, t, kt * P:(kt + 1) * P], identb[:, :])
                            last.then_inc(turned, 1)

                    @block.scalar
                    def _(act):
                        for n in range(KT // 2):
                            act.wait_ge(turned, n + 1)
                            nc.scalar.copy(bias_k[:, 2 * n:2 * n + 2, :],
                                           pm[n % 2][:, :].rearrange("p (i s) -> p i s", i=2)).then_inc(kept, 1)
                nm.clear()
            with ExitStack() as e0:
                q = e0.enter_context(nc.sbuf_tensor("xa_q", [P, QT, D], F32))
                k = e0.enter_context(nc.sbuf_tensor("xa_k", [P, KT, D], F32))
                with ExitStack() as e1:
                    nm = Names(nc, e1, "xap")
                    hTb = nm.sb("hTb", [P, DH, S])
                    cTb = nm.sb("cTb", [P, DH, SK])

                    def lhs(t, src):
                        return [src[:, h, t * P:(t + 1) * P] for h in range(DH)]

                    def whole(ps):
                        return ps[:, 0:D]
                    jobs = [(q[:, t, :], lhs(t, hTb), [w["wqT"][:, h, :] for h in range(DH)], whole) for t in range(QT)]
                    for t in range(KT):
                        jobs.append((k[:, t, :], lhs(t, cTb), [w["wkT"][:, h, :] for h in range(DH)], whole))
                        jobs.append((vt[:, t, :, 0:HD], lhs(t, cTb), [w["wvT"][:, h, :] for h in range(DH)],
                                     lambda ps: ps[:, 0:D].rearrange("p (h e) -> p h e", h=NH)))
                    cv = ctxT[:, :, :, :].rearrange("p b h s -> p (b h) s")
                    project_tokens(nc, nm, jobs)([(hTb[:, :, :], hT[:, :, bass.ds(b * S, S)]),
                                                  (cTb[:, :, :], cv[:, bass.ds(b * DH, DH), 0:SK])])
                    nm.clear()
                with ExitStack() as e1:
                    nm = Names(nc, e1, "xas")
                    stk = [nm.sb(f"stk{i}", [P, QT * NH, STK], BF16) for i in range(2)]
                    rest = nm.sb("rest", [P, QT * NH, HD])
                    v = [s[:, :, :].rearrange("p (t h) e -> p t h e", t=QT) for s in stk]

                    def heads(x, t0):
                        return x[:, t0:t0 + QT, :].rearrange("p t (h e) -> p (t h) e", h=NH)
                    split_stacks(nc, nm, [(heads(q, 0), stk[0], Q_SLOTS, float(HD) ** 0.5, rest[:, :, :]),
                                          (heads(k, 0), stk[1], K_SLOTS, 1.0, rest[:, :, :])])
                    turn_stacks(nc, nm, identb, [(v[0], QT, qT), (v[1], QT, kT[:, :, 0:S])])
                    nm.clear()
                with ExitStack() as e1:
                    nm = Names(nc, e1, "xau")
                    stk = nm.sb("stk", [P, QT * NH, STK], BF16)
                    rest = nm.sb("rest", [P, QT * NH, HD])
                    split_stacks(nc, nm, [(heads(k, QT), stk, K_SLOTS, 1.0, rest[:, :, :])])
                    turn_stacks(nc, nm, identb, [(stk[:, :, :].rearrange("p (t h) e -> p t h e", t=QT), QT,
                                                  kT[:, :, S:SK])])
                    nm.clear()
            with ExitStack() as e1:
                nm = Names(nc, e1, "xaa")
                attend(nc, nm, ident, identb, qT, kT, vt, attn, SK, False,
                       lambda qt, f: bias_q[:, qt, f * 512:(f + 1) * 512], lambda kt: bias_k[:, kt, :])
                nm.clear()
            with ExitStack() as e1:
                nm = Names(nc, e1, "xao")

                def add(t, prod):
                    x = x_sb[:, bass.ds(b * QT + t, 1), :].rearrange("p o d -> p (o d)")
                    return nc.vector.scalar_tensor_tensor(x, prod, gate[:, 1:2], x, ALU.mult, ALU.add)
                project_out(nc, nm, ident, attn, w["woT"], add)
                nm.clear()


FI = 704
QB = 16
FPAD = -(-FI // P)
STEPS_HALF, STEPS_ONE, STEP_TWO = (0.25, 0.75, 1.25, 1.75), (2.5, 3.5), 5.0


def quantize(nc, nm, jobs, width):
    n_blk = width // QB
    amax = nm.sb("amax", [P, 2, n_blk])
    inv = nm.sb("inv", [P, 2, n_blk])
    v = nm.sb("v", [P, 2, width])
    sgn = nm.sb("sgn", [P, 2, width])
    hi = nm.sb("hi", [P, 2, width])
    lo = nm.sb("lo", [P, 2, width])
    maxed, scaled, inverted, divided = nm.sem("maxed"), nm.sem("scaled"), nm.sem("inverted"), nm.sem("divided")
    signed, absed, step, graded, done = nm.sem("signed"), nm.sem("absed"), nm.sem("step"), nm.sem("graded"), nm.sem("done")
    sscaled = nm.sem("sscaled")

    def blocks(ap):
        return ap.rearrange("p (n e) -> p n e", e=QB)

    def wide(t, r, i):
        a = t[0:r, i, :]
        return ap_of(a, 0, [a.ap[0], [1, n_blk], [0, QB]])

    with nc.Block() as block:
        @block.vector
        def _(dve):
            count = [0]

            def then(i):
                count[0] += 1
                i.then_inc(step, 1)
                dve.wait_ge(step, count[0])

            def scale(n):
                src, dst = jobs[n]
                r, i = src.shape[0], n % 2
                if n >= 2:
                    dve.wait_ge(done, n - 1)
                then(nc.vector.tensor_reduce(amax[0:r, i, :], blocks(src), AX.X, ALU.max,
                                             apply_absolute_value=True))
                nc.vector.tensor_scalar(amax[0:r, i, :], amax[0:r, i, :], 1.0 / 6.0, 1e-12, ALU.mult,
                                        ALU.max).then_inc(scaled, 1)
                dve.wait_ge(scaled, n + 1)
                nc.vector.reciprocal(inv[0:r, i, :], amax[0:r, i, :]).then_inc(inverted, 1)

            def grade(n):
                src, dst = jobs[n]
                r, i = src.shape[0], n % 2
                a, h, l = v[0:r, i, :], hi[0:r, i, :], lo[0:r, i, :]
                dve.wait_ge(absed, n + 1)
                stt, ts = nc.vector.scalar_tensor_tensor, nc.vector.tensor_scalar
                ts(h, a, STEP_TWO, 2.0, ALU.is_gt, ALU.mult)
                then(ts(l, a, STEPS_HALF[0], None, ALU.is_gt))
                stt(h, a, STEPS_ONE[0], h, ALU.is_gt, ALU.add)
                then(stt(l, a, STEPS_HALF[1], l, ALU.is_gt, ALU.add))
                stt(h, a, STEPS_ONE[1], h, ALU.is_gt, ALU.add)
                then(stt(l, a, STEPS_HALF[2], l, ALU.is_gt, ALU.add))
                then(stt(l, a, STEPS_HALF[3], l, ALU.is_gt, ALU.add))
                stt(h, l, 0.5, h, ALU.mult, ALU.add).then_inc(graded, 1)

            scale(0)
            for n in range(len(jobs)):
                if n + 1 < len(jobs):
                    scale(n + 1)
                grade(n)

        @block.scalar
        def _(act):
            for n, (src, dst) in enumerate(jobs):
                r, i = src.shape[0], n % 2
                if n >= 2:
                    act.wait_ge(done, n - 1)
                nc.scalar.activation(sgn[0:r, i, :], src, ACT.Sign).then_inc(signed, 1)
                act.wait_ge(divided, n + 1)
                nc.scalar.activation(v[0:r, i, :], v[0:r, i, :], ACT.Abs).then_inc(absed, 1)

        @block.gpsimd
        def _(pool):
            def divide(n):
                src, dst = jobs[n]
                r, i = src.shape[0], n % 2
                pool.wait_ge(inverted, n + 1)
                nc.gpsimd.tensor_tensor(blocks(v[0:r, i, :]), blocks(src), wide(inv, r, i), ALU.mult).then_inc(divided, 1)
                pool.wait_ge(signed, n + 1)
                nc.gpsimd.tensor_tensor(blocks(sgn[0:r, i, :]), blocks(sgn[0:r, i, :]), wide(amax, r, i),
                                        ALU.mult).then_inc(sscaled, 1)

            divide(0)
            for n, (src, dst) in enumerate(jobs):
                r, i = src.shape[0], n % 2
                if n + 1 < len(jobs):
                    divide(n + 1)
                pool.wait_ge(graded, n + 1)
                pool.wait_ge(sscaled, n + 1)
                nc.gpsimd.tensor_tensor(dst, hi[0:r, i, :], sgn[0:r, i, :], ALU.mult).then_inc(done, 1)


def turn_rows(nc, nm, ident, jobs):
    ps = [nm.ps(f"tr{i}", [P, 512]) for i in range(4)]
    turned, kept = nm.sem("tr_turned"), [nm.sem("tr_kept0"), nm.sem("tr_kept1")]
    with nc.Block() as block:
        @block.tensor
        def _(pe):
            for n, (src, dst) in enumerate(jobs):
                r, c = src.shape
                if n >= 4:
                    pe.wait_ge(kept[n % 2], (n - 4) // 2 + 1)
                nc.tensor.transpose(ps[n % 4][0:c, 0:r], src, ident[0:r, 0:r]).then_inc(turned, 1)

        def copies(eng, parity, copy):
            for n, (src, dst) in enumerate(jobs):
                r, c = src.shape
                if n % 2 == parity:
                    eng.wait_ge(turned, n + 1)
                    copy(dst, ps[n % 4][0:c, 0:r]).then_inc(kept[parity], 1)

        @block.vector
        def _(dve):
            copies(dve, 0, nc.vector.tensor_copy)

        @block.scalar
        def _(act):
            copies(act, 1, nc.scalar.copy)


def fp4_ffn(nc, d, x_sb, ident):
    with ExitStack() as es:
        wgu = es.enter_context(nc.sbuf_tensor("ff_wguT", [P, DH, 2, FI], F32))
        wd = es.enter_context(nc.sbuf_tensor("ff_wdT", [P, FPAD, D], F32))
        xqT = es.enter_context(nc.sbuf_tensor("ff_xqT", [P, DH, B * S], F32))
        gate = es.enter_context(nc.sbuf_tensor("ff_gate", [P, 2], F32))
        with ExitStack() as e1:
            nm = Names(nc, e1, "ffw")
            wr = nm.sb("rows", [P, 2, FPAD, D])
            wq = nm.sb("rowsq", [P, 2, FPAD, D])
            dr = nm.sb("down", [P, DH, FI])
            dq = nm.sb("downq", [P, DH, FI])
            got = nm.sem("got")
            last_rows = FI - (FPAD - 1) * P
            with nc.Block() as block:
                @block.sync
                def _(sp):
                    for i, n in enumerate(("L1_ffn_w_gate", "L1_ffn_w_up")):
                        full = (FPAD - 1) * P
                        sp.dma_start(wr[:, i, 0:FPAD - 1, :],
                                     d[n][0:full, :].rearrange("(c p) k -> p c k", p=P)).then_inc(got, 16)
                        sp.dma_start(wr[0:last_rows, i, FPAD - 1, :], d[n][full:FI, :]).then_inc(got, 16)
                    sp.dma_start(dr[:], d["L1_ffn_w_down"].rearrange("(h p) k -> p h k", p=P)).then_inc(got, 16)
                    sp.dma_start(gate[:], ap_of(d["g_ffn"], 0, [[0, P], [1, 2]])).then_inc(got, 16)
                    sp.wait_ge(got, 96)

                @block.scalar
                def _(act):
                    act.wait_ge(got, 96)
                    nc.scalar.activation(gate[:], gate[:], ACT.Tanh)
            with ExitStack() as e2:
                nq = Names(nc, e2, "ffq1")
                jobs = []
                for i in range(2):
                    for c in range(FPAD):
                        r = P if c < FPAD - 1 else last_rows
                        jobs.append((wr[0:r, i, c, :], wq[0:r, i, c, :]))
                quantize(nc, nq, jobs, D)
            with ExitStack() as e2:
                nq = Names(nc, e2, "ffq2")
                quantize(nc, nq, [(dr[:, h, :], dq[:, h, :]) for h in range(DH)], FI)
            jobs = []
            for i in range(2):
                for c in range(FPAD):
                    r = P if c < FPAD - 1 else last_rows
                    for h in range(DH):
                        jobs.append((wq[0:r, i, c, h * P:(h + 1) * P], wgu[:, h, i, c * P:c * P + r]))
            for c in range(FPAD):
                r = P if c < FPAD - 1 else last_rows
                for h in range(DH):
                    jobs.append((dq[:, h, c * P:c * P + r], wd[0:r, c, h * P:(h + 1) * P]))
            turn_rows(nc, nm, ident, jobs)
        with ExitStack() as e1:
            xn = e1.enter_context(nc.sbuf_tensor("ff_xn", [P, NT, D], F32))
            layer_norm(nc, e1, x_sb, xn, "ff")
            nm = Names(nc, e1, "ffx")
            quantize(nc, nm, [(xn[:, 4 * g:4 * g + 4, :].rearrange("p t d -> p (t d)"),
                               xn[:, 4 * g:4 * g + 4, :].rearrange("p t d -> p (t d)")) for g in range(NT // 4)], 4 * D)
            transpose_tokens(nc, e1, xn, lambda g, h: xqT[:, h, g * 512:(g + 1) * 512], ident, "ffT")
        with nc.Fori(0, B) as b, ExitStack() as e0:
            hid = e0.enter_context(nc.sbuf_tensor("ff_hid", [P, QT, FI], F32))
            hq = e0.enter_context(nc.sbuf_tensor("ff_hq", [P, QT, FI], F32))
            with ExitStack() as e1:
                nm = Names(nc, e1, "ffg")
                xb = nm.sb("xb", [P, DH, S])
                sg = nm.sb("sg", [P, 2, FI])
                HALF = FI // 2
                pg = [nm.ps(f"g{i}", [P, 512]) for i in range(4)]
                pu = [nm.ps(f"u{i}", [P, 512]) for i in range(4)]
                static, prod, silued, mixed = nm.sem("static"), nm.sem("prod"), nm.sem("silued"), nm.sem("mixed")
                units = [(t, f) for t in range(QT) for f in range(2)]
                with nc.Block() as block:
                    @block.tensor
                    def _(pe):
                        pe.wait_ge(static, 1)
                        for n, (t, f) in enumerate(units):
                            if n >= 4:
                                pe.wait_ge(mixed, n - 3)
                            for i, ps in enumerate((pg, pu)):
                                for h in range(DH):
                                    last = nc.tensor.matmul(ps[n % 4][:, 0:HALF], xb[:, h, t * P:(t + 1) * P],
                                                            wgu[:, h, i, f * HALF:(f + 1) * HALF], start=(h == 0),
                                                            stop=(h == DH - 1))
                            last.then_inc(prod, 1)

                    @block.scalar
                    def _(act):
                        nc.scalar.copy(xb[:, :, :], xqT[:, :, bass.ds(b * S, S)]).then_inc(static, 1)
                        for n, (t, f) in enumerate(units):
                            act.wait_ge(prod, n + 1)
                            if n >= 4:
                                act.wait_ge(mixed, n - 3)
                            nc.scalar.activation(sg[:, (n // 2) % 2, f * HALF:(f + 1) * HALF], pg[n % 4][:, 0:HALF],
                                                 ACT.Silu).then_inc(silued, 1)

                    @block.vector
                    def _(dve):
                        for n, (t, f) in enumerate(units):
                            dve.wait_ge(silued, n + 1)
                            nc.vector.tensor_tensor(hid[:, t, f * HALF:(f + 1) * HALF], pu[n % 4][:, 0:HALF],
                                                    sg[:, (n // 2) % 2, f * HALF:(f + 1) * HALF],
                                                    ALU.mult).then_inc(mixed, 1)
                nm.clear()
            with ExitStack() as e1:
                nm = Names(nc, e1, "ffh")
                quantize(nc, nm, [(hid[:, t, :], hq[:, t, :]) for t in range(QT)], FI)
                nm.clear()
            with ExitStack() as e1:
                nm = Names(nc, e1, "ffd")
                hqT = nm.sb("hqT", [P, 2, FPAD, P])
                pt = [nm.ps(f"t{i}", [P, 1024]) for i in range(2)]
                py = [nm.ps(f"y{i}", [P, 512]) for i in range(2)]
                turned, kept, down, added = nm.sem("turned"), nm.sem("kept"), nm.sem("down"), nm.sem("added")
                last_rows = FI - (FPAD - 1) * P
                with nc.Block() as block:
                    @block.tensor
                    def _(pe):
                        def turn(t):
                            if t >= 2:
                                pe.wait_ge(kept, 2 * (t - 1))
                            for c in range(FPAD):
                                r = P if c < FPAD - 1 else last_rows
                                last = nc.tensor.transpose(pt[t % 2][0:r, c * P:(c + 1) * P], hq[:, t, c * P:c * P + r],
                                                           ident[:, :])
                            last.then_inc(turned, 1)

                        def product(t):
                            pe.wait_ge(kept, 2 * (t + 1))
                            if t >= 2:
                                pe.wait_ge(added, t - 1)
                            for c in range(FPAD):
                                r = P if c < FPAD - 1 else last_rows
                                last = nc.tensor.matmul(py[t % 2][:, 0:D], hqT[0:r, t % 2, c, :], wd[0:r, c, :],
                                                        start=(c == 0), stop=(c == FPAD - 1))
                            last.then_inc(down, 1)

                        turn(0)
                        for t in range(1, QT):
                            turn(t)
                            product(t - 1)
                        product(QT - 1)

                    @block.scalar
                    def _(act):
                        for t in range(QT):
                            act.wait_ge(turned, t + 1)
                            if t >= 2:
                                act.wait_ge(down, t - 1)
                            n = FPAD - 1
                            nc.scalar.copy(hqT[:, t % 2, 0:n, :],
                                           pt[t % 2][:, 0:n * P].rearrange("p (c s) -> p c s", s=P)).then_inc(kept, 1)
                            nc.scalar.copy(hqT[0:last_rows, t % 2, n, :],
                                           pt[t % 2][0:last_rows, n * P:(n + 1) * P]).then_inc(kept, 1)

                    @block.vector
                    def _(dve):
                        for t in range(QT):
                            dve.wait_ge(down, t + 1)
                            x = x_sb[:, bass.ds(b * QT + t, 1), :].rearrange("p o d -> p (o d)")
                            nc.vector.scalar_tensor_tensor(x, py[t % 2][:, 0:D], gate[:, 1:2], x, ALU.mult,
                                                           ALU.add).then_inc(added, 1)
                nm.clear()


def layouts(a):
    return {
        "b1_epc": np.ascontiguousarray(np.asarray(a["L0_ffn_b1"]).reshape(NEXP, FC, P).transpose(0, 2, 1)),
        "wqT": np.ascontiguousarray(np.asarray(a["L1_xattn_Wq"]).T),
        "wkT": np.ascontiguousarray(np.asarray(a["L1_xattn_Wk"]).T),
        "wvT": np.ascontiguousarray(np.asarray(a["L1_xattn_Wv"]).T),
        "woT": np.ascontiguousarray(np.asarray(a["L1_xattn_Wo"]).T),
    }


def bf16_bits(a):
    return np.ascontiguousarray((np.ascontiguousarray(a, np.float32).view(np.uint32) >> 16).astype(np.uint16))


def constants():
    c = {}
    c["c_ident"] = np.eye(P, dtype=np.float32)
    ones2 = np.zeros((P, 2, 2), np.float32)
    ones2[:, 0, 0] = 1
    ones2[:, 1, 1] = 1
    c["c_ones2"] = ones2
    c["c_add2"] = np.array([[0, 1], [1, 0]], np.float32)
    corner = np.full((P, PITCH), FAR, np.float32)
    corner[::NBLK, 0] = 0
    c["c_corner"] = corner
    inner = np.ones((P, 1), np.float32)
    inner[::NBLK] = 0
    c["c_inner"] = inner
    seed = np.zeros((P, 2 * RB + 2), np.float32)
    seed[NBLK - 1::NBLK, -1] = 1
    c["c_seed"] = bf16_bits(seed)
    c["c_identb"] = bf16_bits(np.eye(P, dtype=np.float32))
    inv = 1.0 / 10000.0 ** (np.arange(0, HD, 2, dtype=np.float32) / np.float32(HD))
    ang = np.arange(S, dtype=np.float32)[:, None] * inv.astype(np.float32)
    tab = np.stack([np.sin(ang), np.cos(ang)]).astype(np.float32)
    tab = tab.reshape(2, QT, P, 1, HD // 2).transpose(2, 0, 1, 3, 4)
    c["c_rope"] = np.ascontiguousarray(np.broadcast_to(tab, (P, 2, QT, NH, HD // 2)).reshape(P, 2, QT * NH, HD // 2))
    tri = np.where(np.arange(P)[None, :] <= np.arange(P)[:, None], 0, NEG).astype(np.float32)
    c["c_tri_q"] = bf16_bits(np.concatenate([np.zeros((P, 512 - P), np.float32), tri], 1))
    c["c_tri_k"] = bf16_bits(tri.T)
    c["c_tri"] = np.ascontiguousarray(np.tri(P, dtype=np.float32).T)
    c["c_ones"] = np.ones((P, P), np.float32)
    c["c_base"] = np.ascontiguousarray(np.broadcast_to(np.arange(NEXP, dtype=np.float32) * CAP - 1, (P, NT, NEXP)))
    c["c_rank"] = np.ascontiguousarray(np.broadcast_to(np.arange(NEXP, 0, -1, dtype=np.float32), (P, NT, NEXP)))
    return c


def load_all(nc, d, x_sb, ident, identb, ctxT, x_src):
    with ExitStack() as es:
        ctx_nat = es.enter_context(nc.sbuf_tensor("ctx_nat", [P, B * KT, D], F32))
        came = es.enter_context(nc.semaphore("inputs_came"))
        with nc.Block() as block:
            @block.sync
            def _(sp):
                sp.dma_start(x_sb[:], x_src.rearrange("b (t p) d -> p (b t) d", p=P)).then_inc(came, 16)
                sp.dma_start(ident[:], d["c_ident"]).then_inc(came, 16)
                sp.dma_start(identb[:], d["c_identb"].bitcast(BF16)).then_inc(came, 16)
                sp.wait_ge(came, 64)

            @block.scalar
            def _(act):
                act.dma_start(ctx_nat[:], d["ctx_1024"].rearrange("b (t p) d -> p (b t) d", p=P)).then_inc(came, 16)

            @block.gpsimd
            def _(pool):
                nc.gpsimd.memset(ctxT[:, :, :, SK:PADI], 0.0)
        transpose_tokens(nc, es, ctx_nat, lambda g, h: ctxT[:, g // 2, h, (g % 2) * 512:(g % 2) * 512 + 512],
                         ident, "cT")


def build(nc, d, out, phases=("dtw", "l0", "xa", "ffn")):
    with ExitStack() as es:
        sent = es.enter_context(nc.semaphore("rows_sent"))
        rows_came = es.enter_context(nc.semaphore("ctx_rows_came"))
        came = [es.enter_context(nc.semaphore(f"rows_came{i}")) for i in range(8)]
        x_sb = es.enter_context(nc.sbuf_tensor("x_sb", [P, NT, D], F32))
        ident = es.enter_context(nc.sbuf_tensor("ident", [P, P], F32))
        identb = es.enter_context(nc.sbuf_tensor("identb", [P, P], BF16))
        ctxT = es.enter_context(nc.sbuf_tensor("ctxT", [P, B, DH, PADI], F32))
        load_all(nc, d, x_sb, ident, identb, ctxT, d["x"])
        clear_released(nc)
        if "dtw" in phases:
            dtw_block(nc, d, x_sb, ident, ctxT, rows_came)
            clear_released(nc)
        if "l0" in phases:
            with ExitStack() as es1:
                y_sb = es1.enter_context(nc.sbuf_tensor("y_sb", [P, NT, D], F32))
                self_attention(nc, d, x_sb, y_sb, ident, identb)
                clear_released(nc)
                moe(nc, d, x_sb, y_sb, ident, sent, came)
                clear_released(nc)
        if "xa" in phases:
            cross_attention(nc, d, x_sb, ident, identb, ctxT)
            clear_released(nc)
        if "ffn" in phases:
            fp4_ffn(nc, d, x_sb, ident)
            clear_released(nc)
        stored = es.enter_context(nc.semaphore("out_stored"))
        with nc.Block() as block:
            @block.sync
            def _(sp):
                sp.dma_start(out.rearrange("b (t p) d -> p (b t) d", p=P), x_sb[:]).then_inc(stored, 16)
                sp.wait_ge(stored, 16)


_INS = ("x", "ctx_1024", "mask_BxSxS2_ik0", "g_xattn", "g_ffn", "L0_ffn_ln1_g", "L0_ffn_ln1_b", "L0_ffn_Wqkv",
        "L0_ffn_Wproj", "L0_ffn_ln2_g", "L0_ffn_ln2_b", "L0_ffn_Wgate", "L0_ffn_W1", "L0_ffn_W2", "L0_ffn_b2",
        "L1_ffn_w_gate", "L1_ffn_w_up", "L1_ffn_w_down")


def kernel(**inputs):
    import concourse.bacc as bacc
    from concourse.bass_utils import run_bass_kernel_spmd

    nc = bacc.Bacc("TRN2", target_bir_lowering=False, num_devices=1)
    arrays = {n: np.ascontiguousarray(inputs[n]) for n in _INS}
    arrays.update(layouts(inputs))
    arrays.update(constants())
    d = {n: nc.dram_tensor(n, a.shape, mybir.dt.from_np(a.dtype), kind="ExternalInput").ap()
         for n, a in arrays.items()}
    out = nc.dram_tensor("out", (B, S, D), F32, kind="ExternalOutput").ap()
    build(nc, d, out)
    r = run_bass_kernel_spmd(nc, [arrays], core_ids=[0])
    return r.results[0]["out"]
```

```python
import numpy as np
import concourse.bass as bass
from concourse import mybir
from contextlib import ExitStack

F32, BF16, I32, U32, I8 = mybir.dt.float32, mybir.dt.bfloat16, mybir.dt.int32, mybir.dt.uint32, mybir.dt.int8
ALU, ACT, AX = mybir.AluOpType, mybir.ActivationFunctionType, mybir.AxisListType
P = 128
B, S, D, SK = 4, 512, 256, 1024
QT = S // P
KT = SK // P
NT = B * QT
DH = D // P
NBLK, RB = 32, 33
PADI = NBLK * RB
PITCH = RB + 1
SLOTS = S + NBLK
CH = 16
NCH = SLOTS // CH
ROW = SLOTS * PITCH
FAR = 1e30
FAR2 = 1e34
EPS = 1e-5


def ap_of(t, offset, dims):
    return bass.AP(tensor=t.tensor, offset=t.offset + offset, ap=dims)


def clear_released(nc):
    nums = sorted(set(nc.released_uncleared_semaphores))
    while nums:
        n = 1
        while n < len(nums) and nums[n] == nums[0] + n:
            n += 1
        nc.gpsimd.sem_clear(range(nums[0], nums[0] + n))
        nums = nums[n:]
    nc.all_engine_barrier()


def layer_norm(nc, es, x_sb, out_sb, name):
    stats = es.enter_context(nc.sbuf_tensor(f"{name}_stats", [P, NT, 6], F32))
    mv = es.enter_context(nc.sbuf_tensor(f"{name}_mv", [P, NT, 2], F32))
    std = es.enter_context(nc.sbuf_tensor(f"{name}_std", [P, NT], F32))
    rstd = es.enter_context(nc.sbuf_tensor(f"{name}_rstd", [P, NT], F32))
    stats_done = es.enter_context(nc.semaphore(f"{name}_stats_done"))
    var_done = es.enter_context(nc.semaphore(f"{name}_var_done"))
    std_done = es.enter_context(nc.semaphore(f"{name}_std_done"))
    rstd_done = es.enter_context(nc.semaphore(f"{name}_rstd_done"))
    with nc.Block() as block:
        @block.vector
        def _(dve):
            for t in range(NT):
                nc.vector.bn_stats(stats[:, t, :], x_sb[:, t, :]).then_inc(stats_done, 1)
            for t in range(NT):
                dve.wait_ge(stats_done, t + 1)
                nc.vector.bn_aggr(mv[:, t, :], stats[:, t, :]).then_inc(var_done, 1)
            dve.wait_ge(var_done, NT)
            nc.vector.tensor_scalar(std[:, :], mv[:, :, 1], EPS, None, ALU.add).then_inc(var_done, 1)
            dve.wait_ge(std_done, 1)
            nc.vector.reciprocal(rstd[:, :], std[:, :]).then_inc(rstd_done, 1)
            dve.wait_ge(rstd_done, 1)
            for t in range(NT):
                nc.vector.tensor_scalar(out_sb[:, t, :], x_sb[:, t, :], mv[:, t, 0:1], rstd[:, t:t + 1],
                                        ALU.subtract, ALU.mult)

        @block.scalar
        def _(act):
            act.wait_ge(var_done, NT + 1)
            nc.scalar.activation(std[:, :], std[:, :], ACT.Sqrt).then_inc(std_done, 1)


def transpose_tokens(nc, es, src, dst, ident, name, scale=None, bias=None, mul=1.0):
    ps = [es.enter_context(nc.psum_tensor(f"{name}_ps{i}", [P, 512], F32)) for i in range(2)]
    turned = es.enter_context(nc.semaphore(f"{name}_turned"))
    copied = es.enter_context(nc.semaphore(f"{name}_copied"))
    groups = src.shape[1] // 4
    with nc.Block() as block:
        @block.tensor
        def _(pe):
            for n in range(groups * DH):
                g, h = n // DH, n % DH
                if n >= 2:
                    pe.wait_ge(copied, n - 1)
                for q in range(4):
                    last = nc.tensor.transpose(ps[n % 2][:, q * P:(q + 1) * P],
                                               src[:, 4 * g + q, h * P:(h + 1) * P], ident[:, :])
                last.then_inc(turned, 1)

        @block.vector
        def _(dve):
            for n in range(groups * DH):
                g, h = n // DH, n % DH
                dve.wait_ge(turned, n + 1)
                out = dst(g, h)
                if scale is not None:
                    i = nc.vector.tensor_scalar(out, ps[n % 2][:, :], scale[:, h:h + 1], bias[:, h:h + 1],
                                                ALU.mult, ALU.add)
                else:
                    i = nc.vector.tensor_scalar(out, ps[n % 2][:, :], float(mul), None, ALU.mult)
                i.then_inc(copied, 1)


def tanh_gate(nc, es, g, name):
    gate = es.enter_context(nc.sbuf_tensor(f"{name}_gate", [P, 2], F32))
    got = es.enter_context(nc.semaphore(f"{name}_gate_got"))
    with nc.Block() as block:
        @block.sync
        def _(sp):
            sp.dma_start(gate[:], ap_of(g, 0, [[0, P], [1, 2]])).then_inc(got, 16)

        @block.scalar
        def _(act):
            act.wait_ge(got, 16)
            nc.scalar.activation(gate[:], gate[:], ACT.Tanh)
    return gate


def dtw_block(nc, d, x_sb, ident, ctxT, ctxT_d, rows_came):
    dist = nc.dram_tensor("dist", [P, ROW], F32).ap()
    path = nc.dram_tensor("path", [P, SLOTS * RB], BF16).ap()
    with ExitStack() as es:
        xnT = es.enter_context(nc.sbuf_tensor("xnT", [P, DH, B * S], F32))
        with ExitStack() as es1:
            xn = es1.enter_context(nc.sbuf_tensor("dtw_xn", [P, NT, D], F32))
            layer_norm(nc, es1, x_sb, xn, "ln0")
            transpose_tokens(nc, es1, xn, lambda g, h: xnT[:, h, g * 512:(g + 1) * 512], ident, "xT", mul=-2.0)
        dtw_distances(nc, d, xnT, ctxT, ctxT_d, dist)
    with ExitStack() as es:
        part = [es.enter_context(nc.sbuf_tensor(f"ctx_part{i}", [P, RB, D], BF16)) for i in range(3)]
        ways = [es.enter_context(nc.sbuf_tensor(f"way_{n}", [P, CH + SLOTS + 2, RB], I8))
                for n in ("diag", "up", "left")]
        gate = tanh_gate(nc, es, d["g_xattn"], "dtw")
        dtw_costs(nc, d, dist, ways, part, rows_came)
        backtrack(nc, d, ways, path, part, x_sb, gate)


def dtw_distances(nc, d, xnT, ctxT, ctxT_d, dist):
    with ExitStack() as es:
        sq = es.enter_context(nc.sbuf_tensor("sq", [P, 2, 2, 512], F32))
        ones2 = es.enter_context(nc.sbuf_tensor("ones2", [P, 2, 2], F32))
        add2 = es.enter_context(nc.sbuf_tensor("add2", [2, 2], F32))
        rows_i = es.enter_context(nc.sbuf_tensor("rows_i", [2, B, PADI], F32))
        rows_j = es.enter_context(nc.sbuf_tensor("rows_j", [2, B, S], F32))
        stage = es.enter_context(nc.sbuf_tensor("stage", [P, SLOTS, PITCH], F32))
        ps_n = [es.enter_context(nc.psum_tensor(f"ps_n{i}", [P, 512], F32)) for i in range(2)]
        ps_d = [es.enter_context(nc.psum_tensor(f"ps_d{i}", [P, 512], F32)) for i in range(2)]
        consts = es.enter_context(nc.semaphore("d_consts"))
        squared = es.enter_context(nc.semaphore("squared"))
        normed = es.enter_context(nc.semaphore("normed"))
        norm_kept = es.enter_context(nc.semaphore("norm_kept"))
        prod = es.enter_context(nc.semaphore("d_prod"))
        clipped = es.enter_context(nc.semaphore("d_clipped"))
        rooted = es.enter_context(nc.semaphore("d_rooted"))
        filled = es.enter_context(nc.semaphore("d_filled"))
        stored = es.enter_context(nc.semaphore("d_stored"))
        spilled = es.enter_context(nc.semaphore("d_spilled"))
        jobs = [(0, b, c, 1.0) for b in range(B) for c in range(0, SK, 512)] + [(1, b, 0, 0.25) for b in range(B)]
        with nc.Block() as block:
            def keep_norm(dve, n):
                w, b, c, f = jobs[n]
                if n == 0:
                    dve.wait_ge(consts, 32)
                    dve.wait_ge(filled, 4)
                dve.wait_ge(normed, n + 1)
                dst = rows_j[:, b, :] if w else rows_i[:, b, c:c + 512]
                nc.vector.tensor_scalar(dst, ps_n[n % 2][0:2, :], add2[:, w:w + 1], None,
                                        ALU.add).then_inc(norm_kept, 1)

            @block.sync
            def _(sp):
                sp.dma_start(ones2[:], d["c_ones2"]).then_inc(consts, 16)
                sp.dma_start(add2[:], d["c_add2"]).then_inc(consts, 16)

            @block.gpsimd
            def _(pool):
                nc.gpsimd.memset(rows_i[:, :, :], 1.0).then_inc(filled, 1)
                pool.wait_ge(filled, 1)
                nc.gpsimd.memset(rows_i[0:1, :, SK:PADI], FAR2).then_inc(filled, 1)
                nc.gpsimd.memset(stage[:, S:SLOTS, :], FAR).then_inc(filled, 1)
                nc.gpsimd.memset(stage[:, 0:S, 0], FAR).then_inc(filled, 1)

            @block.vector
            def _(dve):
                for n, (w, b, c, f) in enumerate(jobs):
                    if n >= 2:
                        dve.wait_ge(normed, n - 1)
                    for h in range(DH):
                        src = xnT[:, h, b * S:(b + 1) * S] if w else ctxT[:, b, h, c:c + 512]
                        i = nc.vector.scalar_tensor_tensor(sq[:, n % 2, h, :], src, f, src, ALU.mult, ALU.mult)
                    i.then_inc(squared, 1)
                    if n >= 1:
                        keep_norm(dve, n - 1)
                keep_norm(dve, len(jobs) - 1)

            @block.tensor
            def _(pe):
                pe.wait_ge(consts, 32)
                for n, (w, b, c, f) in enumerate(jobs):
                    pe.wait_ge(squared, n + 1)
                    if n >= 2:
                        pe.wait_ge(norm_kept, n - 1)
                    for h in range(DH):
                        last = nc.tensor.matmul(ps_n[n % 2][0:2, :], ones2[:, w, :], sq[:, n % 2, h, :],
                                                start=(h == 0), stop=(h == DH - 1))
                    last.then_inc(normed, 1)
        with nc.Block() as block:
            @block.tensor
            def _(pe):
                for k in range(RB):
                    if k >= 2:
                        pe.wait_ge(clipped, k - 1)
                    for b in range(B):
                        o = ps_d[k % 2][32 * b:32 * b + 32, :]
                        for h in range(DH):
                            nc.tensor.matmul(o, ctxT[:, b, h, k:PADI:RB], xnT[:, h, b * S:(b + 1) * S],
                                             start=(h == 0), stop=False, tile_position=(0, 32 * b))
                        last = nc.tensor.matmul(o, rows_i[:, b, k:PADI:RB], rows_j[:, b, :], start=False, stop=True,
                                                tile_position=(0, 32 * b))
                    last.then_inc(prod, 1)

            @block.vector
            def _(dve):
                for k in range(RB):
                    dve.wait_ge(prod, k + 1)
                    nc.vector.tensor_scalar(stage[:, 0:S, 1 + k], ps_d[k % 2][:, :], 0.0, None,
                                            ALU.max).then_inc(clipped, 1)

            @block.scalar
            def _(act):
                for k in range(RB):
                    act.wait_ge(clipped, k + 1)
                    nc.scalar.activation(stage[:, 0:S, 1 + k], stage[:, 0:S, 1 + k], ACT.Sqrt).then_inc(rooted, 1)

            @block.sync
            def _(sp):
                for b in range(B):
                    sp.dma_start(ctxT_d[b], ctxT[:, b, :, 0:SK]).then_inc(spilled, 16)
                sp.wait_ge(spilled, 16 * B)
                sp.wait_ge(rooted, RB)
                sp.dma_start(dist.rearrange("p (s k) -> p s k", k=PITCH), stage[:, :, :]).then_inc(stored, 16)
                sp.wait_ge(stored, 16)


def dtw_costs(nc, d, dist, ways, part, rows_came):
    with ExitStack() as es:
        def sb(name, shape, dt):
            return es.enter_context(nc.sbuf_tensor(name, shape, dt))

        def sem(name):
            return es.enter_context(nc.semaphore(name))

        cost = [sb(f"cost{i}", [P, CH + 1, PITCH], F32) for i in range(2)]
        m = sb("m", [P, CH, RB], F32)
        up_ok = sb("up_ok", [P, CH, RB], BF16)
        best = sb("best", [P, CH, RB], F32)
        way = [[sb(f"chunk_{n}{i}", [P, CH, RB], BF16) for n in ("diag", "up", "left")] for i in range(2)]
        KP = RB // 3
        rows = sb("ctx_rows", [P, KP, D], F32)
        loaded = [sem(f"dist_loaded{i}") for i in range(2)]
        freed = [sem(f"dist_freed{i}") for i in range(2)]
        seeded, edge, minned, scanned = sem("seeded"), sem("edge"), sem("minned"), sem("scanned")
        coded, kept, blank = sem("coded"), sem("kept"), sem("blank")
        zeroed, split, tail = sem("zeroed"), sem("split"), sem("tail")
        shift_up = [NBLK - 1] + list(range(NBLK - 1))
        full = SK // RB
        G = 4
        pieces = [(op, s0) for op in range(5) for s0 in range(0, CH, G)]
        with nc.Block() as block:
            @block.sync
            def _(sp):
                sp.wait_ge(blank, 1)
                sp.dma_start(cost[1][:, CH, :], d["c_corner"]).then_inc(seeded, 16)
                with sp.Fori(0, NCH // 2) as it:
                    for h in range(2):
                        sp.wait_ge(freed[h], it + 1)
                        src = ap_of(dist, (2 * it + h) * (CH * PITCH),
                                    [[NBLK * ROW, B], [ROW - PITCH, NBLK], [PITCH, CH], [1, PITCH]])
                        sp.dma_start(cost[h][:, 1:CH + 1, :], src).then_inc(loaded[h], 16)

            @block.vector
            def _(dve):
                def rule(h, op, s0, n=G):
                    w = cost[h]
                    s = slice(s0, s0 + n)
                    cu, cd, cl = w[:, s0 + 1:s0 + n + 1, 0:RB], w[:, s, 0:RB], w[:, s, 1:PITCH]
                    dg, up, lf = (x[:, s, :] for x in way[h])
                    if op == 0:
                        return nc.vector.tensor_tensor(up_ok[:, s, :], cu, cl, ALU.is_le)
                    if op == 1:
                        return nc.vector.tensor_tensor(best[:, s, :], cu, cl, ALU.min)
                    if op == 2:
                        return nc.vector.tensor_tensor(dg, cd, best[:, s, :], ALU.is_le)
                    if op == 3:
                        return nc.vector.tensor_tensor(up, up_ok[:, s, :], dg, ALU.is_gt)
                    return nc.vector.scalar_tensor_tensor(lf, up_ok[:, s, :], 0.0, dg, ALU.is_equal, ALU.is_gt)

                nc.vector.memset(cost[1][:, :, :], FAR).then_inc(blank, 1)
                nc.vector.nop().then_inc(freed[0], 1)
                dve.wait_ge(seeded, 16)
                with dve.Fori(0, NCH // 2) as it:
                    for h in range(2):
                        w, before = cost[h], cost[1 - h]
                        dve.wait_ge(loaded[h], it * 16 + 16)
                        if h == 1:
                            dve.wait_ge(scanned, CH)
                        nc.vector.tensor_copy(w[:, 0, :], before[:, CH, :]).then_inc(edge, 1)
                        todo = list(pieces)
                        for s in range(CH):
                            n = h * CH + s
                            dve.wait_ge(*((edge, h + 1) if s == 0 else (scanned, n)))
                            nc.vector.stream_shuffle(w[:, s + 1, 0:1], w[:, s, RB:RB + 1], shift_up)
                            nc.vector.tensor_tensor(m[:, s, :], w[:, s, 0:RB], w[:, s, 1:PITCH],
                                                    ALU.min).then_inc(minned, 1)
                            if s == 1:
                                dve.wait_ge(kept, it * 2 + h + 1)
                            if s >= 1 and todo:
                                rule(1 - h, *todo.pop(0))
                            dve.wait_ge(minned, n + 1)
                            nc.vector.tensor_tensor_scan(w[:, s + 1, 1:PITCH], m[:, s, :], w[:, s + 1, 1:PITCH],
                                                         w[:, s + 1, 0:1], ALU.min, ALU.add).then_inc(scanned, 1)
                            if s >= 1 and todo:
                                i = rule(1 - h, *todo.pop(0))
                                if not todo:
                                    i.then_inc(coded, 1)
                                    dve.wait_ge(coded, it * 2 + h + 1)
                                    nc.vector.nop().then_inc(freed[1 - h], 1)
                        assert not todo
                    dve.wait_ge(scanned, 2 * CH)
                    dve.sem_clear(scanned)
                    dve.sem_clear(minned)
                    dve.sem_clear(edge)
                dve.wait_ge(kept, NCH)
                for op in range(5):
                    rule(1, op, 0, CH).then_inc(coded if op == 4 else tail, 1)
                    if op < 4:
                        dve.wait_ge(tail, op + 1)

            @block.scalar
            def _(act):
                nc.scalar.nop().then_inc(kept, 1)

                def keep(buf, at):
                    for a, w in zip(ways, way[buf]):
                        last = nc.scalar.copy(a[:, bass.ds(at, CH), :], w[:, :, ::-1])
                    last.then_inc(kept, 1)

                with act.Fori(0, NCH // 2) as it:
                    for h in range(2):
                        act.wait_ge(coded, it * 2 + h + 1)
                        keep(1 - h, it * (2 * CH) + h * CH)
                act.wait_ge(coded, NCH + 1)
                keep(1, NCH * CH)

            @block.gpsimd
            def _(pool):
                for q in range(3):
                    nc.gpsimd.memset(rows[:, :, :], 0.0).then_inc(zeroed, 1)
                    pool.wait_ge(zeroed, q + 1)
                    for b in range(B):
                        c = d["ctx_1024"][b]
                        pool.dma_start(rows[32 * b:32 * b + full, :, :],
                                       c[0:full * RB, :].rearrange("(c k) d -> c k d", k=RB)[:, q * KP:(q + 1) * KP, :]
                                       ).then_inc(rows_came, 16)
                        if q == 0:
                            pool.dma_start(rows[32 * b + full:32 * b + full + 1, 0:SK - full * RB, :],
                                           c[full * RB:SK, :].rearrange("(c k) d -> c k d", c=1)).then_inc(rows_came, 16)
                    pool.wait_ge(rows_came, 16 * B * (q + 2))
                    p0, p1, p2 = (x[:, q * KP:(q + 1) * KP, :] for x in part)
                    nc.gpsimd.tensor_copy(p0, rows[:]).then_inc(split, 1)
                    pool.wait_ge(split, 4 * q + 1)
                    nc.gpsimd.tensor_tensor(rows[:], rows[:], p0, ALU.subtract).then_inc(split, 1)
                    pool.wait_ge(split, 4 * q + 2)
                    nc.gpsimd.tensor_copy(p1, rows[:]).then_inc(split, 1)
                    pool.wait_ge(split, 4 * q + 3)
                    nc.gpsimd.tensor_tensor(p2, rows[:], p1, ALU.subtract).then_inc(split, 1)
                    pool.wait_ge(split, 4 * q + 4)


def backtrack(nc, d, ways, path, part, x_sb, gate):
    with ExitStack() as es:
        def sb(name, shape, dt):
            return es.enter_context(nc.sbuf_tensor(name, shape, dt))

        def sem(name):
            return es.enter_context(nc.semaphore(name))

        W2 = 2 * RB
        on = [sb(f"on{i}", [P, CH, W2 + 2], BF16) for i in range(2)]
        packed = [sb(f"packed{i}", [P, CH, RB], BF16) for i in range(2)]
        came = [sb(f"came{i}", [P, CH + 1, W2 + 2], BF16) for i in range(2)]
        went = [sb(f"went{i}", [P, CH + 1, W2 + 2], BF16) for i in range(2)]
        enter = sb("enter", [P, 2, W2], BF16)
        inner = sb("inner", [P, 1], F32)
        first = sb("first", [P, 2, CH], BF16)
        onp = sb("onp", [P, P, RB], BF16)
        ps = [es.enter_context(nc.psum_tensor(f"ps_e{i}", [P, 512], F32)) for i in range(2 * B)]
        b_end, ones_in, fetched = sem("b_end"), sem("b_ones"), sem("fetched")
        edges, entered, traced, done = sem("b_edges"), sem("b_entered"), sem("b_traced"), sem("b_done")
        pack, saved = sem("b_pack"), [sem("b_saved0"), sem("b_saved1")]
        taken, summed, added = sem("b_taken"), sem("b_summed"), sem("b_added")
        shift_down = list(range(1, NBLK)) + [0]
        turns = [NCH // 2 - jt * (P // CH) // 2 for jt in range(QT - 1, -1, -1)]
        with nc.Block() as block:
            @block.sync
            def _(sp):
                sp.dma_start(inner[:], d["c_inner"]).then_inc(saved[0], 16)
                sp.dma_start(on[1][:, 0, :], d["c_seed"].bitcast(BF16)).then_inc(saved[1], 16)
                start = 0
                for q, end in enumerate(turns):
                    with sp.Fori(start, end) as it:
                        for h in range(2):
                            sp.wait_ge(pack, it * 2 + h + 3)
                            at = (it * (-2 * CH * RB)) + (NCH - 1 - h) * CH * RB
                            sp.dma_start(path[:, bass.ds(at, CH * RB)].rearrange("p (s k) -> p s k", k=RB),
                                         packed[h][:]).then_inc(saved[h], 16)
                    start = end
                    for h in range(2):
                        sp.wait_ge(saved[h], 16 * end + 16)
                    if q:
                        sp.wait_ge(summed, q)
                    src = ap_of(path, (QT - 1 - q) * P * RB,
                                [[NBLK * SLOTS * RB, B], [SLOTS * RB + RB, NBLK], [1, P * RB]])
                    sp.dma_start(onp[:, :, :].rearrange("p s k -> p (s k)"), src).then_inc(taken, 16)

            @block.gpsimd
            def _(pool):
                end = CH + SLOTS
                for n, (a, v) in enumerate(zip(ways, (0.0, 0.0, 1.0))):
                    nc.gpsimd.memset(a[:, end - 1:end + 2, :], v).then_inc(b_end, 1)
                    pool.wait_ge(b_end, n + 1)

            @block.scalar
            def _(act):
                def fetch(h, at):
                    nc.scalar.copy(went[h][:, :, 2:W2 + 2:2], ways[1][:, bass.ds(at, CH + 1), :])
                    nc.scalar.copy(came[h][:, :, 2:W2 + 2:2], ways[0][:, bass.ds(at + 1, CH + 1), :])
                    nc.scalar.copy(came[h][:, :, 1:W2 + 1:2],
                                   ways[2][:, bass.ds(at + 1, CH + 1), :]).then_inc(fetched, 1)

                def keep(h):
                    nc.scalar.copy(packed[h][:], on[h][:, :, 3:W2 + 2:2]).then_inc(pack, 1)

                nc.scalar.nop().then_inc(pack, 2)
                act.wait_ge(b_end, 3)
                for h in range(2):
                    fetch(h, (NCH - 1 - h) * CH + CH)
                with act.Fori(0, NCH // 2 - 1) as it:
                    for h in range(2):
                        act.wait_ge(done, it * 2 + h + 1)
                        act.wait_ge(saved[h], it * 16 + 16)
                        keep(h)
                        fetch(h, (it * (-2 * CH)) + (NCH - 3 - h) * CH + CH)
                for h in range(2):
                    act.wait_ge(done, NCH - 1 + h)
                    act.wait_ge(saved[h], 8 * NCH)
                    keep(h)

            @block.tensor
            def _(pe):
                for q in range(QT):
                    jt = QT - 1 - q
                    pe.wait_ge(taken, 16 * (q + 1))
                    if q >= 2:
                        pe.wait_ge(added, q - 1)
                    for k in range(RB):
                        for i in range(3):
                            for b in range(B):
                                r = slice(32 * b, 32 * b + 32)
                                last = nc.tensor.matmul(ps[2 * b + q % 2][:, 0:D], onp[r, :, RB - 1 - k], part[i][r, k, :],
                                                        start=(k == 0 and i == 0), stop=(k == RB - 1 and i == 2),
                                                        tile_position=(32 * b, 0))
                    last.then_inc(summed, 1)

            @block.vector
            def _(dve):
                def add(q):
                    dve.wait_ge(summed, q + 1)
                    for b in range(B):
                        t = b * QT + QT - 1 - q
                        i = nc.vector.scalar_tensor_tensor(x_sb[:, t, :], ps[2 * b + q % 2][:, 0:D], gate[:, 0:1], x_sb[:, t, :],
                                                           ALU.mult, ALU.add)
                    i.then_inc(added, 1)

                for i in range(2):
                    nc.vector.memset(went[i][:, :, 1:W2 + 2:2], 1.0).then_inc(ones_in, 1)
                dve.wait_ge(ones_in, 2)
                for h in range(2):
                    dve.wait_ge(saved[h], 16)
                start = 0
                for q, end in enumerate(turns):
                    if q >= 2:
                        add(q - 2)
                    with dve.Fori(start, end) as it:
                        for h in range(2):
                            dve.wait_ge(fetched, it * 2 + h + 1)
                            dve.wait_ge(pack, it * 2 + h + 1)
                            for n, a in enumerate((went, came)):
                                nc.vector.tensor_scalar(first[:, n, :], a[h][:, 1:CH + 1, W2], inner[:, 0:1], None,
                                                        ALU.mult).then_inc(edges, 1)
                            dve.wait_ge(edges, 4 * h + 2)
                            for n, a in enumerate((went, came)):
                                nc.vector.stream_shuffle(a[h][:, 0:CH, 0], first[:, n, :], shift_down).then_inc(edges, 1)
                            dve.wait_ge(edges, 4 * h + 4)
                            for s in range(CH - 1, -1, -1):
                                n = h * CH + CH - 1 - s
                                if n:
                                    dve.wait_ge(traced, n)
                                after = on[h][:, s + 1, :] if s < CH - 1 else on[1 - h][:, 0, :]
                                nc.vector.stream_shuffle(on[h][:, s, 1:2], after[:, W2 + 1:W2 + 2], shift_down)
                                pair = ap_of(after, 1, [after.ap[0], [2, RB], [2, 2]])
                                nc.vector.tensor_tensor(
                                    enter[:, s % 2, :].rearrange("p (r e) -> p r e", e=2), pair,
                                    came[h][:, s, 0:W2].rearrange("p (r e) -> p r e", e=2), ALU.mult).then_inc(entered, 1)
                                dve.wait_ge(entered, n + 1)
                                nc.vector.tensor_tensor_scan(on[h][:, s, 2:W2 + 2], went[h][:, s, 0:W2],
                                                             enter[:, s % 2, :], on[h][:, s, 1:2],
                                                             ALU.mult, ALU.add).then_inc(traced, 1)
                            dve.wait_ge(traced, (h + 1) * CH)
                            nc.vector.nop().then_inc(done, 1)
                        for s in (edges, entered, traced):
                            dve.sem_clear(s)
                    start = end
                add(QT - 2)
                add(QT - 1)


NH, HD = 16, 16
HG = 4
NG = NH // HG
GW = HG * HD
NPART = 6
STK = NPART * HD
MAXR = 3
VW = 32
NEG = -1e30
K_SLOTS = ((0, 1, 2), (3, 4), (5,))
Q_SLOTS = ((0, 3, 5), (1, 4), (2,))


class Names:

    def __init__(self, nc, es, stage):
        self.nc, self.es, self.stage = nc, es, stage
        self.sems = []

    def sb(self, name, shape, dt=F32):
        return self.es.enter_context(self.nc.sbuf_tensor(f"{self.stage}_{name}", shape, dt))

    def ps(self, name, shape, dt=F32):
        return self.es.enter_context(self.nc.psum_tensor(f"{self.stage}_{name}", shape, dt))

    def sem(self, name):
        s = self.es.enter_context(self.nc.semaphore(f"{self.stage}_{name}"))
        self.sems.append(s)
        return s

    def clear(self):
        for s in self.sems:
            self.nc.gpsimd.sem_clear(s)
        self.nc.all_engine_barrier()


class Heads:

    def __init__(self, nc, es, stage, keys):
        sb = Names(nc, es, stage)
        self.nc, self.sb, self.keys, self.kt_n = nc, sb, keys, keys // P
        self.causal = keys == S
        self.halves = keys // 512
        self.units = self.kt_n * HG
        self.njobs = 1 + self.halves
        self.qT = sb.sb("qT", [STK + MAXR, NH, S], BF16)
        self.kT = sb.sb("kT", [STK + MAXR, NH, keys], BF16)
        self.vt = sb.sb("vt", [P, self.kt_n, NH, VW])
        self.attn = sb.sb("attn", [P, NT, D])
        self.stk = sb.sb("stk", [P, self.njobs, QT * HG, STK], BF16)
        self.rest = sb.sb("rest", [P, QT * HG, HD])
        self.hTb = sb.sb("hTb", [P, DH, S])

    def plan(self, preps, steps):
        self.rounds = []
        for s in steps:
            here = [(u, s + 2, kind) for u, kind in self.rounds_of] if s + 2 in preps else []
            here += [(u, None, kind) for u, kind in self.mask_rounds(s)]
            self.rounds += [(s, u, p, kind) for u, p, kind in sorted(here, key=lambda r: r[0])]
        self.preps = preps

    def mask_rounds(self, s):
        return []

    def open(self, nm):
        self.bank = [nm.ps(f"prep{i}", [P, 512]) for i in range(2)]
        self.made = nm.sem("made")
        self.freed = {"dve": nm.sem("freed_dve"), "act": nm.sem("freed_act")}
        self.loaded = nm.sem("loaded")
        self.first, self.step = nm.sem("sp_first"), nm.sem("sp_step")
        self.second, self.stacked = nm.sem("sp_second"), nm.sem("sp_stacked")
        self.rep = {"act": nm.sem("rep_act"), "pool": nm.sem("rep_pool")}
        self.steps_made = 0

    def takers(self, kind):
        if kind[0] == "turn":
            return ("dve", "act")[kind[2]:kind[2] + 1]
        return ("act",) if kind[0] == "mask" else ("dve", "act") if kind[0] in ("kv", "qkv") else ("dve",)

    def taken(self, who, upto):
        return sum(who in self.takers(r[3]) for r in self.rounds[:upto + 1])

    def job(self, p, j):
        return (p - self.preps[0]) * self.njobs + j

    def wait_ready(self, pe, g):
        if g in self.preps:
            last = max(i for i, r in enumerate(self.rounds) if r[2] == g)
            for who, sem in self.freed.items():
                pe.wait_ge(sem, self.taken(who, last))

    def fill(self, pe, s, u):
        nc = self.nc
        for rn, (rs, ru, p, kind) in enumerate(self.rounds):
            if (rs, ru) != (s, u):
                continue
            if rn >= 2:
                for who in self.takers(self.rounds[rn - 2][3]):
                    pe.wait_ge(self.freed[who], self.taken(who, rn - 2))
            bank = self.bank[rn % 2]
            if kind[0] == "turn":
                _, j, pair = kind
                n = self.job(p, j) + 1
                pe.wait_ge(self.stacked, n)
                pe.wait_ge(self.rep["act"], n)
                pe.wait_ge(self.rep["pool"], n)
                out = bank[0:STK, :].bitcast(BF16)
                for i in range(2):
                    for t in range(QT):
                        c = (i * QT + t) * P
                        last = nc.tensor.transpose(out[:, c:c + P], self.stk[:, j, t * HG + 2 * pair + i, :],
                                                   self.identb[:, :])
            else:
                last = self.project(pe, bank, p, kind)
            last.then_inc(self.made, 1)

    def take(self, who, eng, s, u):
        for rn, (rs, ru, p, kind) in enumerate(self.rounds):
            after = who == "act" and len(self.takers(kind)) == 2
            if (rs, ru + 1 + after) != (s, u) or who not in self.takers(kind):
                continue
            eng.wait_ge(self.made, rn + 1)
            if after:
                eng.wait_ge(self.freed["dve"], self.taken("dve", rn))
            bank = self.bank[rn % 2]
            if kind[0] == "turn":
                _, j, pair = kind
                h0 = (p % NG) * HG + 2 * pair
                dst = self.qT[0:STK, h0:h0 + 2, :] if j == 0 else self.kT[0:STK, h0:h0 + 2, (j - 1) * 512:j * 512]
                src = bank[0:STK, :].bitcast(BF16).rearrange("p (h s) -> p h s", h=2)
                copy = self.nc.vector.tensor_copy if who == "dve" else self.nc.scalar.copy
                copy(dst, src).then_inc(self.freed[who], 1)
            else:
                self.take_projection(who, eng, bank, p, kind)

    def split(self, dve, p, j, src, slots, scale, frees):
        nc, n = self.nc, self.job(p, j) + 1
        rest = self.rest[:, :, :].rearrange("p (t h) e -> p t h e", t=QT)

        def at(part):
            s = slots[part][0]
            return self.stk[:, j, :, s * HD:(s + 1) * HD].rearrange("p (t h) e -> p t h e", t=QT)
        nc.vector.tensor_scalar(at(0), src, scale, None, ALU.mult).then_inc(self.first, 1)
        dve.wait_ge(self.first, n)
        i = nc.vector.scalar_tensor_tensor(rest, src, scale, at(0), ALU.mult, ALU.subtract)
        i.then_inc(self.step, 1)
        self.steps_made += 1
        dve.wait_ge(self.step, self.steps_made)
        if frees:
            nc.vector.nop().then_inc(self.freed["dve"], 1)
        nc.vector.tensor_copy(at(1), rest).then_inc(self.second, 1)
        dve.wait_ge(self.second, n)
        nc.vector.tensor_tensor(at(2), rest, at(1), ALU.subtract).then_inc(self.stacked, 1)

    def repeat(self, act, s, u):
        for ru, j in self.repeats:
            if ru == u and s + 2 in self.preps:
                act.wait_ge(self.first, self.job(s + 2, j) + 1)
                a, b, c = (Q_SLOTS if j == 0 else K_SLOTS)[0]
                at = [self.stk[:, j, :, x * HD:(x + 1) * HD] for x in (a, b, c)]
                self.nc.scalar.copy(at[1], at[0])
                self.nc.scalar.copy(at[2], at[0]).then_inc(self.rep["act"], 1)

    def pool_all(self, pool):
        for p in self.preps:
            for j in range(self.njobs):
                pool.wait_ge(self.second, self.job(p, j) + 1)
                a, b = (Q_SLOTS if j == 0 else K_SLOTS)[1]
                self.nc.gpsimd.tensor_copy(self.stk[:, j, :, b * HD:(b + 1) * HD],
                                           self.stk[:, j, :, a * HD:(a + 1) * HD]).then_inc(self.rep["pool"], 1)

    def finish(self, dve):
        pass

    def convert(self, dve, s, u):
        pass


def attend(nc, stage, heads, ident, identb, b, firsts, seconds, preps):
    with ExitStack() as es:
        nm = Names(nc, es, stage)
        kt_n, halves, causal = heads.kt_n, heads.halves, heads.causal
        qT, kT, vt = heads.qT, heads.kT, heads.vt
        steps = range(-2, 0) if not len(seconds) else range(0, NG)
        ps1 = [nm.ps(f"s1_{i}", [P, 512]) for i in range(2)]
        ps2 = [nm.ps(f"s2_{i}", [P, 512]) for i in range(2)]
        pso = nm.ps("o", [P, 512])
        pst = nm.ps("turned", [P, 512])
        psm = pst[0:MAXR, :].bitcast(BF16)
        NE = 8
        ebuf = [nm.sb(f"exp{i}", [P, 512]) for i in range(NE)]
        NJ = 4
        junk = nm.sb("junk", [P, NJ, 512], BF16)
        mx = nm.sb("max", [P, 2, HG, QT, halves])
        neg = nm.sb("neg", [P, HG * QT])
        negr = nm.sb("negr", [P, HG * QT])
        parts = nm.sb("parts", [P, 2, HG * QT, MAXR], BF16)
        osb = nm.sb("osb", [P, 2, 512])
        rden = nm.sb("rden", [P, HG * QT])
        scored, maxed = nm.sem("scored"), nm.sem("maxed")
        negated, parted = nm.sem("negated"), nm.sem("parted")
        mturned, mkept = nm.sem("mturned"), nm.sem("mkept")
        scored2, exped, weighed = nm.sem("scored2"), nm.sem("exped"), nm.sem("weighed")
        okept, oturned, inverted, normed = nm.sem("okept"), nm.sem("oturned"), nm.sem("inverted"), nm.sem("normed")
        heads.plan(preps, steps)
        heads.open(nm)
        u1 = [(h, qt, f) for h in range(HG) for qt in range(QT) for f in range(halves)]
        u2 = [(kt, h) for kt in range(kt_n) for h in range(HG)]
        n1, n2 = len(u1), len(u2)
        LAG, WG = 2, 2

        def width1(qt):
            return (qt + 1) * P if causal else 512

        def slot(g, h):
            return (g % NG) * HG + h

        with nc.Block() as block:
            @block.sync
            def _(sp):
                heads.load(sp, b)

            @block.tensor
            def _(pe):
                def first(g, u):
                    h, qt, f = u1[u]
                    n = (g - firsts[0]) * n1 + u
                    if u == 0:
                        heads.wait_ready(pe, g)
                    if n >= 2:
                        pe.wait_ge(maxed, n - 1)
                    w = width1(qt)
                    nc.tensor.matmul(ps1[n % 2][:, 0:w], qT[0:STK, slot(g, h), qt * P:(qt + 1) * P],
                                     kT[0:STK, slot(g, h), f * 512:f * 512 + w], start=True,
                                     stop=True).then_inc(scored, 1)

                def turn_max(g):
                    i = g - firsts[0]
                    pe.wait_ge(parted, 3 * (i + 1))
                    if g - 1 in seconds and g >= 2:
                        pe.wait_ge(normed, g - 1)
                    for pair in range(HG // 2):
                        if i or pair:
                            pe.wait_ge(mkept, i * (HG // 2) + pair)
                        for k in range(2):
                            for qt in range(QT):
                                c = (k * QT + qt) * P
                                last = nc.tensor.transpose(psm[:, c:c + P],
                                                           parts[:, g % 2, (2 * pair + k) * QT + qt, :], identb[:, :])
                        last.then_inc(mturned, 1)

                def second(g, u):
                    kt, h = u2[u]
                    n = g * n2 + u
                    if u == 0 and g in firsts:
                        pe.wait_ge(mkept, (g - firsts[0] + 1) * (HG // 2))
                    if n >= 2:
                        pe.wait_ge(exped, n - 1)
                    q0 = kt * P if causal else 0
                    o = ps2[n % 2]
                    nc.tensor.matmul(o[:, q0:512], kT[:, slot(g, h), kt * P:(kt + 1) * P], qT[:, slot(g, h), q0:512],
                                     start=True, stop=False)
                    w = P if causal else 512
                    nc.tensor.matmul(o[:, q0:q0 + w], identb[:, :], heads.bias_k(kt), start=False,
                                     stop=True).then_inc(scored2, 1)

                def weigh(g, u):
                    kt, h = u2[u]
                    n = g * n2 + u
                    pe.wait_ge(exped, n + 1)
                    if u == 0 and g:
                        pe.wait_ge(okept, g)
                    q0 = kt * P if causal else 0
                    nc.tensor.matmul(pso[32 * h:32 * h + 32, q0:512], vt[:, kt, slot(g, h), :],
                                     ebuf[n % NE][:, q0:512], start=(kt == 0), stop=(kt == kt_n - 1),
                                     tile_position=(0, 32 * h), skip_group_check=True).then_inc(weighed, 1)

                def turn_out(g):
                    pe.wait_ge(okept, g + 1)
                    if g:
                        pe.wait_ge(normed, g)
                    if g + 1 in firsts:
                        pe.wait_ge(mkept, (g + 2 - firsts[0]) * (HG // 2))
                    for qt in range(QT):
                        last = nc.tensor.transpose(pst[:, qt * P:(qt + 1) * P], osb[:, g % 2, qt * P:(qt + 1) * P],
                                                   ident[:, :])
                    last.then_inc(oturned, 1)

                for s in steps:
                    at = 0
                    for u in range(n2):
                        if s in seconds:
                            second(s, u)
                        if s + 1 in firsts:
                            first(s + 1, u)
                        if s in seconds and u - LAG + 1 - at >= WG:
                            for v in range(at, at + WG):
                                weigh(s, v)
                            at += WG
                        if s in seconds and s and u == LAG + 2:
                            turn_out(s - 1)
                        heads.fill(pe, s, u)
                    if s in seconds:
                        for v in range(at, n2):
                            weigh(s, v)
                    if s + 1 in firsts:
                        turn_max(s + 1)
                if len(seconds):
                    turn_out(NG - 1)

            @block.vector
            def _(dve):
                def take_max(g, u):
                    h, qt, f = u1[u]
                    n = (g - firsts[0]) * n1 + u
                    dve.wait_ge(scored, n + 1)
                    w = width1(qt)
                    if n >= NJ:
                        dve.wait_ge(maxed, n - NJ + 1)
                    nc.vector.tensor_tensor_reduce(junk[:, n % NJ, 0:w], ps1[n % 2][:, 0:w], heads.bias_q(g, qt, f),
                                                   1.0, NEG * 4, ALU.add, ALU.max,
                                                   mx[:, g % 2, h, qt, f:f + 1]).then_inc(maxed, 1)

                def negate(g):
                    i = g - firsts[0]
                    dve.wait_ge(maxed, (i + 1) * n1)
                    if i:
                        dve.wait_ge(parted, 3 * i)
                    m = mx[:, g % 2, :, :, :].rearrange("p h t f -> p (h t) f")
                    nc.vector.tensor_reduce(neg[:, :], m, AX.X, ALU.max, negate=True).then_inc(negated, 1)
                    dve.wait_ge(negated, 3 * i + 1)
                    p3 = parts[:, g % 2, :, :]
                    nc.vector.tensor_copy(p3[:, :, 0], neg[:, :]).then_inc(parted, 1)
                    dve.wait_ge(parted, 3 * i + 1)
                    nc.vector.tensor_tensor(negr[:, :], neg[:, :], p3[:, :, 0], ALU.subtract).then_inc(negated, 1)
                    dve.wait_ge(negated, 3 * i + 2)
                    nc.vector.tensor_copy(p3[:, :, 1], negr[:, :]).then_inc(parted, 1)
                    dve.wait_ge(parted, 3 * i + 2)
                    nc.vector.tensor_tensor(neg[:, :], negr[:, :], p3[:, :, 1], ALU.subtract).then_inc(negated, 1)
                    dve.wait_ge(negated, 3 * i + 3)
                    nc.vector.tensor_copy(p3[:, :, 2], neg[:, :]).then_inc(parted, 1)

                def normalise(g):
                    dve.wait_ge(oturned, g + 1)
                    if g:
                        dve.wait_ge(normed, g)
                    t = pst[:, :].rearrange("p (t h e) -> p t h e", t=QT, h=HG)
                    r = rden[:, :].rearrange("p (t h) -> p t h", t=QT)
                    nc.vector.reciprocal(r, t[:, :, :, HD]).then_inc(inverted, 1)
                    dve.wait_ge(inverted, g + 1)
                    for qt in range(QT):
                        o = heads.attn[:, bass.ds(b * QT + qt, 1), g * GW:(g + 1) * GW].rearrange(
                            "p o (h e) -> p (o h) e", h=HG)
                        rb = ap_of(rden[:, qt * HG:(qt + 1) * HG], 0, [rden[:, :].ap[0], [1, HG], [0, HD]])
                        i = nc.vector.tensor_tensor(o, t[:, qt, :, 0:HD], rb, ALU.mult)
                    i.then_inc(normed, 1)

                for s in steps:
                    for u in range(n1):
                        if s + 1 in firsts:
                            take_max(s + 1, u)
                        if s in seconds and s and u == LAG + 3:
                            normalise(s - 1)
                        heads.take("dve", dve, s, u)
                        heads.convert(dve, s, u)
                    if s + 1 in firsts:
                        negate(s + 1)
                if len(seconds):
                    normalise(NG - 1)
                    dve.wait_ge(scored2, NG * n2)
                heads.finish(dve)

            @block.scalar
            def _(act):
                def keep_max(g):
                    i = g - firsts[0]
                    for pair in range(HG // 2):
                        act.wait_ge(mturned, i * (HG // 2) + pair + 1)
                        h0 = slot(g, 2 * pair)
                        nc.scalar.copy(qT[STK:STK + MAXR, h0:h0 + 2, :],
                                       psm.rearrange("p (h s) -> p h s", h=2)).then_inc(mkept, 1)

                for s in steps:
                    for u in range(n2):
                        if s in seconds:
                            n = s * n2 + u
                            kt, h = u2[u]
                            q0 = kt * P if causal else 0
                            act.wait_ge(scored2, n + 1)
                            if n >= NE:
                                act.wait_ge(weighed, n - NE + 1)
                            nc.scalar.activation(ebuf[n % NE][:, q0:512], ps2[n % 2][:, q0:512],
                                                 ACT.Exp).then_inc(exped, 1)
                        heads.take("act", act, s, u)
                        heads.repeat(act, s, u)
                    if s in seconds:
                        act.wait_ge(weighed, (s + 1) * n2)
                        if s >= 2:
                            act.wait_ge(oturned, s - 1)
                        nc.scalar.copy(osb[:, s % 2, :], pso[:, :]).then_inc(okept, 1)
                    if s + 1 in firsts:
                        keep_max(s + 1)

            @block.gpsimd
            def _(pool):
                heads.pool_all(pool)
        nm.clear()


def attend_all(nc, stage, heads, ident, identb):
    with nc.Block() as block:
        @block.vector
        def _(dve):
            nc.vector.memset(heads.kT[STK:STK + MAXR, :, :], 1.0)
            nc.vector.memset(heads.vt[:, :, :, HD:HD + 1], 1.0)
            nc.vector.memset(heads.vt[:, :, :, HD + 1:VW], 0.0)
    nothing = range(0)
    heads.identb = identb
    attend(nc, f"{stage}f", heads, ident, identb, None, range(0, 1), nothing, range(0, 2))
    with nc.Fori(0, B - 1) as b:
        attend(nc, f"{stage}m", heads, ident, identb, b, range(1, NG + 1), range(NG), range(2, NG + 2))
    attend(nc, f"{stage}l", heads, ident, identb, B - 1, range(1, NG), range(NG), range(2, NG))


def project_out(nc, nm, ident, attn, w, add):
    ps = [nm.ps(f"at{i}", [P, 512]) for i in range(2)]
    py = [nm.ps(f"ay{i}", [P, 512]) for i in range(2)]
    aT = nm.sb("attnT", [P, 2, DH, QT * P])
    turned, kept, done, added = nm.sem("at_turned"), nm.sem("at_kept"), nm.sem("at_done"), nm.sem("at_added")
    with nc.Block() as block:
        @block.tensor
        def _(pe):
            def turn(b):
                for h in range(DH):
                    n = b * DH + h
                    if n >= 2:
                        pe.wait_ge(kept, n - 1)
                    for t in range(QT):
                        last = nc.tensor.transpose(ps[n % 2][:, t * P:(t + 1) * P],
                                                   attn[:, b * QT + t, h * P:(h + 1) * P], ident[:, :])
                    last.then_inc(turned, 1)

            turn(0)
            for b in range(B):
                if b + 1 < B:
                    turn(b + 1)
                pe.wait_ge(kept, DH * (b + 1))
                for t in range(QT):
                    n = b * QT + t
                    if n >= 2:
                        pe.wait_ge(added, n - 1)
                    for h in range(DH):
                        last = nc.tensor.matmul(py[n % 2][:, 0:D], aT[:, b % 2, h, t * P:(t + 1) * P], w[:, h, :],
                                                start=(h == 0), stop=(h == DH - 1))
                    last.then_inc(done, 1)

        @block.scalar
        def _(act):
            for b in range(B):
                if b >= 2:
                    act.wait_ge(done, QT * (b - 1))
                for h in range(DH):
                    act.wait_ge(turned, b * DH + h + 1)
                    nc.scalar.copy(aT[:, b % 2, h, :], ps[(b * DH + h) % 2][:, :]).then_inc(kept, 1)

        @block.vector
        def _(dve):
            for t in range(NT):
                dve.wait_ge(done, t + 1)
                add(t, py[t % 2][:, 0:D]).then_inc(added, 1)


def spill(nc, es, name, src, dst):
    stored = es.enter_context(nc.semaphore(f"{name}_stored"))
    with nc.Block() as block:
        @block.sync
        def _(sp):
            for b in range(B):
                sp.dma_start(dst[b], src(b)).then_inc(stored, 16)
            sp.wait_ge(stored, 16 * B)


class SelfHeads(Heads):

    rounds_of = ((0, ("qkv", 0)), (1, ("qkv", 1)), (8, ("turn", 0, 0)), (10, ("turn", 0, 1)), (12, ("turn", 1, 0)),
                 (14, ("turn", 1, 1)))
    repeats = ((5, 0), (6, 1))

    def __init__(self, nc, es, hT_d, wqkv, rope, tri_q, tri_k):
        super().__init__(nc, es, "l0", S)
        self.hT_d, self.wqkv, self.rope, self.tri_q, self.tri_k = hT_d, wqkv, rope, tri_q, tri_k
        self.qr = self.sb.sb("qr", [P, 2, QT * HG, HD])
        self.tmp = self.sb.sb("ropetmp", [P, 4, 2, 2 * HG, HD // 2])

    def open(self, nm):
        super().open(nm)
        self.rotated, self.summed = nm.sem("rotated"), nm.sem("summed")

    def bias_q(self, g, qt, f):
        return self.tri_q[:, 512 - (qt + 1) * P:512]

    def bias_k(self, kt):
        return self.tri_k[:, :]

    def load(self, sp, b):
        if 0 in self.preps:
            sp.dma_start(self.hTb[:, :, :], self.hT_d[0]).then_inc(self.loaded, 16)
        elif NG in self.preps:
            last = max(i for i, r in enumerate(self.rounds) if r[2] == NG - 1 and r[3][0] == "qkv")
            sp.wait_ge(self.made, last + 1)
            sp.dma_start(self.hTb[:, :, :], self.hT_d[bass.ds(b + 1, 1)].rearrange("o p h s -> p (o h) s")).then_inc(
                self.loaded, 16)

    def project(self, pe, bank, p, kind):
        if p % NG == 0 and kind[1] == 0:
            pe.wait_ge(self.loaded, 16)
        w = 3 * GW
        for i in range(2):
            t = 2 * kind[1] + i
            for h in range(DH):
                last = self.nc.tensor.matmul(bank[:, i * w:(i + 1) * w], self.hTb[:, h, t * P:(t + 1) * P],
                                             self.wqkv[:, h, (p % NG) * w:(p % NG + 1) * w], start=(h == 0),
                                             stop=(h == DH - 1))
        return last

    def take_projection(self, who, eng, bank, p, kind):
        nc = self.nc
        half, hw, n = kind[1], HD // 2, (p - self.preps[0]) * 2 + kind[1] + 1
        src = bank[:, 0:6 * GW].rearrange("p (t c e) -> p t c e", t=2 * HG, c=3)
        if who == "act":
            dst = self.vt[:, 2 * half:2 * half + 2, (p % NG) * HG:(p % NG + 1) * HG, 0:HD]
            nc.scalar.copy(dst, bank[:, 0:6 * GW].rearrange("p (t h c e) -> p t h c e", t=2, h=HG, c=3)[
                :, :, :, 2, :]).then_inc(self.freed["act"], 1)
            return
        th = slice(2 * HG * half, 2 * HG * (half + 1))
        for i, (part, table) in enumerate(((0, 1), (1, 0), (0, 0), (1, 1))):
            for c in range(2):
                j = nc.vector.tensor_tensor(self.tmp[:, i, c, :, :], src[:, :, c, part * hw:(part + 1) * hw],
                                            self.rope[:, table, th, :], ALU.mult)
        j.then_inc(self.rotated, 1)
        eng.wait_ge(self.rotated, n)
        nc.vector.nop().then_inc(self.freed["dve"], 1)
        nc.vector.tensor_tensor(self.qr[:, :, th, 0:hw], self.tmp[:, 0, :, :, :], self.tmp[:, 1, :, :, :], ALU.subtract)
        nc.vector.tensor_tensor(self.qr[:, :, th, hw:HD], self.tmp[:, 2, :, :, :], self.tmp[:, 3, :, :, :],
                                ALU.add).then_inc(self.summed, 1)
        eng.wait_ge(self.summed, n)

    def convert(self, dve, s, u):
        if s + 2 in self.preps and u == 3:
            self.split(dve, s + 2, 0, self.qr[:, 0, :, :].rearrange("p (t h) e -> p t h e", t=QT), Q_SLOTS, HD ** -0.5, False)
            self.split(dve, s + 2, 1, self.qr[:, 1, :, :].rearrange("p (t h) e -> p t h e", t=QT), K_SLOTS, 1.0, False)


def self_attention(nc, d, x_sb, y_sb, ident, identb):
    hT_d = nc.dram_tensor("l0_hT_d", [B, P, DH, S], F32).ap()
    with ExitStack() as es:
        vecs = es.enter_context(nc.sbuf_tensor("l0_vecs", [P, 2, DH], F32))
        wqkv = es.enter_context(nc.sbuf_tensor("l0_wqkv", [P, DH, 3 * D], F32))
        wproj = es.enter_context(nc.sbuf_tensor("l0_wproj", [P, DH, D], F32))
        rope = es.enter_context(nc.sbuf_tensor("l0_rope", [P, 2, QT * HG, HD // 2], F32))
        tri_q = es.enter_context(nc.sbuf_tensor("l0_tri_q", [P, 512], BF16))
        tri_k = es.enter_context(nc.sbuf_tensor("l0_tri_k", [P, P], BF16))
        got = es.enter_context(nc.semaphore("l0_got"))
        with nc.Block() as block:
            @block.sync
            def _(sp):
                sp.dma_start(wqkv[:], d["L0_ffn_Wqkv"].rearrange("(h p) n -> p h n", p=P)).then_inc(got, 16)
                sp.dma_start(wproj[:], d["L0_ffn_Wproj"].rearrange("(h p) n -> p h n", p=P)).then_inc(got, 16)
                for i, n in enumerate(("L0_ffn_ln1_g", "L0_ffn_ln1_b")):
                    for h in range(DH):
                        sp.dma_start(vecs[:, i, h:h + 1],
                                     d[n][h * P:(h + 1) * P].rearrange("(p o) -> p o", o=1)).then_inc(got, 16)
                sp.dma_start(rope[:], d["c_rope"]).then_inc(got, 16)
                sp.dma_start(tri_q[:], d["c_tri_q"].bitcast(BF16)).then_inc(got, 16)
                sp.dma_start(tri_k[:], d["c_tri_k"].bitcast(BF16)).then_inc(got, 16)
                sp.wait_ge(got, 16 * 9)
        with ExitStack() as es1:
            hT = es1.enter_context(nc.sbuf_tensor("l0_hT", [P, DH, B * S], F32))
            layer_norm(nc, es1, x_sb, y_sb, "l0a")
            hn = es1.enter_context(nc.sbuf_tensor("l0_hn", [P, NT, D], F32))
            layer_norm(nc, es1, y_sb, hn, "l0b")
            transpose_tokens(nc, es1, hn, lambda g, h: hT[:, h, g * 512:(g + 1) * 512], ident, "l0T",
                             scale=vecs[:, 0, :], bias=vecs[:, 1, :])
            spill(nc, es1, "l0_hT", lambda b: hT[:, :, b * S:(b + 1) * S], hT_d)
        with ExitStack() as es1:
            heads = SelfHeads(nc, es1, hT_d, wqkv, rope, tri_q, tri_k)
            attend_all(nc, "l0", heads, ident, identb)
            nm = Names(nc, es1, "l0o")
            project_out(nc, nm, ident, heads.attn, wproj,
                        lambda t, prod: nc.vector.tensor_tensor(y_sb[:, t, :], prod, y_sb[:, t, :], ALU.add))


NEXP, FF = 8, 4 * D
CAP = -(-2 * B * S // NEXP)
FC = FF // P
FULL = 1 << 16


def route(nc, d, h2T, hn, xs, slots, gates, sent):
    with ExitStack() as es1:
        nm = Names(nc, es1, "rt")
        wg = nm.sb("wg", [P, DH, NEXP])
        tri = nm.sb("tri", [P, P])
        ones = nm.sb("ones", [P, P])
        rank = nm.sb("rank", [P, NT, NEXP])
        base = nm.sb("base", [P, NT, NEXP])
        zeros = nm.sb("zeros", [P, 8, D])
        g = nm.sb("g", [P, NT, NEXP])
        e = nm.sb("e", [P, NT, NEXP])
        eq = nm.sb("eq", [P, NT, NEXP])
        hot = nm.sb("hot", [P, 2, NT, NEXP])
        mask = nm.sb("mask", [P, NT, NEXP])
        before = nm.sb("before", [P, NT, NEXP])
        val = nm.sb("val", [P, 3, NT, NEXP])
        pick = nm.sb("pick", [P, 2, 3, NT, NEXP])
        got_f = nm.sb("slotf", [P, 2, 2, NT])
        m = nm.sb("m", [P, NT])
        s = nm.sb("s", [P, NT])
        ps = nm.ps("lg", [P, 512])
        pc = nm.ps("cum", [P, 512])
        got, scored, lowered, exped = nm.sem("got"), nm.sem("scored"), nm.sem("lowered"), nm.sem("exped")
        step, masked, counted, indexed = nm.sem("step"), nm.sem("masked"), nm.sem("counted"), nm.sem("indexed")
        zeroed, cleared = nm.sem("zeroed"), nm.sem("cleared")

        def per_token(t):
            return ap_of(t[:, :], 0, [t[:, :].ap[0], [1, NT], [0, NEXP]])

        with nc.Block() as block:
            @block.sync
            def _(sp):
                sp.dma_start(wg[:], d["L0_ffn_Wgate"].rearrange("(h p) n -> p h n", p=P)).then_inc(got, 16)
                sp.dma_start(tri[:], d["c_tri"]).then_inc(got, 16)
                sp.dma_start(ones[:], d["c_ones"]).then_inc(got, 16)
                sp.dma_start(rank[:], d["c_rank"]).then_inc(got, 16)
                sp.dma_start(base[:], d["c_base"]).then_inc(got, 16)
                sp.wait_ge(zeroed, 1)
                for q in range(NEXP * CAP // (8 * P)):
                    sp.dma_start(xs[q * 8 * P:(q + 1) * 8 * P, :].rearrange("(p r) k -> p r k", p=P),
                                 zeros[:, :, :]).then_inc(cleared, 16)

            @block.gpsimd
            def _(pool):
                nc.gpsimd.memset(zeros[:, :, :], 0.0).then_inc(zeroed, 1)
                pool.wait_ge(cleared, 16 * (NEXP * CAP // (8 * P)))
                pool.wait_ge(indexed, 1)
                for t in range(NT):
                    for c in range(2):
                        nc.gpsimd.indirect_dma_start(
                            xs[:, :], bass.IndirectOffsetOnAxis(slots[:, c, 0, t:t + 1], 0), hn[:, t, :], None,
                            bounds_check=NEXP * CAP - 1, oob_is_err=False).then_inc(sent, 16)
                pool.wait_ge(sent, 16 * 2 * NT)

            @block.tensor
            def _(pe):
                pe.wait_ge(got, 80)
                for t in range(NT):
                    for h in range(DH):
                        last = nc.tensor.matmul(ps[:, t * NEXP:(t + 1) * NEXP], h2T[:, h, t * P:(t + 1) * P],
                                                wg[:, h, :], start=(h == 0), stop=(h == DH - 1))
                last.then_inc(scored, 1)
                pe.wait_ge(masked, 1)
                n = NT * NEXP
                nc.tensor.matmul(pc[:, 0:n], tri[:, :], mask[:, :, :].rearrange("p t e -> p (t e)"), start=True,
                                 stop=False)
                nc.tensor.matmul(pc[:, 0:n], ones[:, :], before[:, :, :].rearrange("p t e -> p (t e)"), start=False,
                                 stop=True).then_inc(counted, 1)

            @block.scalar
            def _(act):
                act.wait_ge(lowered, 1)
                nc.scalar.activation(e[:, :, :], g[:, :, :], ACT.Exp).then_inc(exped, 1)

            @block.vector
            def _(dve):
                count = [0]

                def then(i):
                    count[0] += 1
                    i.then_inc(step, 1)
                    dve.wait_ge(step, count[0])

                tt, ts = nc.vector.tensor_tensor, nc.vector.tensor_scalar
                dve.wait_ge(scored, 1)
                lg = ps[:, 0:NT * NEXP].rearrange("p (t e) -> p t e", e=NEXP)
                then(nc.vector.tensor_reduce(m[:, :], lg, AX.X, ALU.max))
                tt(g[:, :, :], lg, per_token(m), ALU.subtract).then_inc(lowered, 1)
                dve.wait_ge(exped, 1)
                then(nc.vector.tensor_reduce(s[:, :], e[:, :, :], AX.X, ALU.add))
                then(nc.vector.reciprocal(s[:, :], s[:, :]))
                then(tt(g[:, :, :], e[:, :, :], per_token(s), ALU.mult))
                then(nc.vector.tensor_copy(e[:, :, :], g[:, :, :]))
                dve.wait_ge(got, 80)
                for i in range(2):
                    then(nc.vector.tensor_reduce(m[:, :], e[:, :, :], AX.X, ALU.max))
                    then(tt(eq[:, :, :], e[:, :, :], per_token(m), ALU.is_equal))
                    then(tt(eq[:, :, :], eq[:, :, :], rank[:, :, :], ALU.mult))
                    then(nc.vector.tensor_reduce(m[:, :], eq[:, :, :], AX.X, ALU.max))
                    then(tt(hot[:, i, :, :], eq[:, :, :], per_token(m), ALU.is_equal))
                    if i == 0:
                        then(nc.vector.scalar_tensor_tensor(e[:, :, :], hot[:, 0, :, :], -2.0, e[:, :, :], ALU.mult,
                                                            ALU.add))
                then(tt(mask[:, :, :], hot[:, 0, :, :], hot[:, 1, :, :], ALU.add))
                then(nc.vector.memset(before[:, 0, :], 0.0))
                for t in range(1, NT):
                    i = tt(before[:, t, :], before[:, t - 1, :], mask[:, t - 1, :], ALU.add)
                    if t < NT - 1:
                        then(i)
                i.then_inc(masked, 1)
                dve.wait_ge(counted, 1)
                cum = pc[:, 0:NT * NEXP].rearrange("p (t e) -> p t e", e=NEXP)
                ts(val[:, 0, :, :], cum, float(CAP), float(FULL), ALU.is_gt, ALU.mult)
                ts(val[:, 1, :, :], cum, float(CAP), None, ALU.min)
                then(ts(val[:, 2, :, :], cum, float(CAP), None, ALU.is_le))
                then(tt(val[:, 0, :, :], val[:, 0, :, :], cum, ALU.add))
                tt(val[:, 2, :, :], val[:, 2, :, :], g[:, :, :], ALU.mult)
                tt(val[:, 0, :, :], val[:, 0, :, :], base[:, :, :], ALU.add)
                then(tt(val[:, 1, :, :], val[:, 1, :, :], base[:, :, :], ALU.add))
                for c in range(2):
                    for v in range(3):
                        i = tt(pick[:, c, v, :, :], val[:, v, :, :], hot[:, c, :, :], ALU.mult)
                then(i)
                for c in range(2):
                    for v in range(2):
                        i = nc.vector.tensor_reduce(got_f[:, c, v, :], pick[:, c, v, :, :], AX.X, ALU.add)
                    nc.vector.tensor_reduce(gates[:, c, :], pick[:, c, 2, :, :], AX.X, ALU.add)
                then(i)
                nc.vector.tensor_copy(slots[:, :, :, :], got_f[:, :, :, :]).then_inc(indexed, 1)
        nm.clear()


def experts(nc, d, y_sb, ident, vecs, xs, ys, slots, gates, came):
    NE = 4
    ST = CAP // P
    with ExitStack() as es:
        nm = Names(nc, es, "ex")
        w1 = [nm.sb(f"w1_{i}", [P, DH, FF]) for i in range(NE)]
        w2 = [nm.sb(f"w2_{i}", [P, FC, D]) for i in range(NE)]
        b1 = [nm.sb(f"b1_{i}", [P, FC]) for i in range(NE)]
        b2 = [nm.sb(f"b2_{i}", [P, D]) for i in range(NE)]
        xr = [nm.sb(f"xr{i}", [P, ST, D]) for i in range(2)]
        xT = [nm.sb(f"xT{i}", [P, DH, CAP]) for i in range(2)]
        hm = [nm.sb(f"hm{i}", [P, FC, CAP]) for i in range(2)]
        yr = nm.sb("yr", [P, 2, ST, D])
        pt = [nm.ps(f"t{i}", [P, CAP]) for i in range(2)]
        pu = [nm.ps(f"up{i}", [P, CAP]) for i in range(4)]
        pd = [nm.ps(f"dn{i}", [P, 512]) for i in range(2)]
        got = [nm.sem(f"got{i}") for i in range(NE)]
        rows = [nm.sem(f"rows{i}") for i in range(2)]
        turned, kept = nm.sem("turned"), nm.sem("kept")
        up, gelued, down, summed = nm.sem("up"), nm.sem("gelued"), nm.sem("down"), nm.sem("summed")
        stored = [nm.sem(f"stored{i}") for i in range(2)]
        with nc.Fori(0, NEXP // NE) as turn:
            with nc.Block() as block:
                @block.sync
                def _(sp):
                    def load_rows(i):
                        if i >= 2:
                            sp.wait_ge(turned, DH * (i - 1))
                        sp.dma_start(xr[i % 2][:, :, :], xs[bass.ds((turn * NE + i) * CAP, CAP), :].rearrange(
                            "(t p) k -> p t k", p=P)).then_inc(rows[i % 2], 16)

                    load_rows(0)
                    for i in range(NE):
                        ex = turn * NE + i
                        sp.dma_start(w1[i][:, :, :], d["L0_ffn_W1"][bass.ds(ex, 1)].rearrange(
                            "o (h p) n -> p (o h) n", p=P)).then_inc(got[i], 16)
                        sp.dma_start(b1[i][:, :], d["b1_epc"][bass.ds(ex, 1)].rearrange(
                            "o p c -> p (o c)", p=P)).then_inc(got[i], 16)
                        if i == 0:
                            load_rows(1)
                    for i in range(2, NE):
                        load_rows(i)
                    for i in range(NE):
                        sp.wait_ge(summed, (i + 1) * ST)
                        sp.dma_start(ys[bass.ds((turn * NE + i) * CAP, CAP), :].rearrange("(t p) k -> p t k", p=P),
                                       yr[:, i % 2, :, :]).then_inc(stored[i % 2], 16)
                    for i in range(2):
                        sp.wait_ge(stored[i], 16 * NE // 2)


                @block.scalar
                def _(act):
                    for i in range(NE):
                        ex = turn * NE + i
                        act.dma_start(w2[i][:, :, :], d["L0_ffn_W2"][bass.ds(ex, 1)].rearrange(
                            "o (c p) n -> p (o c) n", p=P)).then_inc(got[i], 16)
                        src = d["L0_ffn_b2"][bass.ds(ex, 1), :].rearrange("o n -> (o n)").partition_broadcast(P)
                        act.dma_start(b2[i][:, :], src).then_inc(got[i], 16)
                    for i in range(NE):
                        act.wait_ge(got[i], 64)
                        if i >= 2:
                            act.wait_ge(down, (i - 1) * ST)
                        for c in range(FC):
                            k = i * FC + c
                            act.wait_ge(up, k + 1)
                            nc.scalar.activation(hm[i % 2][:, c, :], pu[k % 4][:, :], ACT.Gelu,
                                                 bias=b1[i][:, c:c + 1]).then_inc(gelued, 1)

                @block.tensor
                def _(pe):
                    def turns(i):
                        pe.wait_ge(rows[i % 2], 16 * (i // 2 + 1))
                        for h in range(DH):
                            if i >= 1:
                                pe.wait_ge(kept, DH * (i - 1) + h + 1)
                            for t in range(ST):
                                last = nc.tensor.transpose(pt[h][:, t * P:(t + 1) * P],
                                                           xr[i % 2][:, t, h * P:(h + 1) * P], ident[:, :])
                            last.then_inc(turned, 1)

                    def ups(i):
                        pe.wait_ge(kept, DH * (i + 1))
                        pe.wait_ge(got[i], 64)
                        for c in range(FC):
                            k = i * FC + c
                            if k >= 4:
                                pe.wait_ge(gelued, k - 3)
                            for h in range(DH):
                                last = nc.tensor.matmul(pu[k % 4][:, :], w1[i][:, h, c * P:(c + 1) * P],
                                                        xT[i % 2][:, h, :], start=(h == 0), stop=(h == DH - 1))
                            last.then_inc(up, 1)

                    def downs(i):
                        pe.wait_ge(gelued, (i + 1) * FC)
                        for t in range(ST):
                            k = i * ST + t
                            if k >= 2:
                                pe.wait_ge(summed, k - 1)
                            for c in range(FC):
                                last = nc.tensor.matmul(pd[k % 2][:, 0:D], hm[i % 2][:, c, t * P:(t + 1) * P],
                                                        w2[i][:, c, :], start=(c == 0), stop=(c == FC - 1))
                            last.then_inc(down, 1)

                    turns(0)
                    for i in range(NE):
                        ups(i)
                        if i + 1 < NE:
                            turns(i + 1)
                        if i:
                            downs(i - 1)
                    downs(NE - 1)

                @block.vector
                def _(dve):
                    def keep(i):
                        for h in range(DH):
                            dve.wait_ge(turned, DH * i + h + 1)
                            if i >= 2:
                                dve.wait_ge(up, (i - 1) * FC)
                            nc.vector.tensor_scalar(xT[i % 2][:, h, :], pt[h][:, :], vecs[:, 0, h:h + 1],
                                                    vecs[:, 1, h:h + 1], ALU.mult, ALU.add).then_inc(kept, 1)

                    def sums(i):
                        for t in range(ST):
                            k = i * ST + t
                            dve.wait_ge(down, k + 1)
                            if i >= 2 and t == 0:
                                dve.wait_ge(stored[i % 2], 16 * (i // 2))
                            nc.vector.tensor_tensor(yr[:, i % 2, t, :], pd[k % 2][:, 0:D], b2[i][:, :],
                                                    ALU.add).then_inc(summed, 1)

                    dve.wait_ge(got[0], 64)
                    keep(0)
                    for i in range(NE):
                        if i + 1 < NE:
                            keep(i + 1)
                        if i:
                            sums(i - 1)
                    for j in range(1, NE):
                        dve.wait_ge(got[j], 64)
                    sums(NE - 1)
            nm.clear()
    with ExitStack() as es:
        nm = Names(nc, es, "gb")
        NR = len(came)
        back = nm.sb("back", [P, NR, D])
        added = nm.sem("added")
        units = [(t, c) for c in range(2) for t in range(NT)]
        with nc.Block() as block:
            @block.gpsimd
            def _(pool):
                for n, (t, c) in enumerate(units):
                    if n >= NR:
                        pool.wait_ge(added, n - NR + 1)
                    nc.gpsimd.indirect_dma_start(back[:, n % NR, :], None, ys[:, :],
                                                 bass.IndirectOffsetOnAxis(slots[:, c, 1, t:t + 1], 0),
                                                 bounds_check=NEXP * CAP - 1,
                                                 oob_is_err=False).then_inc(came[n % NR], 16)

            @block.vector
            def _(dve):
                for n, (t, c) in enumerate(units):
                    dve.wait_ge(came[n % NR], 16 * (n // NR + 1))
                    if n >= NT:
                        dve.wait_ge(added, n - NT + 1)
                    nc.vector.scalar_tensor_tensor(y_sb[:, t, :], back[:, n % NR, :], gates[:, c, t:t + 1],
                                                   y_sb[:, t, :], ALU.mult, ALU.add).then_inc(added, 1)
        nm.clear()


def gated_add(nc, d, name, layer, x_sb, y_sb):
    with ExitStack() as es:
        nm = Names(nc, es, f"ga_{name}{layer}")
        gate = nm.sb("gate", [P, 2])
        got, gated = nm.sem("got"), nm.sem("gated")
        with nc.Block() as block:
            @block.sync
            def _(sp):
                sp.dma_start(gate[:], ap_of(d[name], 0, [[0, P], [1, 2]])).then_inc(got, 16)

            @block.scalar
            def _(act):
                act.wait_ge(got, 16)
                nc.scalar.activation(gate[:], gate[:], ACT.Tanh).then_inc(gated, 1)

            @block.vector
            def _(dve):
                dve.wait_ge(gated, 1)
                nc.vector.scalar_tensor_tensor(x_sb[:, :, :], y_sb[:, :, :], gate[:, layer:layer + 1], x_sb[:, :, :],
                                               ALU.mult, ALU.add)


def moe(nc, d, x_sb, y_sb, ident, sent, came):
    xs = nc.dram_tensor("expert_in", [NEXP * CAP, D], F32).ap()
    ys = nc.dram_tensor("expert_out", [NEXP * CAP, D], F32).ap()
    with ExitStack() as es:
        slots = es.enter_context(nc.sbuf_tensor("moe_slots", [P, 2, 2, NT], U32))
        gates = es.enter_context(nc.sbuf_tensor("moe_gates", [P, 2, NT], F32))
        vecs = es.enter_context(nc.sbuf_tensor("moe_vecs", [P, 2, DH], F32))
        with ExitStack() as es1:
            h2T = es1.enter_context(nc.sbuf_tensor("moe_hT", [P, DH, B * S], F32))
            got = es1.enter_context(nc.semaphore("moe_got"))
            with nc.Block() as block:
                @block.sync
                def _(sp):
                    for i, n in enumerate(("L0_ffn_ln2_g", "L0_ffn_ln2_b")):
                        for h in range(DH):
                            sp.dma_start(vecs[:, i, h:h + 1],
                                         d[n][h * P:(h + 1) * P].rearrange("(p o) -> p o", o=1)).then_inc(got, 16)
                    sp.wait_ge(got, 64)
            hn = es1.enter_context(nc.sbuf_tensor("moe_hn", [P, NT, D], F32))
            layer_norm(nc, es1, y_sb, hn, "lnm")
            transpose_tokens(nc, es1, hn, lambda g, h: h2T[:, h, g * 512:(g + 1) * 512], ident, "mT",
                             scale=vecs[:, 0, :], bias=vecs[:, 1, :])
            route(nc, d, h2T, hn, xs, slots, gates, sent)
        experts(nc, d, y_sb, ident, vecs, xs, ys, slots, gates, came)
    gated_add(nc, d, "g_ffn", 0, x_sb, y_sb)


class CrossHeads(Heads):

    rounds_of = ((0, ("q",)), (1, ("kv", 0)), (5, ("turn", 0, 0)), (7, ("turn", 0, 1)), (9, ("kv", 1)),
                 (11, ("turn", 1, 0)), (14, ("turn", 1, 1)), (17, ("turn", 2, 0)), (20, ("turn", 2, 1)))
    repeats = ((3, 0), (4, 1), (12, 2))

    def __init__(self, nc, es, mask_d, hT_d, ctxT_d, wq, wkv):
        super().__init__(nc, es, "xa", SK)
        sb = self.sb.sb
        self.mask_d, self.hT_d, self.ctxT_d, self.wq, self.wkv = mask_d, hT_d, ctxT_d, wq, wkv
        self.cTb = sb("cTb", [P, DH, SK])
        self.mask = sb("mask", [P, QT, SK], I32)
        self.now_q, self.next_q = sb("now_q", [P, QT, SK], BF16), sb("next_q", [P, QT, SK], BF16)
        self.now_k, self.next_k = sb("now_k", [P, KT, S], BF16), sb("next_k", [P, KT, S], BF16)

    def open(self, nm):
        super().open(nm)
        self.masked, self.biased = nm.sem("masked"), nm.sem("biased")

    def mask_rounds(self, s):
        places = {-2: (22, 24, 26, 28), 1: (23, 26), 2: (23, 26)}.get(s, ()) if self.next_batch else ()
        n0 = 2 if s == 2 else 0
        return [(u, ("mask", n0 + i)) for i, u in enumerate(places)]

    def plan(self, preps, steps):
        self.next_batch = 0 in preps or NG in preps
        super().plan(preps, steps)

    def bias_q(self, g, qt, f):
        return (self.next_q if g in (0, NG) else self.now_q)[:, qt, f * 512:(f + 1) * 512]

    def bias_k(self, kt):
        return self.now_k[:, kt, :]

    def load(self, sp, b):
        if not self.next_batch:
            return
        if 0 in self.preps:
            hT, cT, mask = self.hT_d[0], self.ctxT_d[0], self.mask_d[0].rearrange("(t p) k -> p t k", p=P)
        else:
            hT, cT = (x[bass.ds(b + 1, 1)].rearrange("o p h s -> p (o h) s") for x in (self.hT_d, self.ctxT_d))
            mask = self.mask_d[bass.ds(b + 1, 1)].rearrange("o (t p) k -> p (o t) k", p=P)
            sp.dma_start(self.mask[:, :, :], mask).then_inc(self.masked, 16)
            last = max(i for i, r in enumerate(self.rounds) if r[2] == NG - 1 and r[3][0] == "kv")
            sp.wait_ge(self.made, last + 1)
        sp.dma_start(self.hTb[:, :, :], hT).then_inc(self.loaded, 16)
        sp.dma_start(self.cTb[:, :, :], cT).then_inc(self.loaded, 16)
        if 0 in self.preps:
            sp.dma_start(self.mask[:, :, :], mask).then_inc(self.masked, 16)

    def project(self, pe, bank, p, kind):
        nc, g = self.nc, p and p % NG
        if kind[0] == "mask":
            n = kind[1]
            pe.wait_ge(self.biased, QT)
            out = bank[:, :].bitcast(BF16)
            for i in range(2):
                for t in range(QT):
                    kt = 2 * n + i
                    last = nc.tensor.transpose(out[:, (i * QT + t) * P:(i * QT + t + 1) * P],
                                               self.next_q[:, t, kt * P:(kt + 1) * P], self.identb[:, :])
            return last
        if kind[0] == "q":
            if g == 0:
                pe.wait_ge(self.loaded, 32)
            src, w, t0, n = self.hTb, self.wq, 0, GW
        else:
            src, w, t0, n = self.cTb, self.wkv, QT * kind[1], 2 * GW
        for i in range(QT):
            for h in range(DH):
                last = nc.tensor.matmul(bank[:, i * n:(i + 1) * n], src[:, h, (t0 + i) * P:(t0 + i + 1) * P],
                                        w[:, h, g * n:(g + 1) * n], start=(h == 0), stop=(h == DH - 1))
        return last

    def take_projection(self, who, eng, bank, p, kind):
        nc = self.nc
        if kind[0] == "mask":
            n = kind[1]
            nc.scalar.copy(self.next_k[:, 2 * n:2 * n + 2, :],
                           bank[:, :].bitcast(BF16).rearrange("p (i s) -> p i s", i=2)).then_inc(self.freed["act"], 1)
        elif kind[0] == "q":
            src = bank[:, 0:QT * GW].rearrange("p (t h e) -> p t h e", t=QT, h=HG)
            self.split(eng, p, 0, src, Q_SLOTS, float(HD) ** 0.5, True)
        else:
            src = bank[:, :].rearrange("p (t c h e) -> p t c h e", t=QT, c=2, h=HG)
            if who == "dve":
                self.split(eng, p, 1 + kind[1], src[:, :, 0, :, :], K_SLOTS, 1.0, True)
            else:
                t0 = QT * kind[1]
                nc.scalar.copy(self.vt[:, t0:t0 + QT, (p % NG) * HG:(p % NG + 1) * HG, 0:HD],
                               src[:, :, 1, :, :]).then_inc(self.freed["act"], 1)

    def convert(self, dve, s, u):
        places = {-2: (14, 16, 18, 20), 0: (14, 18, 22, 26)}.get(s, ()) if self.next_batch else ()
        if u in places:
            t = places.index(u)
            dve.wait_ge(self.masked, 16)
            self.nc.vector.tensor_scalar(self.next_q[:, t, :], self.mask[:, t, :], 0.0, NEG, ALU.is_equal,
                                         ALU.mult).then_inc(self.biased, 1)
            if t == QT - 1:
                dve.wait_ge(self.biased, QT)

    def finish(self, dve):
        if self.next_batch:
            dve.wait_ge(self.freed["act"], self.taken("act", len(self.rounds) - 1))
            self.nc.vector.tensor_copy(self.now_q[:, :, :], self.next_q[:, :, :])
            self.nc.vector.tensor_copy(self.now_k[:, :, :], self.next_k[:, :, :])


def cross_attention(nc, d, x_sb, ident, identb, ctxT_d):
    hT_d = nc.dram_tensor("xa_hT_d", [B, P, DH, S], F32).ap()
    with ExitStack() as es:
        wq = es.enter_context(nc.sbuf_tensor("xa_wq", [P, DH, D], F32))
        wo = es.enter_context(nc.sbuf_tensor("xa_wo", [P, DH, D], F32))
        wkv = es.enter_context(nc.sbuf_tensor("xa_wkv", [P, DH, 2 * D], F32))
        gate = es.enter_context(nc.sbuf_tensor("xa_gate", [P, 2], F32))
        got = es.enter_context(nc.semaphore("xa_got"))
        with nc.Block() as block:
            @block.sync
            def _(sp):
                for n, t in (("wqT", wq), ("woT", wo), ("wkvT", wkv)):
                    sp.dma_start(t[:], d[n].rearrange("(h p) n -> p h n", p=P)).then_inc(got, 16)
                sp.dma_start(gate[:], ap_of(d["g_xattn"], 0, [[0, P], [1, 2]])).then_inc(got, 16)
                sp.wait_ge(got, 64)

            @block.scalar
            def _(act):
                act.wait_ge(got, 64)
                nc.scalar.activation(gate[:], gate[:], ACT.Tanh)
        with ExitStack() as es1:
            hT = es1.enter_context(nc.sbuf_tensor("xa_hT", [P, DH, B * S], F32))
            xn = es1.enter_context(nc.sbuf_tensor("xa_xn", [P, NT, D], F32))
            layer_norm(nc, es1, x_sb, xn, "xa")
            transpose_tokens(nc, es1, xn, lambda g, h: hT[:, h, g * 512:(g + 1) * 512], ident, "xaT")
            spill(nc, es1, "xa_hT", lambda b: hT[:, :, b * S:(b + 1) * S], hT_d)
        with ExitStack() as es1:
            heads = CrossHeads(nc, es1, d["mask_BxSxS2_ik0"], hT_d, ctxT_d, wq, wkv)
            attend_all(nc, "xa", heads, ident, identb)
            nm = Names(nc, es1, "xao")
            project_out(nc, nm, ident, heads.attn, wo,
                        lambda t, prod: nc.vector.scalar_tensor_tensor(x_sb[:, t, :], prod, gate[:, 1:2], x_sb[:, t, :],
                                                                       ALU.mult, ALU.add))


FI = 704
QB = 16
FPAD = -(-FI // P)
STEPS_HALF, STEPS_ONE, STEP_TWO = (0.25, 0.75, 1.25, 1.75), (2.5, 3.5), 5.0


def quantize(nc, nm, jobs, width):
    n_blk = width // QB
    amax = nm.sb("amax", [P, 2, n_blk])
    inv = nm.sb("inv", [P, 2, n_blk])
    v = nm.sb("v", [P, 2, width])
    sgn = nm.sb("sgn", [P, 2, width])
    hi = nm.sb("hi", [P, 2, width])
    lo = nm.sb("lo", [P, 2, width])
    maxed, scaled, inverted, divided = nm.sem("maxed"), nm.sem("scaled"), nm.sem("inverted"), nm.sem("divided")
    signed, absed, step, graded, done = nm.sem("signed"), nm.sem("absed"), nm.sem("step"), nm.sem("graded"), nm.sem("done")
    sscaled = nm.sem("sscaled")

    def blocks(ap):
        return ap.rearrange("p (n e) -> p n e", e=QB)

    def wide(t, r, i):
        a = t[0:r, i, :]
        return ap_of(a, 0, [a.ap[0], [1, n_blk], [0, QB]])

    with nc.Block() as block:
        @block.vector
        def _(dve):
            count = [0]

            def then(i):
                count[0] += 1
                i.then_inc(step, 1)
                dve.wait_ge(step, count[0])

            def scale(n):
                src, dst = jobs[n]
                r, i = src.shape[0], n % 2
                if n >= 2:
                    dve.wait_ge(done, n - 1)
                then(nc.vector.tensor_reduce(amax[0:r, i, :], blocks(src), AX.X, ALU.max,
                                             apply_absolute_value=True))
                nc.vector.tensor_scalar(amax[0:r, i, :], amax[0:r, i, :], 1.0 / 6.0, 1e-12, ALU.mult,
                                        ALU.max).then_inc(scaled, 1)
                dve.wait_ge(scaled, n + 1)
                nc.vector.reciprocal(inv[0:r, i, :], amax[0:r, i, :]).then_inc(inverted, 1)

            def grade(n):
                src, dst = jobs[n]
                r, i = src.shape[0], n % 2
                a, h, l = v[0:r, i, :], hi[0:r, i, :], lo[0:r, i, :]
                dve.wait_ge(absed, n + 1)
                stt, ts = nc.vector.scalar_tensor_tensor, nc.vector.tensor_scalar
                ts(h, a, STEP_TWO, 2.0, ALU.is_gt, ALU.mult)
                then(ts(l, a, STEPS_HALF[0], None, ALU.is_gt))
                stt(h, a, STEPS_ONE[0], h, ALU.is_gt, ALU.add)
                then(stt(l, a, STEPS_HALF[1], l, ALU.is_gt, ALU.add))
                stt(h, a, STEPS_ONE[1], h, ALU.is_gt, ALU.add)
                then(stt(l, a, STEPS_HALF[2], l, ALU.is_gt, ALU.add))
                then(stt(l, a, STEPS_HALF[3], l, ALU.is_gt, ALU.add))
                stt(h, l, 0.5, h, ALU.mult, ALU.add).then_inc(graded, 1)

            scale(0)
            for n in range(len(jobs)):
                if n + 1 < len(jobs):
                    scale(n + 1)
                grade(n)

        @block.scalar
        def _(act):
            for n, (src, dst) in enumerate(jobs):
                r, i = src.shape[0], n % 2
                if n >= 2:
                    act.wait_ge(done, n - 1)
                nc.scalar.activation(sgn[0:r, i, :], src, ACT.Sign).then_inc(signed, 1)
                act.wait_ge(divided, n + 1)
                nc.scalar.activation(v[0:r, i, :], v[0:r, i, :], ACT.Abs).then_inc(absed, 1)

        @block.gpsimd
        def _(pool):
            def divide(n):
                src, dst = jobs[n]
                r, i = src.shape[0], n % 2
                pool.wait_ge(inverted, n + 1)
                nc.gpsimd.tensor_tensor(blocks(v[0:r, i, :]), blocks(src), wide(inv, r, i), ALU.mult).then_inc(divided, 1)
                pool.wait_ge(signed, n + 1)
                nc.gpsimd.tensor_tensor(blocks(sgn[0:r, i, :]), blocks(sgn[0:r, i, :]), wide(amax, r, i),
                                        ALU.mult).then_inc(sscaled, 1)

            divide(0)
            for n, (src, dst) in enumerate(jobs):
                r, i = src.shape[0], n % 2
                if n + 1 < len(jobs):
                    divide(n + 1)
                pool.wait_ge(graded, n + 1)
                pool.wait_ge(sscaled, n + 1)
                nc.gpsimd.tensor_tensor(dst, hi[0:r, i, :], sgn[0:r, i, :], ALU.mult).then_inc(done, 1)


def turn_rows(nc, nm, ident, jobs):
    ps = [nm.ps(f"tr{i}", [P, 512]) for i in range(4)]
    turned, kept = nm.sem("tr_turned"), [nm.sem("tr_kept0"), nm.sem("tr_kept1")]
    with nc.Block() as block:
        @block.tensor
        def _(pe):
            for n, (src, dst) in enumerate(jobs):
                r, c = src.shape
                if n >= 4:
                    pe.wait_ge(kept[n % 2], (n - 4) // 2 + 1)
                nc.tensor.transpose(ps[n % 4][0:c, 0:r], src, ident[0:r, 0:r]).then_inc(turned, 1)

        def copies(eng, parity, copy):
            for n, (src, dst) in enumerate(jobs):
                r, c = src.shape
                if n % 2 == parity:
                    eng.wait_ge(turned, n + 1)
                    copy(dst, ps[n % 4][0:c, 0:r]).then_inc(kept[parity], 1)

        @block.vector
        def _(dve):
            copies(dve, 0, nc.vector.tensor_copy)

        @block.scalar
        def _(act):
            copies(act, 1, nc.scalar.copy)


def fp4_ffn(nc, d, x_sb, ident):
    with ExitStack() as es:
        wgu = es.enter_context(nc.sbuf_tensor("ff_wguT", [P, DH, 2, FI], F32))
        wd = es.enter_context(nc.sbuf_tensor("ff_wdT", [P, FPAD, D], F32))
        xqT = es.enter_context(nc.sbuf_tensor("ff_xqT", [P, DH, B * S], F32))
        gate = es.enter_context(nc.sbuf_tensor("ff_gate", [P, 2], F32))
        with ExitStack() as e1:
            nm = Names(nc, e1, "ffw")
            wr = nm.sb("rows", [P, 2, FPAD, D])
            wq = nm.sb("rowsq", [P, 2, FPAD, D])
            dr = nm.sb("down", [P, DH, FI])
            dq = nm.sb("downq", [P, DH, FI])
            got = nm.sem("got")
            last_rows = FI - (FPAD - 1) * P
            with nc.Block() as block:
                @block.sync
                def _(sp):
                    for i, n in enumerate(("L1_ffn_w_gate", "L1_ffn_w_up")):
                        full = (FPAD - 1) * P
                        sp.dma_start(wr[:, i, 0:FPAD - 1, :],
                                     d[n][0:full, :].rearrange("(c p) k -> p c k", p=P)).then_inc(got, 16)
                        sp.dma_start(wr[0:last_rows, i, FPAD - 1, :], d[n][full:FI, :]).then_inc(got, 16)
                    sp.dma_start(dr[:], d["L1_ffn_w_down"].rearrange("(h p) k -> p h k", p=P)).then_inc(got, 16)
                    sp.dma_start(gate[:], ap_of(d["g_ffn"], 0, [[0, P], [1, 2]])).then_inc(got, 16)
                    sp.wait_ge(got, 96)

                @block.scalar
                def _(act):
                    act.wait_ge(got, 96)
                    nc.scalar.activation(gate[:], gate[:], ACT.Tanh)
            with ExitStack() as e2:
                nq = Names(nc, e2, "ffq1")
                jobs = []
                for i in range(2):
                    for c in range(FPAD):
                        r = P if c < FPAD - 1 else last_rows
                        jobs.append((wr[0:r, i, c, :], wq[0:r, i, c, :]))
                quantize(nc, nq, jobs, D)
            with ExitStack() as e2:
                nq = Names(nc, e2, "ffq2")
                quantize(nc, nq, [(dr[:, h, :], dq[:, h, :]) for h in range(DH)], FI)
            jobs = []
            for i in range(2):
                for c in range(FPAD):
                    r = P if c < FPAD - 1 else last_rows
                    for h in range(DH):
                        jobs.append((wq[0:r, i, c, h * P:(h + 1) * P], wgu[:, h, i, c * P:c * P + r]))
            for c in range(FPAD):
                r = P if c < FPAD - 1 else last_rows
                for h in range(DH):
                    jobs.append((dq[:, h, c * P:c * P + r], wd[0:r, c, h * P:(h + 1) * P]))
            turn_rows(nc, nm, ident, jobs)
        with ExitStack() as e1:
            xn = e1.enter_context(nc.sbuf_tensor("ff_xn", [P, NT, D], F32))
            layer_norm(nc, e1, x_sb, xn, "ff")
            nm = Names(nc, e1, "ffx")
            quantize(nc, nm, [(xn[:, 4 * g:4 * g + 4, :].rearrange("p t d -> p (t d)"),
                               xn[:, 4 * g:4 * g + 4, :].rearrange("p t d -> p (t d)")) for g in range(NT // 4)], 4 * D)
            transpose_tokens(nc, e1, xn, lambda g, h: xqT[:, h, g * 512:(g + 1) * 512], ident, "ffT")
        with nc.Fori(0, B) as b, ExitStack() as e0:
            hid = e0.enter_context(nc.sbuf_tensor("ff_hid", [P, QT, FI], F32))
            hq = e0.enter_context(nc.sbuf_tensor("ff_hq", [P, QT, FI], F32))
            with ExitStack() as e1:
                nm = Names(nc, e1, "ffg")
                xb = nm.sb("xb", [P, DH, S])
                sg = nm.sb("sg", [P, 2, FI])
                HALF = FI // 2
                pg = [nm.ps(f"g{i}", [P, 512]) for i in range(4)]
                pu = [nm.ps(f"u{i}", [P, 512]) for i in range(4)]
                static, prod, silued, mixed = nm.sem("static"), nm.sem("prod"), nm.sem("silued"), nm.sem("mixed")
                units = [(t, f) for t in range(QT) for f in range(2)]
                with nc.Block() as block:
                    @block.tensor
                    def _(pe):
                        pe.wait_ge(static, 1)
                        for n, (t, f) in enumerate(units):
                            if n >= 4:
                                pe.wait_ge(mixed, n - 3)
                            for i, ps in enumerate((pg, pu)):
                                for h in range(DH):
                                    last = nc.tensor.matmul(ps[n % 4][:, 0:HALF], xb[:, h, t * P:(t + 1) * P],
                                                            wgu[:, h, i, f * HALF:(f + 1) * HALF], start=(h == 0),
                                                            stop=(h == DH - 1))
                            last.then_inc(prod, 1)

                    @block.scalar
                    def _(act):
                        nc.scalar.copy(xb[:, :, :], xqT[:, :, bass.ds(b * S, S)]).then_inc(static, 1)
                        for n, (t, f) in enumerate(units):
                            act.wait_ge(prod, n + 1)
                            if n >= 4:
                                act.wait_ge(mixed, n - 3)
                            nc.scalar.activation(sg[:, (n // 2) % 2, f * HALF:(f + 1) * HALF], pg[n % 4][:, 0:HALF],
                                                 ACT.Silu).then_inc(silued, 1)

                    @block.vector
                    def _(dve):
                        for n, (t, f) in enumerate(units):
                            dve.wait_ge(silued, n + 1)
                            nc.vector.tensor_tensor(hid[:, t, f * HALF:(f + 1) * HALF], pu[n % 4][:, 0:HALF],
                                                    sg[:, (n // 2) % 2, f * HALF:(f + 1) * HALF],
                                                    ALU.mult).then_inc(mixed, 1)
                nm.clear()
            with ExitStack() as e1:
                nm = Names(nc, e1, "ffh")
                quantize(nc, nm, [(hid[:, t, :], hq[:, t, :]) for t in range(QT)], FI)
                nm.clear()
            with ExitStack() as e1:
                nm = Names(nc, e1, "ffd")
                hqT = nm.sb("hqT", [P, 2, FPAD, P])
                pt = [nm.ps(f"t{i}", [P, 1024]) for i in range(2)]
                py = [nm.ps(f"y{i}", [P, 512]) for i in range(2)]
                turned, kept, down, added = nm.sem("turned"), nm.sem("kept"), nm.sem("down"), nm.sem("added")
                last_rows = FI - (FPAD - 1) * P
                with nc.Block() as block:
                    @block.tensor
                    def _(pe):
                        def turn(t):
                            if t >= 2:
                                pe.wait_ge(kept, 2 * (t - 1))
                            for c in range(FPAD):
                                r = P if c < FPAD - 1 else last_rows
                                last = nc.tensor.transpose(pt[t % 2][0:r, c * P:(c + 1) * P], hq[:, t, c * P:c * P + r],
                                                           ident[:, :])
                            last.then_inc(turned, 1)

                        def product(t):
                            pe.wait_ge(kept, 2 * (t + 1))
                            if t >= 2:
                                pe.wait_ge(added, t - 1)
                            for c in range(FPAD):
                                r = P if c < FPAD - 1 else last_rows
                                last = nc.tensor.matmul(py[t % 2][:, 0:D], hqT[0:r, t % 2, c, :], wd[0:r, c, :],
                                                        start=(c == 0), stop=(c == FPAD - 1))
                            last.then_inc(down, 1)

                        turn(0)
                        for t in range(1, QT):
                            turn(t)
                            product(t - 1)
                        product(QT - 1)

                    @block.scalar
                    def _(act):
                        for t in range(QT):
                            act.wait_ge(turned, t + 1)
                            if t >= 2:
                                act.wait_ge(down, t - 1)
                            n = FPAD - 1
                            nc.scalar.copy(hqT[:, t % 2, 0:n, :],
                                           pt[t % 2][:, 0:n * P].rearrange("p (c s) -> p c s", s=P)).then_inc(kept, 1)
                            nc.scalar.copy(hqT[0:last_rows, t % 2, n, :],
                                           pt[t % 2][0:last_rows, n * P:(n + 1) * P]).then_inc(kept, 1)

                    @block.vector
                    def _(dve):
                        for t in range(QT):
                            dve.wait_ge(down, t + 1)
                            x = x_sb[:, bass.ds(b * QT + t, 1), :].rearrange("p o d -> p (o d)")
                            nc.vector.scalar_tensor_tensor(x, py[t % 2][:, 0:D], gate[:, 1:2], x, ALU.mult,
                                                           ALU.add).then_inc(added, 1)
                nm.clear()


def layouts(a):
    return {
        "b1_epc": np.ascontiguousarray(np.asarray(a["L0_ffn_b1"]).reshape(NEXP, FC, P).transpose(0, 2, 1)),
        "wqT": np.ascontiguousarray(np.asarray(a["L1_xattn_Wq"]).T),
        "wkvT": np.ascontiguousarray(np.stack([np.asarray(a[f"L1_xattn_W{n}"]).T.reshape(D, NG, GW) for n in "kv"],
                                              2).reshape(D, 2 * D)),
        "woT": np.ascontiguousarray(np.asarray(a["L1_xattn_Wo"]).T),
    }


def bf16_bits(a):
    return np.ascontiguousarray((np.ascontiguousarray(a, np.float32).view(np.uint32) >> 16).astype(np.uint16))


def constants():
    c = {}
    c["c_ident"] = np.eye(P, dtype=np.float32)
    ones2 = np.zeros((P, 2, 2), np.float32)
    ones2[:, 0, 0] = 1
    ones2[:, 1, 1] = 1
    c["c_ones2"] = ones2
    c["c_add2"] = np.array([[0, 1], [1, 0]], np.float32)
    corner = np.full((P, PITCH), FAR, np.float32)
    corner[::NBLK, 0] = 0
    c["c_corner"] = corner
    inner = np.ones((P, 1), np.float32)
    inner[::NBLK] = 0
    c["c_inner"] = inner
    seed = np.zeros((P, 2 * RB + 2), np.float32)
    seed[NBLK - 1::NBLK, -1] = 1
    c["c_seed"] = bf16_bits(seed)
    c["c_identb"] = bf16_bits(np.eye(P, dtype=np.float32))
    inv = 1.0 / 10000.0 ** (np.arange(0, HD, 2, dtype=np.float32) / np.float32(HD))
    ang = np.arange(S, dtype=np.float32)[:, None] * inv.astype(np.float32)
    tab = np.stack([np.sin(ang), np.cos(ang)]).astype(np.float32)
    tab = tab.reshape(2, QT, P, 1, HD // 2).transpose(2, 0, 1, 3, 4)
    c["c_rope"] = np.ascontiguousarray(np.broadcast_to(tab, (P, 2, QT, HG, HD // 2)).reshape(P, 2, QT * HG, HD // 2))
    tri = np.where(np.arange(P)[None, :] <= np.arange(P)[:, None], 0, NEG).astype(np.float32)
    c["c_tri_q"] = bf16_bits(np.concatenate([np.zeros((P, 512 - P), np.float32), tri], 1))
    c["c_tri_k"] = bf16_bits(tri.T)
    c["c_tri"] = np.ascontiguousarray(np.tri(P, dtype=np.float32).T)
    c["c_ones"] = np.ones((P, P), np.float32)
    c["c_base"] = np.ascontiguousarray(np.broadcast_to(np.arange(NEXP, dtype=np.float32) * CAP - 1, (P, NT, NEXP)))
    c["c_rank"] = np.ascontiguousarray(np.broadcast_to(np.arange(NEXP, 0, -1, dtype=np.float32), (P, NT, NEXP)))
    return c


def load_all(nc, d, x_sb, ident, identb, ctxT, x_src):
    with ExitStack() as es:
        ctx_nat = es.enter_context(nc.sbuf_tensor("ctx_nat", [P, B * KT, D], F32))
        came = es.enter_context(nc.semaphore("inputs_came"))
        with nc.Block() as block:
            @block.sync
            def _(sp):
                sp.dma_start(x_sb[:], x_src.rearrange("b (t p) d -> p (b t) d", p=P)).then_inc(came, 16)
                sp.dma_start(ident[:], d["c_ident"]).then_inc(came, 16)
                sp.dma_start(identb[:], d["c_identb"].bitcast(BF16)).then_inc(came, 16)
                sp.wait_ge(came, 64)

            @block.scalar
            def _(act):
                act.dma_start(ctx_nat[:], d["ctx_1024"].rearrange("b (t p) d -> p (b t) d", p=P)).then_inc(came, 16)

            @block.gpsimd
            def _(pool):
                nc.gpsimd.memset(ctxT[:, :, :, SK:PADI], 0.0)
        transpose_tokens(nc, es, ctx_nat, lambda g, h: ctxT[:, g // 2, h, (g % 2) * 512:(g % 2) * 512 + 512],
                         ident, "cT")


def build(nc, d, out, phases=("dtw", "l0", "xa", "ffn")):
    with ExitStack() as es:
        sent = es.enter_context(nc.semaphore("rows_sent"))
        rows_came = es.enter_context(nc.semaphore("ctx_rows_came"))
        came = [es.enter_context(nc.semaphore(f"rows_came{i}")) for i in range(8)]
        x_sb = es.enter_context(nc.sbuf_tensor("x_sb", [P, NT, D], F32))
        ident = es.enter_context(nc.sbuf_tensor("ident", [P, P], F32))
        identb = es.enter_context(nc.sbuf_tensor("identb", [P, P], BF16))
        ctxT_d = nc.dram_tensor("ctxT_d", [B, P, DH, SK], F32).ap()
        with ExitStack() as es1:
            ctxT = es1.enter_context(nc.sbuf_tensor("ctxT", [P, B, DH, PADI], F32))
            load_all(nc, d, x_sb, ident, identb, ctxT, d["x"])
            clear_released(nc)
            if "dtw" in phases:
                dtw_block(nc, d, x_sb, ident, ctxT, ctxT_d, rows_came)
            else:
                spill(nc, es1, "ctxT", lambda b: ctxT[:, b, :, 0:SK], ctxT_d)
        clear_released(nc)
        if "l0" in phases:
            with ExitStack() as es1:
                y_sb = es1.enter_context(nc.sbuf_tensor("y_sb", [P, NT, D], F32))
                self_attention(nc, d, x_sb, y_sb, ident, identb)
                clear_released(nc)
                moe(nc, d, x_sb, y_sb, ident, sent, came)
                clear_released(nc)
        if "xa" in phases:
            cross_attention(nc, d, x_sb, ident, identb, ctxT_d)
            clear_released(nc)
        if "ffn" in phases:
            fp4_ffn(nc, d, x_sb, ident)
            clear_released(nc)
        stored = es.enter_context(nc.semaphore("out_stored"))
        with nc.Block() as block:
            @block.sync
            def _(sp):
                sp.dma_start(out.rearrange("b (t p) d -> p (b t) d", p=P), x_sb[:]).then_inc(stored, 16)
                sp.wait_ge(stored, 16)


_INS = ("x", "ctx_1024", "mask_BxSxS2_ik0", "g_xattn", "g_ffn", "L0_ffn_ln1_g", "L0_ffn_ln1_b", "L0_ffn_Wqkv",
        "L0_ffn_Wproj", "L0_ffn_ln2_g", "L0_ffn_ln2_b", "L0_ffn_Wgate", "L0_ffn_W1", "L0_ffn_W2", "L0_ffn_b2",
        "L1_ffn_w_gate", "L1_ffn_w_up", "L1_ffn_w_down")


def kernel(**inputs):
    import concourse.bacc as bacc
    from concourse.bass_utils import run_bass_kernel_spmd

    nc = bacc.Bacc("TRN2", target_bir_lowering=False, num_devices=1)
    arrays = {n: np.ascontiguousarray(inputs[n]) for n in _INS}
    arrays.update(layouts(inputs))
    arrays.update(constants())
    d = {n: nc.dram_tensor(n, a.shape, mybir.dt.from_np(a.dtype), kind="ExternalInput").ap()
         for n, a in arrays.items()}
    out = nc.dram_tensor("out", (B, S, D), F32, kind="ExternalOutput").ap()
    build(nc, d, out)
    r = run_bass_kernel_spmd(nc, [arrays], core_ids=[0])
    return r.results[0]["out"]
```
